# Optimizing a Trainium2 kernel written in Bass

```python
import numpy as np
import jax
import jax.numpy as jnp

def _softmax(x, axis=-1):
    return jax.nn.softmax(x, axis=axis)

def _gelu(x):
    return jax.nn.gelu(x, approximate=True)

def _silu(x):
    return jax.nn.silu(x)

def _sigmoid(x):
    return jax.nn.sigmoid(x)

def _layernorm(x, axis=-1, eps=1e-05):
    m = jnp.mean(x, axis=axis, keepdims=True)
    v = jnp.var(x, axis=axis, keepdims=True)
    return (x - m) / jnp.sqrt(v + eps)

def _scatter_add(tgt, idx, src, axis=0):
    return tgt.at[idx].add(src)

def _segment_sum(src, seg, n):
    return jax.ops.segment_sum(src, seg, n)
kernel_name = 'mk_flamingo_gated_d2_seqx_r4_137342'

def setup_inputs(seed: int=0):
    np.random.seed(seed)
    _w = jnp.asarray

    def _rec_inputs():
        import jax
        import jax.numpy as jnp
        _rk = jax.random.key(seed)
        x = 7.22e-05 + 1 * jax.random.normal(jax.random.fold_in(_rk, 1), (64, 256, 256), jnp.float32)
        _lenS = 256 - jax.random.randint(jax.random.fold_in(_rk, 7), (64,), 0, max(1, 256 // 4) + 1, jnp.int32)
        _lenS2 = 120 - jax.random.randint(jax.random.fold_in(_rk, 8), (64,), 0, max(1, 120 // 4) + 1, jnp.int32)
        _ctx_1024P = jax.random.normal(jax.random.fold_in(_rk, 11), (64, 16, 256), jnp.float32)
        _ctx_1024c = jax.random.dirichlet(jax.random.fold_in(_rk, 511), 0.3 * jnp.ones((16,), jnp.float32), (64, 120))
        _ctx_1024t = jnp.einsum('bsk,bkd->bsd', _ctx_1024c, _ctx_1024P)
        _ctx_1024t = _ctx_1024t * jax.lax.rsqrt(jnp.mean(jnp.square(_ctx_1024t)) + 1e-12) * 0.953939
        ctx_1024 = 4.13588e-05 + 0.999923 * (_ctx_1024t + 0.3 * jax.random.normal(jax.random.fold_in(_rk, 611), (64, 120, 256), jnp.float32))
        _g = jax.random.normal(jax.random.fold_in(_rk, 9001), (2, 2), jnp.float32)
        _g = jnp.sign(_g) * jnp.maximum(jnp.abs(_g), 1.0) + (_g == 0) * 1.0
        g_xattn = _g[0]
        g_ffn = _g[1]
        return (x, ctx_1024, g_xattn, g_ffn)
    x, ctx_1024, g_xattn, g_ffn = _rec_inputs()

    def _L0_xattn_setup():
        import jax, jax.numpy as jnp
        import numpy as np
        B, NQ, NK = (4, 512, 512)
        QDIM = CDIM = 256
        H, DH = (16, 64)
        SCALE = DH ** (-0.5)
        WSTD = 0.02
        key = jax.random.key(seed)
        ks = jax.random.split(key, 6)
        inner = H * DH
        return {'x': jax.random.normal(ks[0], (B, NQ, QDIM), dtype=jnp.float32), 'context': jax.random.normal(ks[1], (B, NK, CDIM), dtype=jnp.float32), 'Wq': jax.random.normal(ks[2], (inner, QDIM), dtype=jnp.float32) * WSTD, 'Wk': jax.random.normal(ks[3], (inner, CDIM), dtype=jnp.float32) * WSTD, 'Wv': jax.random.normal(ks[4], (inner, CDIM), dtype=jnp.float32) * WSTD, 'Wo': jax.random.normal(ks[5], (QDIM, inner), dtype=jnp.float32) * WSTD, 'bo': jnp.zeros((QDIM,), dtype=jnp.float32)}
    _L0_xattn_all = _L0_xattn_setup()
    _L0_xattn_in = {k: v for k, v in _L0_xattn_all.items() if k in ('Wq', 'Wk', 'Wv', 'Wo', 'bo')}
    del _L0_xattn_all

    def _L0_ffn_setup():
        import jax, jax.numpy as jnp
        import numpy as np
        THRESHOLD = 0.1
        key = jax.random.key(seed)
        k1, k2, k3 = jax.random.split(key, 3)
        B, S, D, E = (4, 1024, 256, 8)
        inputs = jax.random.normal(k1, (B, S, D), dtype=jnp.float32)
        gate_w = jax.random.normal(k2, (D, E), dtype=jnp.float32) * 0.02
        gate_b = jnp.zeros((E,), dtype=jnp.float32)
        expert_w = jax.random.normal(k3, (E, D, D), dtype=jnp.float32) * 0.02
        expert_b = jnp.zeros((E, D), dtype=jnp.float32)
        return {'inputs': inputs, 'gate_w': gate_w, 'gate_b': gate_b, 'expert_w': expert_w, 'expert_b': expert_b}
    _L0_ffn_all = _L0_ffn_setup()
    _L0_ffn_in = {k: v for k, v in _L0_ffn_all.items() if k in ('gate_w', 'gate_b', 'expert_w', 'expert_b')}
    del _L0_ffn_all

    def _L1_xattn_setup():
        import jax, jax.numpy as jnp
        import numpy as np
        B, S, D, H = (4, 512, 256, 16)
        DK = D // H
        key = jax.random.key(seed)
        ks = jax.random.split(key, 8)
        scale = 1.0 / np.sqrt(D)
        return {'q': jax.random.normal(ks[0], (B, S, D), jnp.float32), 'k': jax.random.normal(ks[1], (B, S, D), jnp.float32), 'v': jax.random.normal(ks[2], (B, S, D), jnp.float32), 'wq': jax.random.normal(ks[3], (D, D), jnp.float32) * scale, 'bq': jnp.zeros((D,), jnp.float32), 'wk': jax.random.normal(ks[4], (D, D), jnp.float32) * scale, 'bk': jnp.zeros((D,), jnp.float32), 'wv': jax.random.normal(ks[5], (D, D), jnp.float32) * scale, 'bv': jnp.zeros((D,), jnp.float32), 'wo': jax.random.normal(ks[6], (D, D), jnp.float32) * scale, 'bo': jnp.zeros((D,), jnp.float32)}
    _L1_xattn_all = _L1_xattn_setup()
    _L1_xattn_in = {k: v for k, v in _L1_xattn_all.items() if k in ('wq', 'bq', 'wk', 'bk', 'wv', 'bv', 'wo', 'bo')}
    del _L1_xattn_all

    def _L1_ffn_setup():
        import jax, jax.numpy as jnp
        import numpy as np
        NUM_EXPERTS = 8
        HIDDEN = 256
        INTER = 256
        BATCH = 2
        SEQ = 256
        TOP_K = 2
        SWIGLU_ALPHA = 1.702
        LIMIT = 7.0

        def _grouped_mm(x, w, expert_ids):
            onehot = jax.nn.one_hot(expert_ids, w.shape[0], dtype=x.dtype)
            y_all = jnp.einsum('tk,ekn->etn', x, w)
            return jnp.einsum('te,etn->tn', onehot, y_all)

        def _gpt_oss_swiglu(x):
            gate = jnp.minimum(x[..., ::2], LIMIT)
            up = jnp.clip(x[..., 1::2], -LIMIT, LIMIT)
            glu = gate * jax.nn.sigmoid(gate * SWIGLU_ALPHA)
            return (up + 1.0) * glu
        key = jax.random.key(seed)
        ks = jax.random.split(key, 7)
        hidden_states = jax.random.normal(ks[0], (BATCH, SEQ, HIDDEN), jnp.float32)
        router_indices = jax.random.randint(ks[1], (BATCH * SEQ, TOP_K), 0, NUM_EXPERTS)
        routing_weights = jax.nn.softmax(jax.random.normal(ks[2], (BATCH * SEQ, NUM_EXPERTS), jnp.float32), axis=-1)
        scale = 0.02
        gate_up_proj = jax.random.normal(ks[3], (NUM_EXPERTS, HIDDEN, 2 * INTER), jnp.float32) * scale
        gate_up_proj_bias = jax.random.normal(ks[4], (NUM_EXPERTS, 2 * INTER), jnp.float32) * scale
        down_proj = jax.random.normal(ks[5], (NUM_EXPERTS, INTER, HIDDEN), jnp.float32) * scale
        down_proj_bias = jax.random.normal(ks[6], (NUM_EXPERTS, HIDDEN), jnp.float32) * scale
        return {'hidden_states': hidden_states, 'router_indices': router_indices, 'routing_weights': routing_weights, 'gate_up_proj': gate_up_proj, 'gate_up_proj_bias': gate_up_proj_bias, 'down_proj': down_proj, 'down_proj_bias': down_proj_bias}
    _L1_ffn_all = _L1_ffn_setup()
    _L1_ffn_in = {k: v for k, v in _L1_ffn_all.items() if k in ('router_indices', 'routing_weights', 'gate_up_proj', 'gate_up_proj_bias', 'down_proj', 'down_proj_bias')}
    del _L1_ffn_all
    return {'x': x, 'ctx_1024': ctx_1024, 'g_xattn': g_xattn, 'g_ffn': g_ffn, 'L0_xattn_Wq': _L0_xattn_in['Wq'], 'L0_xattn_Wk': _L0_xattn_in['Wk'], 'L0_xattn_Wv': _L0_xattn_in['Wv'], 'L0_xattn_Wo': _L0_xattn_in['Wo'], 'L0_xattn_bo': _L0_xattn_in['bo'], 'L0_ffn_gate_w': _L0_ffn_in['gate_w'], 'L0_ffn_gate_b': _L0_ffn_in['gate_b'], 'L0_ffn_expert_w': _L0_ffn_in['expert_w'], 'L0_ffn_expert_b': _L0_ffn_in['expert_b'], 'L1_xattn_wq': _L1_xattn_in['wq'], 'L1_xattn_bq': _L1_xattn_in['bq'], 'L1_xattn_wk': _L1_xattn_in['wk'], 'L1_xattn_bk': _L1_xattn_in['bk'], 'L1_xattn_wv': _L1_xattn_in['wv'], 'L1_xattn_bv': _L1_xattn_in['bv'], 'L1_xattn_wo': _L1_xattn_in['wo'], 'L1_xattn_bo': _L1_xattn_in['bo'], 'L1_ffn_router_indices': _L1_ffn_in['router_indices'], 'L1_ffn_routing_weights': _L1_ffn_in['routing_weights'], 'L1_ffn_gate_up_proj': _L1_ffn_in['gate_up_proj'], 'L1_ffn_gate_up_proj_bias': _L1_ffn_in['gate_up_proj_bias'], 'L1_ffn_down_proj': _L1_ffn_in['down_proj'], 'L1_ffn_down_proj_bias': _L1_ffn_in['down_proj_bias']}

def reference(x, ctx_1024, g_xattn, g_ffn, L0_xattn_Wq, L0_xattn_Wk, L0_xattn_Wv, L0_xattn_Wo, L0_xattn_bo, L0_ffn_gate_w, L0_ffn_gate_b, L0_ffn_expert_w, L0_ffn_expert_b, L1_xattn_wq, L1_xattn_bq, L1_xattn_wk, L1_xattn_bk, L1_xattn_wv, L1_xattn_bv, L1_xattn_wo, L1_xattn_bo, L1_ffn_router_indices, L1_ffn_routing_weights, L1_ffn_gate_up_proj, L1_ffn_gate_up_proj_bias, L1_ffn_down_proj, L1_ffn_down_proj_bias):
    import jax
    import jax.numpy as jnp

    def _L0_xattn_ref(x, context, Wq, Wk, Wv, Wo, bo):
        import jax, jax.numpy as jnp
        import numpy as np
        B, NQ, NK = (4, 512, 512)
        QDIM = CDIM = 256
        H, DH = (16, 64)
        SCALE = DH ** (-0.5)
        WSTD = 0.02
        b, nq, _ = x.shape
        nk = context.shape[1]
        q = (x @ Wq.T).reshape(b, nq, H, DH)
        k = (context @ Wk.T).reshape(b, nk, H, DH)
        v = (context @ Wv.T).reshape(b, nk, H, DH)
        sim = jnp.einsum('bihd,bjhd->bhij', q, k) * SCALE
        attn = jax.nn.softmax(sim, axis=-1)
        out = jnp.einsum('bhij,bjhd->bihd', attn, v).reshape(b, nq, H * DH)
        return out @ Wo.T + bo

    def _L0_ffn_ref(inputs, gate_w, gate_b, expert_w, expert_b):
        import jax, jax.numpy as jnp
        import numpy as np
        THRESHOLD = 0.1
        d = inputs.shape[-1]
        x = inputs.reshape(-1, d)
        gate_logits = jax.nn.softmax(x @ gate_w + gate_b, axis=-1)
        selected = (gate_logits >= THRESHOLD).astype(x.dtype)
        weights = gate_logits * selected
        wsum = jnp.sum(weights, axis=-1, keepdims=True)
        weights = weights / jnp.where(wsum == 0, jnp.ones_like(wsum), wsum)
        E = expert_w.shape[0]
        out = jnp.zeros((x.shape[0], expert_w.shape[-1]), dtype=x.dtype)
        for e in range(E):
            out = out + weights[:, e:e + 1] * (x @ expert_w[e] + expert_b[e])
        return out.reshape(*inputs.shape[:-1], out.shape[-1])

    def _L1_xattn_ref(q, k, v, wq, bq, wk, bk, wv, bv, wo, bo):
        import jax, jax.numpy as jnp
        import numpy as np
        B, S, D, H = (4, 512, 256, 16)
        DK = D // H
        b, s, _ = q.shape

        def proj(x, w, bias):
            y = x @ w + bias
            return y.reshape(b, -1, H, DK).transpose(0, 2, 1, 3)
        qh, kh, vh = (proj(q, wq, bq), proj(k, wk, bk), proj(v, wv, bv))
        scores = jnp.einsum('bhqd,bhkd->bhqk', qh, kh) / np.sqrt(DK).astype(jnp.float32)
        attn = jax.nn.softmax(scores, axis=-1)
        out = jnp.einsum('bhqk,bhkd->bhqd', attn, vh)
        out = out.transpose(0, 2, 1, 3).reshape(b, s, D)
        return out @ wo + bo

    def _L1_ffn_ref(hidden_states, router_indices, routing_weights, gate_up_proj, gate_up_proj_bias, down_proj, down_proj_bias):
        import jax, jax.numpy as jnp
        import numpy as np
        NUM_EXPERTS = 8
        HIDDEN = 256
        INTER = 256
        BATCH = 2
        SEQ = 256
        TOP_K = 2
        SWIGLU_ALPHA = 1.702
        LIMIT = 7.0

        def _grouped_mm(x, w, expert_ids):
            onehot = jax.nn.one_hot(expert_ids, w.shape[0], dtype=x.dtype)
            y_all = jnp.einsum('tk,ekn->etn', x, w)
            return jnp.einsum('te,etn->tn', onehot, y_all)

        def _gpt_oss_swiglu(x):
            gate = jnp.minimum(x[..., ::2], LIMIT)
            up = jnp.clip(x[..., 1::2], -LIMIT, LIMIT)
            glu = gate * jax.nn.sigmoid(gate * SWIGLU_ALPHA)
            return (up + 1.0) * glu
        B = hidden_states.shape[0]
        H = hidden_states.shape[-1]
        x = hidden_states.reshape(-1, H)
        M = x.shape[0]
        top_k = router_indices.shape[1]
        num_experts = gate_up_proj.shape[0]
        topk_weights = jnp.take_along_axis(routing_weights, router_indices, axis=1)
        flat_experts = router_indices.reshape(-1)
        sort_idx = jnp.argsort(flat_experts)
        sorted_pos = sort_idx // top_k
        expert_sorted = flat_experts[sort_idx]
        grouped = x[sorted_pos]
        gate_up = _grouped_mm(grouped, gate_up_proj, expert_sorted)
        gate_up = gate_up + gate_up_proj_bias[expert_sorted]
        inter = _gpt_oss_swiglu(gate_up)
        down = _grouped_mm(inter, down_proj, expert_sorted)
        down = down + down_proj_bias[expert_sorted]
        down = down * topk_weights.reshape(-1)[sort_idx][:, None]
        out = jnp.zeros((M, H), x.dtype).at[sorted_pos].add(down)
        return out.reshape(B, -1, H)
    x = x + jnp.tanh(g_xattn[0]) * _L0_xattn_ref(_layernorm(x, axis=-1), ctx_1024, L0_xattn_Wq, L0_xattn_Wk, L0_xattn_Wv, L0_xattn_Wo, L0_xattn_bo)
    x = x + jnp.tanh(g_ffn[0]) * _L0_ffn_ref(_layernorm(x, axis=-1), L0_ffn_gate_w, L0_ffn_gate_b, L0_ffn_expert_w, L0_ffn_expert_b)
    x = x + jnp.tanh(g_xattn[1]) * _L1_xattn_ref(_layernorm(x, axis=-1), ctx_1024, ctx_1024, L1_xattn_wq, L1_xattn_bq, L1_xattn_wk, L1_xattn_bk, L1_xattn_wv, L1_xattn_bv, L1_xattn_wo, L1_xattn_bo)
    x = x + jnp.tanh(g_ffn[1]) * _L1_ffn_ref(_layernorm(x, axis=-1), L1_ffn_router_indices, L1_ffn_routing_weights, L1_ffn_gate_up_proj, L1_ffn_gate_up_proj_bias, L1_ffn_down_proj, L1_ffn_down_proj_bias)
    return x

_drawn_inputs = setup_inputs


def setup_inputs(seed=0):
    import zlib

    import numpy as np

    out = dict(_drawn_inputs(seed))
    spreads = {'g_ffn': (-1.0, 0.6),
     'L0_xattn_bo': (0.0, 0.1),
     'L0_ffn_gate_b': (0.0, 0.272),
     'L0_ffn_expert_b': (0.0, 0.1),
     'L1_xattn_bq': (0.0, 0.417),
     'L1_xattn_bk': (0.0, 2.0),
     'L1_xattn_bv': (0.0, 0.1),
     'L1_xattn_bo': (0.0, 0.1)}
    factors = {'L0_xattn_Wq': 8.0,
     'L0_xattn_Wk': 8.0,
     'L1_ffn_routing_weights': 8.0,
     'L1_ffn_gate_up_proj': 8.0,
     'L1_ffn_gate_up_proj_bias': 8.0,
     'L1_ffn_down_proj': 8.0,
     'L1_ffn_down_proj_bias': 36.08}
    for name, (base, spread) in spreads.items():
        noise = np.random.default_rng([zlib.crc32(name.encode()), seed]).standard_normal(out[name].shape)
        drawn = base * np.exp(spread * noise) if base else spread * noise
        out[name] = jnp.asarray(drawn.astype(out[name].dtype))
    for name, factor in factors.items():
        out[name] = (out[name] * factor).astype(out[name].dtype)
    return out
```

```python
from contextlib import ExitStack

import concourse.bass as bass
from concourse import mybir

F32 = mybir.dt.float32
F32R = mybir.dt.float32r
I32 = mybir.dt.int32
ALU = mybir.AluOpType
ACT = mybir.ActivationFunctionType
AX_X = mybir.AxisListType.X

P = 128
B, S, D = 64, 256, 256
NK = 120
T = S // P
KD = D // P
H = 16
DH0, DH1 = 64, 16
INNER = H * DH0
NPAIR = H // 2
HPT1 = P // DH1
NE = 8
NTOK = 512
TT = NTOK // P
EPS = 1e-5
THRESHOLD = 0.1
SWIGLU_ALPHA, LIMIT = 1.702, 7.0
SCALE0, SCALE1 = DH0 ** -0.5, DH1 ** -0.5

X_TR, X_CTX, X_K, X_V, X_Q, X_MAX, X_MAXT, X_OUT = 0, 1, 2, 4, 6, 10, 18, 19
X_JOBS = 20
(Y_CTX, Y_TR2, Y_K, Y_V, Y_GATE, Y_WT, Y_EB, Y_FFN, Y_TR3, Y_Q, Y_MAX, Y_MAXT, Y_OUT) = (
    0, 1, 2, 3, 4, 5, 6, 7, 15, 16, 17, 25, 26)
Y_JOBS = 28
Y_LAG = 6


def steps(x, y, nxt):
    out = []

    def xs(*names):
        if x is not None:
            out.extend(names)

    def ys(*names):
        if y is not None:
            out.extend(names)

    ys(("y_norm2", 0))
    xs(("x_tr", 0), ("x_ctx", 0))
    ys(("y_ctx", 0))
    out.append(("n_load", 0))
    xs(("x_k", 0), ("x_k", 1), ("x_v", 0), ("x_v", 1), ("x_q", 0), ("x_q", 1), ("x_q", 2), ("x_q", 3))
    ys(("y_tr2", 0), ("y_k", 0), ("y_v", 0), ("y_gate", 0))
    xs(*[("x_max", j) for j in range(4)])
    ys(("y_wt", 0), ("y_eb", 0))
    for j in range(4):
        ys(("y_ffn", j))
        xs(("x_max", 4 + j))
    ys(*[("y_ffn", j) for j in range(4, 8)])
    ys(("y_norm3", 0))
    xs(("x_maxt", 0))
    for s in range(NPAIR + Y_LAG + 2):
        if s < NPAIR:
            xs(("x_st", s))
        if 0 <= s - Y_LAG < NPAIR:
            ys(("y_st", s - Y_LAG))
        if 0 <= s - 1 < NPAIR:
            xs(("x_pv", s - 1))
        if 0 <= s - 1 - Y_LAG < NPAIR:
            ys(("y_pv", s - 1 - Y_LAG))
        if 0 <= s - 2 < NPAIR:
            xs(("x_hi", s - 2))
        if s == 1:
            ys(("y_tr3", 0))
        if s == 2:
            ys(("y_q", 0))
        if s == 3:
            ys(*[("y_max", j) for j in range(4)])
        if s == 4:
            ys(*[("y_max", j) for j in range(4, 8)])
        if s == Y_LAG - 1:
            ys(("y_maxt", 0))
        if s in (Y_LAG + 5, Y_LAG + 9):
            ys(("y_hi", (s - Y_LAG - 5) // 4))
        if s == 7 and nxt is not None:
            out.append(("n_norm", 0))
        if 9 <= s < 13:
            xs(("x_out", s - 9))
    ys(("y_out", 0), ("y_out", 1))
    return out


class Signal:

    def __init__(self, sem, per):
        self.sem, self.per = sem, per

    def wait(self, eng, i, k):
        value = i * self.per + k
        if isinstance(value, int) and value <= 0:
            return
        eng.wait_ge(self.sem, value)


class Ring:

    def __init__(self, banks, filled, emptied):
        self.banks, self.filled, self.emptied, self.n = banks, filled, emptied, len(banks)

    def bank(self, job):
        return self.banks[job % self.n]

    def to_fill(self, eng, i, job):
        self.emptied[job % self.n].wait(eng, i, job // self.n)

    def full(self, eng, i, job):
        self.filled[job % self.n].wait(eng, i, job // self.n + 1)

    def empty(self, eng, i, job):
        self.emptied[job % self.n].wait(eng, i, job // self.n + 1)

    def has_filled(self, ins, job):
        ins.then_inc(self.filled[job % self.n].sem, 1)

    def has_emptied(self, ins, job):
        ins.then_inc(self.emptied[job % self.n].sem, 1)


def flamingo_stack(nc, x, ctx, gates, wq, wk, wv, wo, bo, gate_b, ew, eb, w1, w1k, w1v, bqkv1, bo1,
                   router_idx, router_w, gu, gu_b, dn, dn_b, out):
    es = ExitStack()
    with es:
        def sb(name, shape, dt=F32):
            return es.enter_context(nc.sbuf_tensor(name, shape, dt))

        def pb(name):
            return es.enter_context(nc.psum_tensor(name, [P, 512], F32))

        def sem(name):
            return es.enter_context(nc.semaphore(name))

        def signal(name, per=1):
            return Signal(sem(name), per)

        def pair(name, shape):
            return sb(name + "_hi", shape, F32R), sb(name + "_lo", shape, F32R)

        wq_s = pair("wq", [P, KD, INNER])
        wo_s = pair("wo", [P, INNER // P, D])
        ew_s = pair("ew", [P, KD, NE * D])
        w1_s = pair("w1", [P, 2 * KD * D + KD * NE])
        wk_s, wv_s = sb("wk_s", [P, KD, INNER]), sb("wv_s", [P, KD, INNER])
        w1k_s, w1v_s = sb("w1k_s", [P, KD, D]), sb("w1v_s", [P, KD, D])
        eb_s = sb("eb_s", [P, D])
        stage = (wk_s, wv_s)

        def w1q_s(n):
            return w1_s[n][:, 0:KD * D].rearrange("p (k n) -> p k n", k=KD)

        def w1o_s(n):
            return w1_s[n][:, KD * D:2 * KD * D].rearrange("p (k n) -> p k n", k=KD)

        def gate_s(n):
            return w1_s[n][:, 2 * KD * D:].rearrange("p (k n) -> p k n", k=KD)

        ident = sb("ident", [P, P])
        ident_r = sb("ident_r", [P, H], F32R)
        own_head = sb("own_head", [P, HPT1])
        tg = sb("tg", [P, 4])
        bo_tg, bo1_tg = sb("bo_tg", [P, D]), sb("bo1_tg", [P, D])
        gate_b_s = sb("gate_b_s", [P, NE])
        bqkv1_s = sb("bqkv1_s", [P, 3, KD])
        neg_half, eps = sb("neg_half", [P, TT]), sb("eps", [P, T])
        x_in, x_xn = sb("x_in", [P, T, D]), sb("x_xn", [P, T, D])
        x_res = sb("x_res", [P, T, D])
        x_st6, x_mv, x_rstd = sb("x_st6", [P, T, 6]), sb("x_mv", [P, T, 2]), sb("x_rstd", [P, 2, T])
        xT = pair("xT", [P, KD, S])
        ctx_in, ctxT = sb("ctx_in", [NK, D]), sb("ctxT", [P, KD, NK])
        q = pair("q", [P, NPAIR, S])
        kbd = pair("kbd", [P, H, NK])
        vx = sb("vx", [P, H, P])
        x_nm, x_nmT = sb("x_nm", [P, T, H]), sb("x_nmT", [P, S], F32R)
        x_prob = sb("x_prob", [NK, 2, S])
        x_an = sb("x_an", [P, 2, S])
        x1 = sb("x1", [P, T, D])
        y_xn = sb("y_xn", [P, T, D])
        y_st6, y_mv, y_rstd = sb("y_st6", [P, T, 6]), sb("y_mv", [P, T, 2]), sb("y_rstd", [P, 2, T])
        yT = pair("yT", [P, KD, S])
        acc = sb("acc", [P, T, D])
        ctx_in1, ctxT1 = sb("ctx_in1", [NK, D]), sb("ctxT1", [P, KD, NK])
        lg, lg_n = sb("lg", [P, T, NE]), sb("lg_n", [P, 4, T])
        wT = sb("wT", [P, S])
        q1 = pair("q1", [P, KD, S])
        k1 = pair("k1", [P, KD, NK])
        kbd1 = pair("kbd1", [P, KD, HPT1, NK])
        VX1 = H * P + 4 * DH1 + P
        vx1 = sb("vx1", [P, VX1])
        y_nm, y_nmT = sb("y_nm", [P, T, H]), sb("y_nmT", [P, S], F32R)
        y_prob = sb("y_prob", [NK, 2, S])
        y_an = sb("y_an", [P, S])
        y_x3 = sb("y_x3", [P, T, D])

        def v1_block(g, ones):
            at = g * 4 * P + 64 * ((g + ones) % 2)
            return vx1[:, at:at + 4 * (P + DH1)].rearrange("p (j c) -> p j c", j=4)[:, :, 0:DH1]

        xg, yg = [pb("xg0"), pb("xg1")], [pb("yg0"), pb("yg1")]
        x_scores, y_scores, x_pvo, y_pvo = pb("x_scores"), pb("y_scores"), pb("x_pvo"), pb("y_pvo")

        stage_in = [sem("stage_in0"), sem("stage_in1")]
        small_in = sem("small_in")
        last_in = sem("last_in")
        split_hi, split_lo = sem("split_hi"), sem("split_lo")
        tanh_done, const_done, setup_done = sem("tanh_done"), sem("const_done"), sem("setup_done")

        xr = Ring(xg, [signal(f"x_filled{n}", X_JOBS // 2) for n in range(2)],
                  [signal(f"x_emptied{n}", X_JOBS // 2) for n in range(2)])
        yr = Ring(yg, [signal(f"y_filled{n}", Y_JOBS // 2) for n in range(2)],
                  [signal(f"y_emptied{n}", Y_JOBS // 2) for n in range(2)])
        x_loaded, ctx_loaded, ctx1_loaded = (signal("x_loaded", 16), signal("ctx_loaded", 16),
                                             signal("ctx1_loaded", 16))
        x_stats, x_rs, x_resd, x_normed = (signal("x_stats", 2), signal("x_rs", 2), signal("x_resd"),
                                           signal("x_normed"))
        x_hi = signal("x_hi", 7)
        x_scored, x_probs, x_mixed = (signal("x_scored", NPAIR), signal("x_probs", NPAIR),
                                      signal("x_mixed", NPAIR))
        x_sums, x_recip, x_attn = (signal("x_sums", NPAIR), signal("x_recip", NPAIR),
                                   signal("x_attn", NPAIR))
        x_attn_hi, x_attn_lo = signal("x_attn_hi", NPAIR), signal("x_attn_lo", NPAIR)
        y_stats, y_rs, y_resd, y_normed = (signal("y_stats", 4), signal("y_rs", 4), signal("y_resd"),
                                           signal("y_normed", 2))
        y_hi, y_kmask = signal("y_hi", 4), signal("y_kmask", 1)
        y_gated, y_exp = signal("y_gated", 10), signal("y_exp")
        y_acc = signal("y_acc", NE)
        y_scored, y_probs, y_mixed = (signal("y_scored", NPAIR), signal("y_probs", NPAIR),
                                      signal("y_mixed", NPAIR))
        y_sums, y_recip, y_attn = signal("y_sums", 2), signal("y_recip", 2), signal("y_attn", 2)
        y_attn_hi, y_attn_lo = signal("y_attn_hi", 2), signal("y_attn_lo", 2)
        y_stored = signal("y_stored", 16)
        m_in, m_w = sem("m_in"), [sem("m_w0"), sem("m_w1")]
        (m_norm, m_rs, m_coef, m_tr, m_trc, m_up, m_gate, m_upc, m_sig, m_inter, m_down, m_acc, m_stored, m_glu) = (
            sem(n) for n in ("m_norm", "m_rs", "m_coef", "m_tr", "m_trc", "m_up", "m_gate", "m_upc", "m_sig",
                             "m_inter", "m_down", "m_acc", "m_stored", "m_glu"))

        x_rows = x.rearrange("b (t p) d -> b p t d", p=P)
        out_rows = out.rearrange("b (t p) d -> b p t d", p=P)

        def flat(a):
            return a.rearrange("p k n -> p (k n)")

        wv_f, vx_f, wk_f = flat(wv_s[:]), flat(vx[:]), flat(wk_s[:])
        xm = wv_f[:, 0:TT * D].rearrange("p (t d) -> p t d", t=TT)
        xmn = wv_f[:, TT * D:2 * TT * D].rearrange("p (t d) -> p t d", t=TT)
        xmT = vx_f[:, 0:KD * NTOK].rearrange("p (k n) -> p k n", k=KD)
        inter = vx_f[:, KD * NTOK:2 * KD * NTOK].rearrange("p (k n) -> p k n", k=KD)
        gu_s = [wk_f[:, r * 4 * D:(r + 1) * 4 * D].rearrange("p (k g n) -> p k g n", k=KD, g=2) for r in range(2)]
        dn_s = [w1k_s, w1v_s]
        m_g, m_u, m_s = flat(x_in[:]), flat(x_xn[:]), flat(x_res[:])
        m_cT = flat(acc[:])
        M_COEF = 1 + 3 * TT
        coef, coef_k = sb("coef", [P, NE, TT]), sb("coef_k", [P, NE])
        rw_s, idx_s, idx_f = sb("rw_s", [P, TT, NE]), sb("idx_s", [P, TT, 2], I32), sb("idx_f", [P, TT, 2])
        gu_b_s, expert_no = sb("gu_b_s", [P, NE, KD, 2]), sb("expert_no", [P, NE])
        m_st6, m_mv, m_rstd = sb("m_st6", [P, TT, 6]), sb("m_mv", [P, TT, 2]), sb("m_rstd", [P, 2, TT])

        block = es.enter_context(nc.Block())

        def run(eng, table):
            def one(i, y, nxt):
                for name, k in steps(i, y, nxt):
                    if name == "n_load":
                        if name in table:
                            table[name](i, nxt)
                    elif name in table:
                        table[name](nxt if name == "n_norm" else i if name[0] == "x" else y, k)

            one(0, None, 1)
            one(1, 0, 2)
            with eng.Fori(2, B - 1) as i:
                one(i, i - 1, i + 1)
            one(B - 1, B - 2, None)
            one(None, B - 1, None)

        splits = [(flat(wq), flat(wq_s[0][:]), flat(wq_s[1][:])), (flat(wo), flat(wo_s[0][:]), flat(wo_s[1][:]))]
        splits += [(ew[:, k, :], ew_s[0][:, k, :], ew_s[1][:, k, :]) for k in range(KD)]
        splits += [(w1, w1_s[0][:], w1_s[1][:])]
        NSPLIT = len(splits)

        def staged(n):
            return flat(stage[n % 2][:])[:, 0:splits[n][0].shape[1]]

        SMALL = 16 * 9
        ZEROED, CONST = 9, 14
        SET_UP = 5

        @block.sync
        def _(sp):
            sp.dma_start(x_in[:], x_rows[0]).then_inc(x_loaded.sem, 16)
            sp.dma_start(ctx_in[:], ctx[0]).then_inc(ctx_loaded.sem, 16)
            for n in range(NSPLIT):
                if n >= 2:
                    sp.wait_ge(split_lo, n - 1)
                sp.dma_start(staged(n), splits[n][0]).then_inc(stage_in[n % 2], 16)
                if n == 0:
                    for dst, src in ((tg, gates), (bo_tg, bo), (bo1_tg, bo1), (gate_b_s, gate_b)):
                        sp.dma_start(dst[:], src.partition_broadcast(P)).then_inc(small_in, 16)
                    for dst, src in ((bqkv1_s, bqkv1), (rw_s, router_w), (idx_s, router_idx), (gu_b_s, gu_b)):
                        sp.dma_start(dst[:], src).then_inc(small_in, 16)
                    sp.wait_ge(const_done, ZEROED)
                    sp.dma_start(eb_s[0:NE, :], eb).then_inc(small_in, 16)
            sp.dma_start(w1k_s[:], w1k).then_inc(last_in, 16)
            sp.dma_start(w1v_s[:], w1v).then_inc(last_in, 16)
            sp.wait_ge(split_lo, NSPLIT)
            sp.dma_start(wk_s[:], wk).then_inc(last_in, 16)
            sp.dma_start(wv_s[:], wv).then_inc(last_in, 16)

            def y_out(i, t):
                if t == T - 1:
                    yr.empty(sp, i, Y_OUT)
                    yr.empty(sp, i, Y_OUT + 1)
                    sp.dma_start(out_rows[i], y_x3[:]).then_inc(y_stored.sem, 16)

            run(sp, {"y_out": y_out})
            sp.wait_ge(y_stored.sem, 16 * B)
            for b in range(NTOK // S):
                sp.dma_start(xm[:, b * T:(b + 1) * T, :], out_rows[b]).then_inc(m_in, 16)
            sp.dma_start(eb_s[0:NE, :], dn_b).then_inc(m_in, 16)
            for e in range(NE):
                if e >= 2:
                    sp.wait_ge(m_down, e)
                sp.dma_start(gu_s[e % 2], gu[e]).then_inc(m_w[e % 2], 16)
                sp.dma_start(dn_s[e % 2][:], dn[e]).then_inc(m_w[e % 2], 16)
            sp.wait_ge(m_acc, 1 + NE)
            for b in range(NTOK // S):
                sp.dma_start(out_rows[b], xm[:, b * T:(b + 1) * T, :]).then_inc(m_stored, 16)
            sp.wait_ge(m_stored, 16 * (NTOK // S))

        @block.gpsimd
        def _(pool):
            g = nc.gpsimd
            for tile, value in ((ident, 0.0), (own_head, 1.0), (neg_half, -0.5), (eps, EPS), (eb_s, 0.0), (vx, 1.0), (vx1, 0.0),
                                (wT, 0.0)):
                g.memset(tile[:], value).then_inc(const_done, 1)
            g.iota(expert_no[:], pattern=[[1, NE]], base=0, channel_multiplier=0,
                   allow_small_or_imprecise_dtypes=True).then_inc(const_done, 1)
            pool.wait_ge(const_done, ZEROED)
            g.affine_select(out=ident[:], in_=ident[:], compare_op=ALU.not_equal, fill=1.0, base=0,
                            pattern=[[-1, P]], channel_multiplier=1).then_inc(const_done, 1)
            g.affine_select(out=own_head[:], in_=own_head[:], compare_op=ALU.is_ge, fill=0.0, base=0,
                            pattern=[[-DH1, HPT1]], channel_multiplier=1).then_inc(const_done, 1)
            pool.wait_ge(const_done, ZEROED + 2)
            g.affine_select(out=own_head[:], in_=own_head[:], compare_op=ALU.is_ge, fill=0.0, base=DH1 - 1,
                            pattern=[[DH1, HPT1]], channel_multiplier=-1).then_inc(const_done, 1)
            for half in range(2):
                for gr in range(half, 4, 2):
                    last = g.memset(v1_block(gr, 1), 1.0)
                last.then_inc(const_done, 1)

            def rstd(mv, rs, stats, k_stats, done, k, i):
                stats.wait(pool, i, k_stats)
                g.tensor_tensor(rs[:, 0, :], mv[:, :, 1], eps[:], ALU.add).then_inc(done.sem, 1)
                done.wait(pool, i, k + 1)
                g.tensor_tensor(rs[:, 1, :], rs[:, 0, :], neg_half[:, 0:T], ALU.pow).then_inc(done.sem, 1)

            def n_norm(i, _):
                rstd(x_mv, x_rstd, x_stats, 2, x_rs, 0, i)

            def x_tr(i, _):
                x_loaded.wait(pool, i, 16)
                xr.emptied[X_OUT % 2].wait(pool, i, 0)
                g.tensor_tensor(x_res[:], x_in[:], bo_tg[:].unsqueeze(1).broadcast_to([P, T, D]),
                                ALU.add).then_inc(x_resd.sem, 1)

            def y_norm2(i, _):
                rstd(y_mv, y_rstd, y_stats, 2, y_rs, 0, i)

            def y_norm3(i, _):
                rstd(y_mv, y_rstd, y_stats, 4, y_rs, 2, i)
                y_normed.wait(pool, i, 2)
                g.tensor_tensor(acc[:], acc[:], bo1_tg[:].unsqueeze(1).broadcast_to([P, T, D]),
                                ALU.add).then_inc(y_resd.sem, 1)

            def y_k(i, _):
                yr.empty(pool, i, Y_K)
                for part in range(2):
                    for m in range(KD):
                        last = g.tensor_tensor(
                            kbd1[part][:, m, :, :],
                            k1[part][:, m, :].bitcast(F32).unsqueeze(1).broadcast_to([P, HPT1, NK]),
                            own_head[:].unsqueeze(2).broadcast_to([P, HPT1, NK]), ALU.mult)
                last.then_inc(y_kmask.sem, 1)

            def x_lo(i, p):
                x_attn_hi.wait(pool, i, p + 1)
                g.tensor_tensor(q[1][:, p, :], x_an[:, p % 2, :], q[0][:, p, :].bitcast(F32),
                                ALU.subtract).then_inc(x_attn_lo.sem, 1)

            pool.wait_ge(setup_done, SET_UP)
            n_norm(0, 0)
            run(pool, {"n_norm": n_norm, "x_tr": x_tr, "y_norm2": y_norm2, "y_norm3": y_norm3, "y_k": y_k,
                       "x_hi": x_lo})
            pool.wait_ge(m_norm, 2)
            g.tensor_scalar(m_rstd[:, 0, :], m_mv[:, :, 1], EPS, None, ALU.add).then_inc(m_rs, 1)
            pool.wait_ge(m_rs, 1)
            g.tensor_tensor(m_rstd[:, 1, :], m_rstd[:, 0, :], neg_half[:], ALU.pow).then_inc(m_rs, 1)
            g.memset(m_cT, 0.0).then_inc(m_rs, 1)

        @block.scalar
        def _(act):
            a = nc.scalar
            for n in range(NSPLIT):
                act.wait_ge(stage_in[n % 2], 16 * (n // 2 + 1))
                a.copy(splits[n][1], staged(n)).then_inc(split_hi, 1)
            act.wait_ge(small_in, SMALL)
            a.activation(tg[:], tg[:], ACT.Tanh).then_inc(tanh_done, 1)
            act.wait_ge(const_done, CONST)
            a.copy(ident_r[:], ident[:, 0:H]).then_inc(setup_done, 1)

            def hi_of(ring, done, i, job, cols, dst):
                ring.full(act, i, job)
                a.copy(dst, ring.bank(job)[:, 0:cols]).then_inc(done.sem, 1)

            def x_tr(i, _):
                hi_of(xr, x_hi, i, X_TR, KD * S, flat(xT[0][:]))

            def x_ctx(i, _):
                xr.full(act, i, X_CTX)
                xr.has_emptied(a.copy(flat(ctxT[:]), xr.bank(X_CTX)[:, 0:KD * NK]), X_CTX)

            def y_ctx(i, _):
                yr.full(act, i, Y_CTX)
                yr.has_emptied(a.copy(flat(ctxT1[:]), yr.bank(Y_CTX)[:, 0:KD * NK]), Y_CTX)

            def n_load(i, nxt):
                if nxt is not None:
                    x_resd.wait(act, i, 1)
                    act.dma_start(x_in[:], x_rows[nxt]).then_inc(x_loaded.sem, 16)
                    act.dma_start(ctx_in[:], ctx[nxt]).then_inc(ctx_loaded.sem, 16)
                if i is not None:
                    act.dma_start(ctx_in1[:], ctx[i]).then_inc(ctx1_loaded.sem, 16)

            def x_k(i, c):
                xr.full(act, i, X_K + c)
                view = xr.bank(X_K + c)[:, 0:4 * NK].rearrange("p (m n) -> p m n", m=4)
                for half in range(2):
                    rows = slice(64 * half, 64 * half + 64)
                    last = a.copy(kbd[0][rows, 8 * c + half:8 * c + 8:2, :], view[rows])
                last.then_inc(x_hi.sem, 1)

            def x_v(i, c):
                xr.full(act, i, X_V + c)
                view = xr.bank(X_V + c)[0:NK, :].rearrange("p (m o d) -> p m o d", o=2, d=DH0)
                for odd in range(2):
                    last = a.copy(vx[0:NK, 8 * c + odd:8 * c + 8:2, 64 * odd:64 * odd + 64], view[:, :, odd, :])
                xr.has_emptied(last, X_V + c)

            def x_q(i, c):
                hi_of(xr, x_hi, i, X_Q + c, 2 * S, flat(q[0][:, 2 * c:2 * c + 2, :]))

            def y_tr(job):
                return lambda i, _: hi_of(yr, y_hi, i, job, KD * S, flat(yT[0][:]))

            def biased_hi(i, job, cols, dst, b):
                yr.full(act, i, job)
                for m in range(KD):
                    last = a.activation(dst[:, m, :], yr.bank(job)[:, m * cols:(m + 1) * cols], ACT.Identity,
                                        bias=bqkv1_s[:, b, m:m + 1])
                last.then_inc(y_hi.sem, 1)

            def y_k(i, _):
                y_kmask.wait(act, i, 0)
                biased_hi(i, Y_K, NK, k1[0], 1)

            def y_q(i, _):
                biased_hi(i, Y_Q, S, q1[0], 0)

            def y_v(i, _):
                yr.full(act, i, Y_V)
                for gr in range(4):
                    last = a.copy(v1_block(gr, 0)[0:NK], yr.bank(Y_V)[0:NK, gr * 64:(gr + 1) * 64]
                                  .rearrange("p (j d) -> p j d", j=4))
                yr.has_emptied(last, Y_V)

            def y_gate(i, _):
                y_gated.wait(act, i, 2)
                a.activation(flat(lg[:]), flat(lg[:]), ACT.Exp).then_inc(y_exp.sem, 1)

            def y_wt(i, _):
                yr.full(act, i, Y_WT)
                yr.has_emptied(a.copy(wT[0:NE, :], yr.bank(Y_WT)[0:NE, 0:S]), Y_WT)

            def maxt(ring, job, dst):
                def step(i, _):
                    ring.full(act, i, job)
                    ring.has_emptied(a.copy(dst[0:H, :], ring.bank(job)[0:H, 0:S]), job)
                return step

            def st(scored, mixed, probs, scores, prob, scale):
                def step(i, p):
                    scored.wait(act, i, p + 1)
                    mixed.wait(act, i, p)
                    a.activation(flat(prob[:]), scores[0:NK, :], ACT.Exp, scale=scale).then_inc(probs.sem, 1)
                return step

            def sums(pvo, an):
                a.copy(an[0:64, :], pvo[64:128, 0:S])
                return a.copy(an[64:128, :], pvo[0:64, S:2 * S])

            def x_pv(i, p):
                x_mixed.wait(act, i, p + 1)
                if p >= 2:
                    x_attn_lo.wait(act, i, p - 1)
                else:
                    x_attn_lo.wait(act, i, 0)
                sums(x_pvo, x_an[:, p % 2, :]).then_inc(x_sums.sem, 1)

            def x_attn_split(i, p):
                x_attn.wait(act, i, p + 1)
                a.copy(q[0][:, p, :], x_an[:, p % 2, :]).then_inc(x_attn_hi.sem, 1)

            def y_pv(i, p):
                if p % 4 == 3:
                    y_mixed.wait(act, i, p + 1)
                    y_attn_lo.wait(act, i, p // 4)
                    sums(y_pvo, y_an[:]).then_inc(y_sums.sem, 1)

            def y_attn_split(i, m):
                y_attn.wait(act, i, m + 1)
                a.activation(q1[0][:, m, :], y_an[:], ACT.Identity,
                             bias=bqkv1_s[:, 2, m:m + 1]).then_inc(y_attn_hi.sem, 1)

            run(act, {"x_tr": x_tr, "x_ctx": x_ctx, "y_ctx": y_ctx, "n_load": n_load, "x_k": x_k, "x_v": x_v,
                      "x_q": x_q, "y_tr2": y_tr(Y_TR2), "y_k": y_k, "y_v": y_v, "y_gate": y_gate, "y_wt": y_wt,
                      "y_tr3": y_tr(Y_TR3), "y_q": y_q,
                      "x_maxt": maxt(xr, X_MAXT, x_nmT), "y_maxt": maxt(yr, Y_MAXT, y_nmT),
                      "x_st": st(x_scored, x_mixed, x_probs, x_scores, x_prob, SCALE0),
                      "y_st": st(y_scored, y_mixed, y_probs, y_scores, y_prob, SCALE1),
                      "x_pv": x_pv, "y_pv": y_pv, "x_hi": x_attn_split, "y_hi": y_attn_split})
            for k in range(KD):
                act.wait_ge(m_tr, k + 1)
                a.copy(xmT[:, k, :], (x_pvo, y_pvo)[k][:]).then_inc(m_trc, 1)
            act.wait_ge(m_tr, KD + 1)
            act.wait_ge(m_rs, 3)
            a.copy(m_cT[0:NE, :], xg[0][0:NE, :]).then_inc(m_trc, 1)
            for n in range(KD * NE):
                act.wait_ge(m_gate, n + 1)
                if n >= 1:
                    act.wait_ge(m_inter, n)
                a.activation(m_s, m_g, ACT.Sigmoid, scale=SWIGLU_ALPHA).then_inc(m_sig, 1)

        @block.tensor
        def _(pe):
            t_ = nc.tensor
            pe.wait_ge(setup_done, SET_UP)
            pe.wait_ge(const_done, CONST)
            pe.wait_ge(split_lo, NSPLIT)
            pe.wait_ge(last_in, 16 * 4)

            def products(out_, terms, first=True, last=True):
                n = 0
                for lhsT, rhs in terms:
                    for u, v in ((0, 0), (1, 0), (0, 1)):
                        n += 1
                        ins = t_.matmul(out_, lhsT[u], rhs[v], start=first and n == 1,
                                        stop=last and n == 3 * len(terms))
                return ins

            def products32(out_, terms):
                for n, (lhsT, rhs) in enumerate(terms):
                    ins = t_.matmul(out_, lhsT, rhs, start=n == 0, stop=n == len(terms) - 1)
                return ins

            def both(parts, *at):
                return parts[0][at], parts[1][at]

            ALL = slice(None)

            def transposes(ring, job, src, normed, k_normed):
                def step(i, _):
                    normed.wait(pe, i, k_normed)
                    ring.to_fill(pe, i, job)
                    for k in range(KD):
                        for t in range(T):
                            ins = t_.transpose(ring.bank(job)[:, k * S + t * P:k * S + (t + 1) * P],
                                               src[:, t, k * P:(k + 1) * P], ident[:])
                    ring.has_filled(ins, job)
                return step

            def ctx_transposes(ring, job, src, loaded):
                def step(i, _):
                    loaded.wait(pe, i, 16)
                    ring.to_fill(pe, i, job)
                    for k in range(KD):
                        ins = t_.transpose(ring.bank(job)[:, k * NK:(k + 1) * NK], src[:, k * P:(k + 1) * P],
                                           ident[0:NK, 0:NK])
                    ring.has_filled(ins, job)
                return step

            def x_k(i, c):
                xr.empty(pe, i, X_CTX)
                xr.to_fill(pe, i, X_K + c)
                for m in range(4):
                    col = (4 * c + m) * P
                    ins = products32(xr.bank(X_K + c)[:, m * NK:(m + 1) * NK],
                                     [(wk_s[:, k, col:col + P], ctxT[:, k, :]) for k in range(KD)])
                xr.has_filled(ins, X_K + c)

            def x_v(i, c):
                xr.to_fill(pe, i, X_V + c)
                ins = products32(xr.bank(X_V + c)[0:NK, :],
                                 [(ctxT[:, k, :], wv_s[:, k, 512 * c:512 * (c + 1)]) for k in range(KD)])
                xr.has_filled(ins, X_V + c)

            def x_q(i, c):
                xr.empty(pe, i, X_TR)
                xr.to_fill(pe, i, X_Q + c)
                for m in range(2):
                    col = slice((2 * c + m) * P, (2 * c + m + 1) * P)
                    ins = products(xr.bank(X_Q + c)[:, m * S:(m + 1) * S],
                                   [(both(wq_s, ALL, k, col), both(xT, ALL, k, ALL)) for k in range(KD)])
                xr.has_filled(ins, X_Q + c)

            def x_max(i, j):
                t, c = j // 4, j % 4
                xr.empty(pe, i, X_Q + c)
                xr.to_fill(pe, i, X_MAX + j)
                for m in range(2):
                    p = 2 * c + m
                    ins = t_.matmul(xr.bank(X_MAX + j)[:, m * 2 * NK:(m + 1) * 2 * NK],
                                    q[0][:, p, t * P:(t + 1) * P], flat(kbd[0][:, 2 * p:2 * p + 2, :]),
                                    start=True, stop=True)
                xr.has_filled(ins, X_MAX + j)

            def y_max(i, j):
                t, c = j // 4, j % 4
                yr.empty(pe, i, Y_Q)
                y_kmask.wait(pe, i, 1)
                yr.to_fill(pe, i, Y_MAX + j)
                ins = t_.matmul(yr.bank(Y_MAX + j)[:, 0:4 * NK], q1[0][:, c // 2, t * P:(t + 1) * P],
                                flat(kbd1[0][:, c // 2, 4 * (c % 2):4 * (c % 2) + 4, :]), start=True, stop=True)
                yr.has_filled(ins, Y_MAX + j)

            def maxt(ring, max_job, job, nm):
                def step(i, _):
                    ring.empty(pe, i, max_job + 6)
                    ring.empty(pe, i, max_job + 7)
                    ring.to_fill(pe, i, job)
                    for t in range(T):
                        ins = t_.transpose(ring.bank(job)[0:H, t * P:(t + 1) * P], nm[:, t, :], ident[:])
                    ring.has_filled(ins, job)
                return step

            def st(ring, maxt_job, probs, scored, scores, keys, queries, nmT):
                def step(i, p):
                    ring.empty(pe, i, maxt_job)
                    probs.wait(pe, i, p)
                    for o in range(2):
                        h = 2 * p + o
                        dst = scores[0:NK, o * S:(o + 1) * S]
                        products(dst, [(keys(h), queries(h))], last=False)
                        ins = t_.matmul(dst, ident_r[:, h:h + 1].broadcast_to([P, NK]), nmT[:], start=False,
                                        stop=True)
                    ins.then_inc(scored.sem, 1)
                return step

            def x_pv(i, p):
                x_probs.wait(pe, i, p + 1)
                x_attn.wait(pe, i, p)
                for o in range(2):
                    ins = t_.matmul(x_pvo[:, o * S:(o + 1) * S], vx[0:NK, 2 * p + o, :], x_prob[:, o, :],
                                    start=True, stop=True)
                ins.then_inc(x_mixed.sem, 1)

            def y_pv(i, p):
                y_probs.wait(pe, i, p + 1)
                if p % 4 == 0:
                    y_attn.wait(pe, i, p // 4)
                cols = slice((p // 2) % 2 * S, ((p // 2) % 2 + 1) * S)
                for o in range(2):
                    h = 2 * p + o
                    ins = t_.matmul(y_pvo[:, cols], vx1[0:NK, h * P:(h + 1) * P], y_prob[:, o, :],
                                    start=h % 4 == 0, stop=h % 4 == 3)
                ins.then_inc(y_mixed.sem, 1)

            def x_out(i, c):
                t, k0 = c // 2, (c % 2) * 4
                if c == 0:
                    xr.to_fill(pe, i, X_OUT)
                x_attn_lo.wait(pe, i, k0 + 4)
                ins = products(xr.bank(X_OUT)[:, t * D:(t + 1) * D],
                               [(both(q, ALL, k, slice(t * P, (t + 1) * P)), both(wo_s, ALL, k, ALL))
                                for k in range(k0, k0 + 4)], first=k0 == 0, last=k0 == 4)
                if c == 3:
                    xr.has_filled(ins, X_OUT)

            def y_k(i, _):
                yr.empty(pe, i, Y_CTX)
                yr.to_fill(pe, i, Y_K)
                for m in range(KD):
                    ins = products32(yr.bank(Y_K)[:, m * NK:(m + 1) * NK],
                                     [(w1k_s[:, k, m * P:(m + 1) * P], ctxT1[:, k, :]) for k in range(KD)])
                yr.has_filled(ins, Y_K)

            def y_v(i, _):
                yr.to_fill(pe, i, Y_V)
                ins = products32(yr.bank(Y_V)[0:NK, 0:D], [(ctxT1[:, k, :], w1v_s[:, k, :]) for k in range(KD)])
                yr.has_filled(ins, Y_V)

            def y_gate(i, _):
                yr.empty(pe, i, Y_TR2)
                yr.to_fill(pe, i, Y_GATE)
                for t in range(T):
                    ins = products(yr.bank(Y_GATE)[:, t * NE:(t + 1) * NE],
                                   [(both(yT, ALL, k, slice(t * P, (t + 1) * P)),
                                     (gate_s(0)[:, k, :], gate_s(1)[:, k, :])) for k in range(KD)])
                yr.has_filled(ins, Y_GATE)

            def y_wt(i, _):
                y_gated.wait(pe, i, 10)
                yr.to_fill(pe, i, Y_WT)
                for t in range(T):
                    ins = t_.transpose(yr.bank(Y_WT)[0:NE, t * P:(t + 1) * P], lg[:, t, :], ident[:])
                yr.has_filled(ins, Y_WT)

            def y_eb(i, _):
                yr.empty(pe, i, Y_WT)
                yr.to_fill(pe, i, Y_EB)
                for t in range(T):
                    ins = t_.matmul(yr.bank(Y_EB)[:, t * D:(t + 1) * D], wT[:, t * P:(t + 1) * P], eb_s[:],
                                    start=True, stop=True)
                yr.has_filled(ins, Y_EB)

            def y_ffn(i, j):
                t, n = j % T, j // T
                yr.to_fill(pe, i, Y_FFN + j)
                ins = products(yr.bank(Y_FFN + j)[:], [(both(yT, ALL, k, slice(t * P, (t + 1) * P)),
                                                        both(ew_s, ALL, k, slice(2 * D * n, 2 * D * (n + 1))))
                                                       for k in range(KD)])
                yr.has_filled(ins, Y_FFN + j)

            def y_q(i, _):
                yr.empty(pe, i, Y_TR3)
                yr.to_fill(pe, i, Y_Q)
                for m in range(KD):
                    col = slice(m * P, (m + 1) * P)
                    ins = products(yr.bank(Y_Q)[:, m * S:(m + 1) * S],
                                   [((w1q_s(0)[:, k, col], w1q_s(1)[:, k, col]), both(yT, ALL, k, ALL))
                                    for k in range(KD)])
                yr.has_filled(ins, Y_Q)

            def y_out(i, t):
                y_attn_lo.wait(pe, i, 2)
                yr.to_fill(pe, i, Y_OUT + t)
                ins = products(yr.bank(Y_OUT + t)[:, 0:D],
                               [(both(q1, ALL, k, slice(t * P, (t + 1) * P)),
                                 (w1o_s(0)[:, k, :], w1o_s(1)[:, k, :])) for k in range(KD)])
                yr.has_filled(ins, Y_OUT + t)

            run(pe, {
                "x_tr": transposes(xr, X_TR, x_xn, x_normed, 1),
                "x_ctx": ctx_transposes(xr, X_CTX, ctx_in, ctx_loaded),
                "y_ctx": ctx_transposes(yr, Y_CTX, ctx_in1, ctx1_loaded),
                "x_k": x_k, "x_v": x_v, "x_q": x_q, "y_tr2": transposes(yr, Y_TR2, y_xn, y_normed, 1),
                "y_k": y_k, "y_v": y_v, "y_gate": y_gate, "x_max": x_max, "y_wt": y_wt, "y_eb": y_eb,
                "y_ffn": y_ffn, "x_maxt": maxt(xr, X_MAX, X_MAXT, x_nm),
                "x_st": st(xr, X_MAXT, x_probs, x_scored, x_scores, lambda h: both(kbd, ALL, h, ALL),
                           lambda h: both(q, ALL, h // 2, ALL), x_nmT),
                "y_st": st(yr, Y_MAXT, y_probs, y_scored, y_scores, lambda h: both(kbd1, ALL, h // 8, h % 8, ALL),
                           lambda h: both(q1, ALL, h // 8, ALL), y_nmT),
                "x_pv": x_pv, "y_pv": y_pv, "y_tr3": transposes(yr, Y_TR3, y_xn, y_normed, 2), "y_q": y_q,
                "y_max": y_max, "y_maxt": maxt(yr, Y_MAX, Y_MAXT, y_nm), "x_out": x_out, "y_out": y_out})

            pe.wait_ge(m_norm, 3)
            for k in range(KD):
                for t in range(TT):
                    ins = t_.transpose((x_pvo, y_pvo)[k][:, t * P:(t + 1) * P], xmn[:, t, k * P:(k + 1) * P],
                                       ident[:])
                ins.then_inc(m_tr, 1)
            pe.wait_ge(m_coef, M_COEF)
            for t in range(TT):
                ins = t_.transpose(xg[0][0:NE, t * P:(t + 1) * P], coef[:, :, t], ident[:])
            ins.then_inc(m_tr, 1)
            pe.wait_ge(m_trc, KD + 1)
            pe.wait_ge(m_in, 16 * (NTOK // S + 1))
            for t in range(TT):
                ins = t_.matmul((x_scores, y_scores)[t // 2][:, (t % 2) * D:(t % 2 + 1) * D],
                                m_cT[:, t * P:(t + 1) * P], eb_s[:], start=True, stop=True)
            ins.then_inc(m_down, 1)
            for e in range(NE):
                pe.wait_ge(m_w[e % 2], 32 * (e // 2 + 1))
                for m in range(KD):
                    n = KD * e + m
                    if n >= 2:
                        pe.wait_ge(m_upc, n - 1)
                    for u in range(2):
                        ins = products32((xg, yg)[n % 2][u][:], [(gu_s[e % 2][:, k, u, m * P:(m + 1) * P],
                                                                 xmT[:, k, :]) for k in range(KD)])
                    ins.then_inc(m_up, 1)
                pe.wait_ge(m_inter, KD * (e + 1))
                pe.wait_ge(m_acc, e + 1)
                for t in range(TT):
                    ins = products32((x_scores, y_scores)[t // 2][:, (t % 2) * D:(t % 2 + 1) * D],
                                     [(inter[:, k, t * P:(t + 1) * P], dn_s[e % 2][:, k, :]) for k in range(KD)])
                ins.then_inc(m_down, 1)

        @block.vector
        def _(dve):
            v = nc.vector
            for n in range(NSPLIT):
                dve.wait_ge(split_hi, n + 1)
                v.tensor_tensor(splits[n][2], staged(n), splits[n][1].bitcast(F32), ALU.subtract).then_inc(split_lo, 1)
            dve.wait_ge(tanh_done, 1)
            v.tensor_scalar(bo_tg[:], bo_tg[:], tg[:, 0:1], None, ALU.mult).then_inc(setup_done, 1)
            v.tensor_scalar(bo1_tg[:], bo1_tg[:], tg[:, 1:2], None, ALU.mult).then_inc(setup_done, 1)
            for part in range(2):
                v.memset(flat(kbd[part][:]).bitcast(F32), 0.0)
            v.memset(x_nmT[:].bitcast(F32), 0.0).then_inc(setup_done, 1)
            v.memset(y_nmT[:].bitcast(F32), 0.0).then_inc(setup_done, 1)

            def norm(src, st6, mv, rs, dst, stats, k_stats, rstd, k_rstd, normed, i):
                for t in range(T):
                    ins = v.bn_stats(st6[:, t, :], src[:, t, :])
                ins.then_inc(stats.sem, 1)
                dve.drain()
                for t in range(T):
                    ins = v.bn_aggr(mv[:, t, :], st6[:, t, :])
                ins.then_inc(stats.sem, 1)
                rstd.wait(dve, i, k_rstd)
                for t in range(T):
                    ins = v.tensor_scalar(dst[:, t, :], src[:, t, :], mv[:, t, 0:1], rs[:, 1, t:t + 1],
                                          ALU.subtract, ALU.mult)
                ins.then_inc(normed.sem, 1)

            def n_norm(i, _):
                x_loaded.wait(dve, i, 16)
                norm(x_in, x_st6, x_mv, x_rstd, x_xn, x_stats, 0, x_rs, 2, x_normed, i)

            def y_norm2(i, _):
                xr.empty(dve, i, X_OUT)
                norm(x1, y_st6, y_mv, y_rstd, y_xn, y_stats, 0, y_rs, 2, y_normed, i)

            def y_norm3(i, _):
                yr.empty(dve, i, Y_FFN + 6)
                yr.empty(dve, i, Y_FFN + 7)
                norm(acc, y_st6, y_mv, y_rstd, y_xn, y_stats, 2, y_rs, 4, y_normed, i)

            def lo_of(ring, done, k, i, job, cols, dst, hi):
                done.wait(dve, i, k)
                ring.has_emptied(v.tensor_tensor(dst, ring.bank(job)[:, 0:cols], hi.bitcast(F32), ALU.subtract), job)

            def x_tr(i, _):
                lo_of(xr, x_hi, 1, i, X_TR, KD * S, flat(xT[1][:]), flat(xT[0][:]))

            def x_k(i, c):
                x_hi.wait(dve, i, 2 + c)
                view = xr.bank(X_K + c)[:, 0:4 * NK].rearrange("p (m n) -> p m n", m=4)
                for half in range(2):
                    rows, heads = slice(64 * half, 64 * half + 64), slice(8 * c + half, 8 * c + 8, 2)
                    ins = v.tensor_tensor(kbd[1][rows, heads, :], view[rows], kbd[0][rows, heads, :].bitcast(F32),
                                          ALU.subtract)
                xr.has_emptied(ins, X_K + c)

            def x_q(i, c):
                lo_of(xr, x_hi, 4 + c, i, X_Q + c, 2 * S, flat(q[1][:, 2 * c:2 * c + 2, :]),
                      flat(q[0][:, 2 * c:2 * c + 2, :]))

            def y_tr(job, k):
                return lambda i, _: lo_of(yr, y_hi, k, i, job, KD * S, flat(yT[1][:]), flat(yT[0][:]))

            def biased_lo(i, k, job, cols, parts, b):
                y_hi.wait(dve, i, k)
                for m in range(KD):
                    ins = v.scalar_tensor_tensor(out=parts[1][:, m, :], in0=yr.bank(job)[:, m * cols:(m + 1) * cols],
                                                 scalar=bqkv1_s[:, b, m:m + 1], in1=parts[0][:, m, :].bitcast(F32),
                                                 op0=ALU.add, op1=ALU.subtract)
                yr.has_emptied(ins, job)

            def y_k(i, _):
                y_kmask.wait(dve, i, 0)
                biased_lo(i, 2, Y_K, NK, k1, 1)

            def y_q(i, _):
                biased_lo(i, 4, Y_Q, S, q1, 0)

            def maxima(ring, max_job, nm):
                def step(i, j):
                    t, c = j // 4, j % 4
                    ring.full(dve, i, max_job + j)
                    ring.has_emptied(v.tensor_reduce(
                        nm[:, t, 4 * c:4 * c + 4],
                        ring.bank(max_job + j)[:, 0:4 * NK].rearrange("p (h n) -> p h n", h=4), AX_X, ALU.max,
                        negate=True), max_job + j)
                return step

            def over_experts(a):
                return a.unsqueeze(2).broadcast_to([P, T, NE])

            def y_gate(i, _):
                done = y_gated
                yr.full(dve, i, Y_GATE)
                yr.has_emptied(v.tensor_tensor(
                    lg[:], yr.bank(Y_GATE)[:, 0:T * NE].rearrange("p (t e) -> p t e", t=T),
                    gate_b_s[:].unsqueeze(1).broadcast_to([P, T, NE]), ALU.add), Y_GATE)
                yr.empty(dve, i, Y_GATE)
                v.tensor_reduce(lg_n[:, 0, :], lg[:], AX_X, ALU.max, negate=True).then_inc(done.sem, 1)
                done.wait(dve, i, 1)
                v.tensor_tensor(lg[:], lg[:], over_experts(lg_n[:, 0, :]), ALU.add).then_inc(done.sem, 1)
                y_exp.wait(dve, i, 1)
                v.tensor_reduce(lg_n[:, 1, :], lg[:], AX_X, ALU.add).then_inc(done.sem, 1)
                done.wait(dve, i, 3)
                v.reciprocal(lg_n[:, 2, :], lg_n[:, 1, :]).then_inc(done.sem, 1)
                done.wait(dve, i, 4)
                v.tensor_tensor(lg[:], lg[:], over_experts(lg_n[:, 2, :]), ALU.mult).then_inc(done.sem, 1)
                done.wait(dve, i, 5)
                v.scalar_tensor_tensor(out=flat(lg[:]), in0=flat(lg[:]), scalar=THRESHOLD, in1=flat(lg[:]),
                                       op0=ALU.is_ge, op1=ALU.mult).then_inc(done.sem, 1)
                done.wait(dve, i, 6)
                v.tensor_reduce(lg_n[:, 1, :], lg[:], AX_X, ALU.add).then_inc(done.sem, 1)
                done.wait(dve, i, 7)
                v.scalar_tensor_tensor(out=lg_n[:, 3, :], in0=lg_n[:, 1, :], scalar=0.0, in1=lg_n[:, 1, :],
                                       op0=ALU.is_equal, op1=ALU.add).then_inc(done.sem, 1)
                done.wait(dve, i, 8)
                v.reciprocal(lg_n[:, 2, :], lg_n[:, 3, :]).then_inc(done.sem, 1)
                done.wait(dve, i, 9)
                v.scalar_tensor_tensor(out=lg[:], in0=lg[:], scalar=tg[:, 2:3], in1=over_experts(lg_n[:, 2, :]),
                                       op0=ALU.mult, op1=ALU.mult).then_inc(done.sem, 1)

            def y_eb(i, _):
                yr.full(dve, i, Y_EB)
                yr.has_emptied(v.tensor_tensor(flat(acc[:]), yr.bank(Y_EB)[:], flat(x1[:]), ALU.add), Y_EB)

            def y_ffn(i, j):
                t, n = j % T, j // T
                y_gated.wait(dve, i, 10)
                yr.empty(dve, i, Y_EB)
                yr.full(dve, i, Y_FFN + j)
                for o in range(2):
                    ins = v.scalar_tensor_tensor(out=acc[:, t, :], in0=yr.bank(Y_FFN + j)[:, o * D:(o + 1) * D],
                                                 scalar=lg[:, t, 2 * n + o:2 * n + o + 1], in1=acc[:, t, :],
                                                 op0=ALU.mult, op1=ALU.add)
                    if o == 0:
                        ins.then_inc(y_acc.sem, 1)
                        y_acc.wait(dve, i, j + 1)
                yr.has_emptied(ins, Y_FFN + j)

            def normalise(pvo, an, sums_done, recip, attn, i, k):
                sums_done.wait(dve, i, k)
                v.reciprocal(an, an).then_inc(recip.sem, 1)
                recip.wait(dve, i, k)
                v.tensor_tensor(an[0:64, :], pvo[0:64, 0:S], an[0:64, :], ALU.mult)
                v.tensor_tensor(an[64:128, :], pvo[64:128, S:2 * S], an[64:128, :], ALU.mult).then_inc(attn.sem, 1)

            def x_pv(i, p):
                normalise(x_pvo, x_an[:, p % 2, :], x_sums, x_recip, x_attn, i, p + 1)

            def y_pv(i, p):
                if p % 4 == 3:
                    normalise(y_pvo, y_an[:], y_sums, y_recip, y_attn, i, p // 4 + 1)

            def y_attn_split(i, m):
                y_attn_hi.wait(dve, i, m + 1)
                v.scalar_tensor_tensor(out=q1[1][:, m, :], in0=y_an[:], scalar=bqkv1_s[:, 2, m:m + 1],
                                       in1=q1[0][:, m, :].bitcast(F32), op0=ALU.add,
                                       op1=ALU.subtract).then_inc(y_attn_lo.sem, 1)

            def x_out(i, c):
                if c == 3:
                    x_resd.wait(dve, i, 1)
                    xr.full(dve, i, X_OUT)
                    xr.has_emptied(v.scalar_tensor_tensor(out=flat(x1[:]), in0=xr.bank(X_OUT)[:], scalar=tg[:, 0:1],
                                                          in1=flat(x_res[:]), op0=ALU.mult, op1=ALU.add), X_OUT)

            def y_out(i, t):
                y_resd.wait(dve, i, 1)
                y_stored.wait(dve, i, 0)
                yr.full(dve, i, Y_OUT + t)
                yr.has_emptied(v.scalar_tensor_tensor(out=y_x3[:, t, :], in0=yr.bank(Y_OUT + t)[:, 0:D],
                                                      scalar=tg[:, 1:2], in1=acc[:, t, :], op0=ALU.mult,
                                                      op1=ALU.add), Y_OUT + t)

            n_norm(0, 0)
            run(dve, {"n_norm": n_norm, "y_norm2": y_norm2, "y_norm3": y_norm3, "x_tr": x_tr, "x_k": x_k, "x_q": x_q,
                      "y_tr2": y_tr(Y_TR2, 1), "y_tr3": y_tr(Y_TR3, 3), "y_k": y_k, "y_q": y_q,
                      "x_max": maxima(xr, X_MAX, x_nm), "y_max": maxima(yr, Y_MAX, y_nm), "y_gate": y_gate,
                      "y_eb": y_eb, "y_ffn": y_ffn, "x_pv": x_pv, "y_pv": y_pv, "y_hi": y_attn_split,
                      "x_out": x_out, "y_out": y_out})

            dve.wait_ge(m_in, 16 * (NTOK // S + 1))
            for t in range(TT):
                ins = v.bn_stats(m_st6[:, t, :], xm[:, t, :])
            ins.then_inc(m_norm, 1)
            dve.wait_ge(m_norm, 1)
            for t in range(TT):
                ins = v.bn_aggr(m_mv[:, t, :], m_st6[:, t, :])
            ins.then_inc(m_norm, 1)
            v.tensor_copy(idx_f[:], idx_s[:]).then_inc(m_coef, 1)
            dve.wait_ge(m_coef, 1)
            n = 1
            for t in range(TT):
                v.tensor_scalar(coef_k[:], expert_no[:], idx_f[:, t, 0:1], None, ALU.is_equal).then_inc(m_coef, 1)
                dve.wait_ge(m_coef, n + 1)
                v.scalar_tensor_tensor(out=coef_k[:], in0=expert_no[:], scalar=idx_f[:, t, 1:2], in1=coef_k[:],
                                       op0=ALU.is_equal, op1=ALU.add).then_inc(m_coef, 1)
                dve.wait_ge(m_coef, n + 2)
                v.scalar_tensor_tensor(out=coef[:, :, t], in0=rw_s[:, t, :], scalar=tg[:, 3:4], in1=coef_k[:],
                                       op0=ALU.mult, op1=ALU.mult).then_inc(m_coef, 1)
                n += 3
                dve.wait_ge(m_coef, n)
            dve.wait_ge(m_rs, 2)
            for t in range(TT):
                ins = v.tensor_scalar(xmn[:, t, :], xm[:, t, :], m_mv[:, t, 0:1], m_rstd[:, 1, t:t + 1],
                                      ALU.subtract, ALU.mult)
            ins.then_inc(m_norm, 1)

            def add_down(t, scalar):
                dst, src = xm[:, t, :], (x_scores, y_scores)[t // 2][:, (t % 2) * D:(t % 2 + 1) * D]
                if scalar is None:
                    return v.tensor_tensor(dst, src, dst, ALU.add)
                return v.scalar_tensor_tensor(out=dst, in0=src, scalar=scalar, in1=dst, op0=ALU.mult, op1=ALU.add)

            dve.wait_ge(m_norm, 3)
            dve.wait_ge(m_down, 1)
            for t in range(TT):
                ins = add_down(t, None)
            ins.then_inc(m_acc, 1)
            for e in range(NE):
                for m in range(KD):
                    n = KD * e + m
                    banks = (xg, yg)[n % 2]
                    dve.wait_ge(m_up, n + 1)
                    v.tensor_scalar(m_g, banks[0][:], gu_b_s[:, e, m, 0:1], LIMIT, ALU.add,
                                    ALU.min).then_inc(m_gate, 1)
                    v.tensor_scalar(m_u, banks[1][:], gu_b_s[:, e, m, 1:2], LIMIT, ALU.add,
                                    ALU.min).then_inc(m_upc, 1)
                    dve.wait_ge(m_upc, n + 1)
                    v.tensor_scalar(m_u, m_u, -LIMIT, 1.0, ALU.max, ALU.add)
                    dve.wait_ge(m_sig, n + 1)
                    v.tensor_tensor(m_g, m_g, m_s, ALU.mult).then_inc(m_glu, 1)
                    dve.wait_ge(m_glu, n + 1)
                    v.tensor_tensor(inter[:, m, :], m_g, m_u, ALU.mult).then_inc(m_inter, 1)
                    dve.wait_ge(m_inter, n + 1)
                dve.wait_ge(m_down, e + 2)
                for t in range(TT):
                    ins = add_down(t, coef[:, e, t:t + 1])
                ins.then_inc(m_acc, 1)
                dve.wait_ge(m_acc, e + 2)


def kernel(**inputs):
    import numpy as _np
    import concourse.bacc as _bacc
    from concourse import mybir as _mybir
    from concourse.bass_utils import run_bass_kernel_spmd as _run

    a = {k: _np.asarray(v) for k, v in inputs.items()}
    kd, ne = D // P, NE

    def rows(w):
        return _np.ascontiguousarray(w.reshape(-1, P, w.shape[-1]).transpose(1, 0, 2))

    def columns(b):
        return b.reshape(-1, P).T

    w1 = _np.concatenate([rows(a[n]).reshape(P, -1) for n in ("L1_xattn_wq", "L1_xattn_wo", "L0_ffn_gate_w")], 1)
    gu = a["L1_ffn_gate_up_proj"].reshape(ne, kd, P, D, 2).transpose(0, 2, 1, 4, 3)
    arrays = {
        "x": a["x"], "ctx": a["ctx_1024"],
        "gates": _np.concatenate([a["g_xattn"], a["g_ffn"]]),
        "wq": rows(a["L0_xattn_Wq"].T), "wk": rows(a["L0_xattn_Wk"].T), "wv": rows(a["L0_xattn_Wv"].T),
        "wo": rows(a["L0_xattn_Wo"].T), "bo": a["L0_xattn_bo"],
        "gate_b": a["L0_ffn_gate_b"],
        "ew": a["L0_ffn_expert_w"].reshape(ne, kd, P, D).transpose(2, 1, 0, 3).reshape(P, kd, ne * D),
        "eb": a["L0_ffn_expert_b"], "w1": w1,
        "w1k": rows(a["L1_xattn_wk"]), "w1v": rows(a["L1_xattn_wv"]),
        "bqkv1": _np.stack([columns(a[n]) for n in ("L1_xattn_bq", "L1_xattn_bk", "L1_xattn_bv")], 1),
        "bo1": a["L1_xattn_bo"],
        "router_idx": a["L1_ffn_router_indices"].reshape(TT, P, 2).transpose(1, 0, 2),
        "router_w": a["L1_ffn_routing_weights"].reshape(TT, P, ne).transpose(1, 0, 2),
        "gu": gu, "gu_b": a["L1_ffn_gate_up_proj_bias"].reshape(ne, kd, P, 2).transpose(2, 0, 1, 3),
        "dn": a["L1_ffn_down_proj"].reshape(ne, kd, P, D).transpose(0, 2, 1, 3), "dn_b": a["L1_ffn_down_proj_bias"],
    }
    order = ["x", "ctx", "gates", "wq", "wk", "wv", "wo", "bo", "gate_b", "ew", "eb", "w1", "w1k", "w1v", "bqkv1",
             "bo1", "router_idx", "router_w", "gu", "gu_b", "dn", "dn_b"]
    nc = _bacc.Bacc("TRN2", target_bir_lowering=False, num_devices=1)
    maps, args = {}, []
    for name in order:
        v = _np.ascontiguousarray(arrays[name])
        maps[f"in_{name}"] = v
        args.append(nc.dram_tensor(f"in_{name}", v.shape, _mybir.dt.from_np(v.dtype), kind="ExternalInput").ap())
    args.append(nc.dram_tensor("out_0", (B, S, D), F32, kind="ExternalOutput").ap())
    flamingo_stack(nc, *args)
    r = _run(nc, [maps], core_ids=[0])
    return r.results[0]["out_0"]
```

```python
from contextlib import ExitStack

import concourse.bass as bass
from concourse import mybir

F32 = mybir.dt.float32
F32R = mybir.dt.float32r
I32 = mybir.dt.int32
ALU = mybir.AluOpType
ACT = mybir.ActivationFunctionType
AX_X = mybir.AxisListType.X

P = 128
B, S, D = 64, 256, 256
NK = 120
T = S // P
KD = D // P
H = 16
DH0, DH1 = 64, 16
INNER = H * DH0
NPAIR = H // 2
HPT1 = P // DH1
NE = 8
NTOK = 512
TT = NTOK // P
EPS = 1e-5
THRESHOLD = 0.1
SWIGLU_ALPHA, LIMIT = 1.702, 7.0
SCALE0, SCALE1 = DH0 ** -0.5, DH1 ** -0.5

X_CTX, X_K, X_TR, X_V, X_Q = 0, (1, 4), 2, (3, 5), 6
X_MAX, X_MAXT = (10, 11, 12, 13, 14, 15, 17, 18), (16, 19)
X_JOBS = 20
Y_TR2, Y_GATE, Y_WT, Y_EB = 0, 1, 2, 3
Y_CTX, Y_K, Y_V = 4, 6, 8
Y_FFN = (5, 7, 9, 10, 11, 12, 13, 14)
Y_TR3, Y_Q, Y_MAX, Y_MAXT = 15, 16, tuple(range(17, 25)), 25
Y_JOBS = 26


def steps(x, y, n, p, z):
    batch = {"x": x, "y": y, "n": n, "p": p, "z": z}
    out = []

    def do(name, k=0):
        if batch[name[0]] is not None:
            out.append((name, k, batch[name[0]]))

    for s in range(NPAIR):
        do("y_ffn", s)
        do("x_st", s)
        if s == 0:
            do("n_load")
            do("y_k")
            do("z_hi", 1)
        if s == 1:
            do("y_v")
            do("z_out")
        if s >= 1:
            do("x_pv", s - 1)
        if s >= 2:
            do("x_hi", s - 2)
        if s == 2:
            do("p_load")
        if s == 4:
            do("n_ctx")
            do("n_stat")
        if s == 5:
            do("n_k", 0)
            do("n_norm")
        if s == 6:
            do("n_tr")
            do("n_v", 0)
    do("y_stat3")
    do("n_k", 1)
    do("x_pv", NPAIR - 1)
    do("y_norm3")
    do("x_hi", NPAIR - 2)
    do("n_v", 1)
    do("y_tr3")
    do("x_hi", NPAIR - 1)
    do("x_out", 0)
    do("y_q")
    do("x_out", 1)
    do("y_max", 0)
    do("y_max", 1)
    do("x_out", 2)
    do("y_max", 2)
    do("y_max", 3)
    do("x_out", 3)
    do("y_max", 4)
    do("y_max", 5)
    do("n_q", 0)
    do("y_max", 6)
    do("y_max", 7)
    do("n_q", 1)
    do("y_maxt")
    do("n_q", 2)
    do("x_made")
    for s in range(NPAIR):
        do("y_st", s)
        if s == 0:
            do("n_q", 3)
            do("n_res")
            do("p_stat")
        if s >= 1:
            do("y_pv", s - 1)
        if s == 4:
            do("n_maxt", 0)
        if 1 <= s <= 4:
            do("n_max", 2 * (s - 1))
            do("n_max", 2 * (s - 1) + 1)
        if s == 1:
            do("p_norm")
        if s == 2:
            do("p_tr2")
        if s == 3:
            do("p_gate")
        if s == 5:
            do("p_wt")
            do("y_hi", 0)
        if s == 6:
            do("n_maxt", 1)
            do("p_eb")
        if s == 7:
            do("p_ctx")
    do("y_pv", NPAIR - 1)
    return out


class Signal:

    def __init__(self, sem, per):
        self.sem, self.per = sem, per

    def wait(self, eng, i, k):
        value = i * self.per + k
        if isinstance(value, int) and value <= 0:
            return
        eng.wait_ge(self.sem, value)


class Ring:

    def __init__(self, banks, filled, emptied):
        self.banks, self.filled, self.emptied, self.n = banks, filled, emptied, len(banks)

    def bank(self, job):
        return self.banks[job % self.n]

    def to_fill(self, eng, i, job):
        self.emptied[job % self.n].wait(eng, i, job // self.n)

    def full(self, eng, i, job):
        self.filled[job % self.n].wait(eng, i, job // self.n + 1)

    def empty(self, eng, i, job):
        self.emptied[job % self.n].wait(eng, i, job // self.n + 1)

    def has_filled(self, ins, job):
        ins.then_inc(self.filled[job % self.n].sem, 1)

    def has_emptied(self, ins, job):
        ins.then_inc(self.emptied[job % self.n].sem, 1)


def flamingo_stack(nc, x, ctx, gates, wq, wk, wv, wo, bo, gate_b, ew, eb, w1, w1k, w1v, bqkv1, bo1,
                   router_idx, router_w, gu, gu_b, dn, dn_b, out):
    es = ExitStack()
    with es:
        def sb(name, shape, dt=F32):
            return es.enter_context(nc.sbuf_tensor(name, shape, dt))

        def pb(name):
            return es.enter_context(nc.psum_tensor(name, [P, 512], F32))

        def sem(name):
            return es.enter_context(nc.semaphore(name))

        def signal(name, per=1):
            return Signal(sem(name), per)

        def pair(name, shape):
            return sb(name + "_hi", shape, F32R), sb(name + "_lo", shape, F32R)

        wq_s = pair("wq", [P, KD, INNER])
        wo_s = pair("wo", [P, INNER // P, D])
        ew_s = pair("ew", [P, KD, NE * D])
        w1_s = pair("w1", [P, 2 * KD * D + KD * NE])
        wk_s, wv_s = sb("wk_s", [P, KD, INNER]), sb("wv_s", [P, KD, INNER])
        w1k_s, w1v_s = sb("w1k_s", [P, KD, D]), sb("w1v_s", [P, KD, D])
        eb_s = sb("eb_s", [P, D])
        stage = (wk_s, wv_s)

        def w1q_s(n):
            return w1_s[n][:, 0:KD * D].rearrange("p (k n) -> p k n", k=KD)

        def w1o_s(n):
            return w1_s[n][:, KD * D:2 * KD * D].rearrange("p (k n) -> p k n", k=KD)

        def gate_s(n):
            return w1_s[n][:, 2 * KD * D:].rearrange("p (k n) -> p k n", k=KD)

        ident = sb("ident", [P, P])
        ident_r = sb("ident_r", [P, H], F32R)
        own_head = sb("own_head", [P, HPT1])
        tg = sb("tg", [P, 4])
        bo_tg, bo1_tg = sb("bo_tg", [P, D]), sb("bo1_tg", [P, D])
        gate_b_s = sb("gate_b_s", [P, NE])
        bqkv1_s = sb("bqkv1_s", [P, 3, KD])
        neg_half, eps = sb("neg_half", [P, TT]), sb("eps", [P, T])
        x_in, x_xn = sb("x_in", [P, T, D]), sb("x_xn", [P, T, D])
        x_res = sb("x_res", [P, T, D])
        x_st6, x_mv, x_rstd = sb("x_st6", [P, T, 6]), sb("x_mv", [P, T, 2]), sb("x_rstd", [P, 2, T])
        xT = pair("xT", [P, KD, S])
        ctx_in, ctxT = sb("ctx_in", [NK, D]), sb("ctxT", [P, KD, NK])
        q = pair("q", [P, NPAIR, S])
        kbd = pair("kbd", [P, H, NK])
        vx = sb("vx", [P, H, P])
        x_nm, x_nmT = sb("x_nm", [P, T, H]), sb("x_nmT", [P, S], F32R)
        prob = sb("prob", [NK, 2, 2, S])
        an, sums = sb("an", [P, 3, S]), sb("sums", [P, 2, S])
        x1 = sb("x1", [P, T, D])
        y_xn = sb("y_xn", [P, T, D])
        y_st6, y_mv, y_rstd = sb("y_st6", [P, T, 6]), sb("y_mv", [P, T, 2]), sb("y_rstd", [P, 2, T])
        yT = pair("yT", [P, KD, S])
        acc = sb("acc", [P, T, D])
        ctx_in1, ctxT1 = sb("ctx_in1", [NK, D]), sb("ctxT1", [P, KD, NK])
        lg, lg_n = sb("lg", [P, T, NE]), sb("lg_n", [P, 4, T])
        wT = sb("wT", [P, S])
        q1 = pair("q1", [P, KD, S])
        k1 = pair("k1", [P, KD, NK])
        kbd1 = pair("kbd1", [P, KD, HPT1, NK])
        VX1 = H * P + 4 * DH1 + P
        vx1 = sb("vx1", [P, VX1])
        y_nm, y_nmT = sb("y_nm", [P, T, H]), sb("y_nmT", [P, S], F32R)
        y_x3 = sb("y_x3", [P, T, D])

        def v1_block(g, ones):
            at = g * 4 * P + 64 * ((g + ones) % 2)
            return vx1[:, at:at + 4 * (P + DH1)].rearrange("p (j c) -> p j c", j=4)[:, :, 0:DH1]

        xg, yg = [pb("xg0"), pb("xg1")], [pb("yg0"), pb("yg1")]
        scores, pv = [pb("scores0"), pb("scores1")], [pb("pv0"), pb("pv1")]

        stage_in = [sem("stage_in0"), sem("stage_in1")]
        small_in = sem("small_in")
        last_in = sem("last_in")
        split_hi, split_lo = sem("split_hi"), sem("split_lo")
        tanh_done, const_done, setup_done = sem("tanh_done"), sem("const_done"), sem("setup_done")

        xr = Ring(xg, [signal(f"x_filled{n}", X_JOBS // 2) for n in range(2)],
                  [signal(f"x_emptied{n}", X_JOBS // 2) for n in range(2)])
        yr = Ring(yg, [signal(f"y_filled{n}", Y_JOBS // 2) for n in range(2)],
                  [signal(f"y_emptied{n}", Y_JOBS // 2) for n in range(2)])
        x_loaded, ctx_loaded, ctx1_loaded = (signal("x_loaded", 16), signal("ctx_loaded", 16),
                                             signal("ctx1_loaded", 16))
        x_stats, x_rs, x_resd, x_normed = (signal("x_stats", 2), signal("x_rs", 2), signal("x_resd"),
                                           signal("x_normed"))
        x_hi = signal("x_hi", 7)
        x_scored, x_probs, x_mixed = (signal("x_scored", NPAIR), signal("x_probs", NPAIR),
                                      signal("x_mixed", NPAIR))
        x_logged, y_logged = signal("x_logged", NPAIR), signal("y_logged", 2)
        x_copied, x_recip, x_attn = (signal("x_copied", NPAIR), signal("x_recip", NPAIR),
                                     signal("x_attn", NPAIR))
        x_out_in, x_made = signal("x_out_in"), signal("x_made")
        y_out_in, y_made = signal("y_out_in"), signal("y_made")
        x_attn_hi, x_attn_lo = signal("x_attn_hi", NPAIR), signal("x_attn_lo", NPAIR)
        y_stats, y_rs, y_resd, y_normed = (signal("y_stats", 4), signal("y_rs", 4), signal("y_resd"),
                                           signal("y_normed", 2))
        y_hi, y_kmask = signal("y_hi", 4), signal("y_kmask", 1)
        y_gated, y_exp = signal("y_gated", 10), signal("y_exp")
        y_acc = signal("y_acc", NE)
        y_scored, y_probs, y_mixed = (signal("y_scored", NPAIR), signal("y_probs", NPAIR),
                                      signal("y_mixed", NPAIR))
        y_copied, y_recip, y_attn = signal("y_copied", 2), signal("y_recip", 2), signal("y_attn", 2)
        y_attn_hi, y_attn_lo = signal("y_attn_hi", 2), signal("y_attn_lo", 2)
        y_stored = signal("y_stored", 16)
        m_in, m_w = sem("m_in"), [sem("m_w0"), sem("m_w1")]
        (m_norm, m_rs, m_coef, m_tr, m_trc, m_up, m_gate, m_upc, m_sig, m_inter, m_down, m_acc, m_stored, m_glu) = (
            sem(n) for n in ("m_norm", "m_rs", "m_coef", "m_tr", "m_trc", "m_up", "m_gate", "m_upc", "m_sig",
                             "m_inter", "m_down", "m_acc", "m_stored", "m_glu"))

        x_rows = x.rearrange("b (t p) d -> b p t d", p=P)
        out_rows = out.rearrange("b (t p) d -> b p t d", p=P)

        def flat(a):
            return a.rearrange("p k n -> p (k n)")

        wv_f, vx_f, wk_f = flat(wv_s[:]), flat(vx[:]), flat(wk_s[:])
        xm = wv_f[:, 0:TT * D].rearrange("p (t d) -> p t d", t=TT)
        xmn = wv_f[:, TT * D:2 * TT * D].rearrange("p (t d) -> p t d", t=TT)
        xmT = vx_f[:, 0:KD * NTOK].rearrange("p (k n) -> p k n", k=KD)
        inter = vx_f[:, KD * NTOK:2 * KD * NTOK].rearrange("p (k n) -> p k n", k=KD)
        gu_s = [wk_f[:, r * 4 * D:(r + 1) * 4 * D].rearrange("p (k g n) -> p k g n", k=KD, g=2) for r in range(2)]
        dn_s = [w1k_s, w1v_s]
        m_g, m_u, m_s = flat(x_in[:]), flat(x_xn[:]), flat(x_res[:])
        m_cT = flat(acc[:])
        M_COEF = 1 + 3 * TT
        coef, coef_k = sb("coef", [P, NE, TT]), sb("coef_k", [P, NE])
        rw_s, idx_s, idx_f = sb("rw_s", [P, TT, NE]), sb("idx_s", [P, TT, 2], I32), sb("idx_f", [P, TT, 2])
        gu_b_s, expert_no = sb("gu_b_s", [P, NE, KD, 2]), sb("expert_no", [P, NE])
        m_st6, m_mv, m_rstd = sb("m_st6", [P, TT, 6]), sb("m_mv", [P, TT, 2]), sb("m_rstd", [P, 2, TT])

        block = es.enter_context(nc.Block())

        def run(eng, table):
            def one(*batches):
                for name, k, i in steps(*batches):
                    if name in table:
                        table[name](i, k)

            one(None, None, 0, None, None)
            one(0, None, 1, 0, None)
            one(1, 0, 2, 1, None)
            with eng.Fori(2, B - 1) as i:
                one(i, i - 1, i + 1, i, i - 2)
            one(B - 1, B - 2, None, B - 1, B - 3)
            one(None, B - 1, None, None, B - 2)
            one(None, None, None, None, B - 1)

        splits = [(flat(wq), flat(wq_s[0][:]), flat(wq_s[1][:])), (flat(wo), flat(wo_s[0][:]), flat(wo_s[1][:]))]
        splits += [(ew[:, k, :], ew_s[0][:, k, :], ew_s[1][:, k, :]) for k in range(KD)]
        splits += [(w1, w1_s[0][:], w1_s[1][:])]
        NSPLIT = len(splits)

        def staged(n):
            return flat(stage[n % 2][:])[:, 0:splits[n][0].shape[1]]

        SMALL = 16 * 9
        ZEROED, CONST = 9, 14
        SET_UP = 5

        @block.sync
        def _(sp):
            for n in range(NSPLIT):
                if n >= 2:
                    sp.wait_ge(split_lo, n - 1)
                sp.dma_start(staged(n), splits[n][0]).then_inc(stage_in[n % 2], 16)
                if n == 0:
                    for dst, src in ((tg, gates), (bo_tg, bo), (bo1_tg, bo1), (gate_b_s, gate_b)):
                        sp.dma_start(dst[:], src.partition_broadcast(P)).then_inc(small_in, 16)
                    for dst, src in ((bqkv1_s, bqkv1), (rw_s, router_w), (idx_s, router_idx), (gu_b_s, gu_b)):
                        sp.dma_start(dst[:], src).then_inc(small_in, 16)
                    sp.wait_ge(const_done, ZEROED)
                    sp.dma_start(eb_s[0:NE, :], eb).then_inc(small_in, 16)
            sp.dma_start(w1k_s[:], w1k).then_inc(last_in, 16)
            sp.dma_start(w1v_s[:], w1v).then_inc(last_in, 16)
            sp.wait_ge(split_lo, NSPLIT)
            sp.dma_start(wk_s[:], wk).then_inc(last_in, 16)
            sp.dma_start(wv_s[:], wv).then_inc(last_in, 16)

            def y_out(i, _):
                y_made.wait(sp, i, 1)
                sp.dma_start(out_rows[i], y_x3[:]).then_inc(y_stored.sem, 16)

            run(sp, {"z_out": y_out})
            sp.wait_ge(y_stored.sem, 16 * B)
            for b in range(NTOK // S):
                sp.dma_start(xm[:, b * T:(b + 1) * T, :], out_rows[b]).then_inc(m_in, 16)
            sp.dma_start(eb_s[0:NE, :], dn_b).then_inc(m_in, 16)
            for e in range(NE):
                if e >= 2:
                    sp.wait_ge(m_down, e)
                sp.dma_start(gu_s[e % 2], gu[e]).then_inc(m_w[e % 2], 16)
                sp.dma_start(dn_s[e % 2][:], dn[e]).then_inc(m_w[e % 2], 16)
            sp.wait_ge(m_acc, 1 + NE)
            for b in range(NTOK // S):
                sp.dma_start(out_rows[b], xm[:, b * T:(b + 1) * T, :]).then_inc(m_stored, 16)
            sp.wait_ge(m_stored, 16 * (NTOK // S))

        @block.gpsimd
        def _(pool):
            g = nc.gpsimd
            for tile, value in ((ident, 0.0), (own_head, 1.0), (neg_half, -0.5), (eps, EPS), (eb_s, 0.0), (vx, 1.0), (vx1, 0.0),
                                (wT, 0.0)):
                g.memset(tile[:], value).then_inc(const_done, 1)
            g.iota(expert_no[:], pattern=[[1, NE]], base=0, channel_multiplier=0,
                   allow_small_or_imprecise_dtypes=True).then_inc(const_done, 1)
            pool.wait_ge(const_done, ZEROED)
            g.affine_select(out=ident[:], in_=ident[:], compare_op=ALU.not_equal, fill=1.0, base=0,
                            pattern=[[-1, P]], channel_multiplier=1).then_inc(const_done, 1)
            g.affine_select(out=own_head[:], in_=own_head[:], compare_op=ALU.is_ge, fill=0.0, base=0,
                            pattern=[[-DH1, HPT1]], channel_multiplier=1).then_inc(const_done, 1)
            pool.wait_ge(const_done, ZEROED + 2)
            g.affine_select(out=own_head[:], in_=own_head[:], compare_op=ALU.is_ge, fill=0.0, base=DH1 - 1,
                            pattern=[[DH1, HPT1]], channel_multiplier=-1).then_inc(const_done, 1)
            for half in range(2):
                for gr in range(half, 4, 2):
                    last = g.memset(v1_block(gr, 1), 1.0)
                last.then_inc(const_done, 1)

            def rstd(mv, rs, stats, k_stats, done, k, i):
                stats.wait(pool, i, k_stats)
                g.tensor_tensor(rs[:, 0, :], mv[:, :, 1], eps[:], ALU.add).then_inc(done.sem, 1)
                done.wait(pool, i, k + 1)
                g.tensor_tensor(rs[:, 1, :], rs[:, 0, :], neg_half[:, 0:T], ALU.pow).then_inc(done.sem, 1)

            def n_norm(i, _):
                rstd(x_mv, x_rstd, x_stats, 2, x_rs, 0, i)

            def n_res(i, _):
                x_loaded.wait(pool, i, 16)
                x_made.wait(pool, i, 0)
                g.tensor_tensor(x_res[:], x_in[:], bo_tg[:].unsqueeze(1).broadcast_to([P, T, D]),
                                ALU.add).then_inc(x_resd.sem, 1)

            def y_norm2(i, _):
                rstd(y_mv, y_rstd, y_stats, 2, y_rs, 0, i)

            def y_stat3(i, _):
                rstd(y_mv, y_rstd, y_stats, 4, y_rs, 2, i)

            def y_res(i, _):
                y_stored.wait(pool, i, 0)
                g.tensor_tensor(y_x3[:], acc[:], bo1_tg[:].unsqueeze(1).broadcast_to([P, T, D]),
                                ALU.add).then_inc(y_resd.sem, 1)

            def y_k(i, _):
                yr.empty(pool, i, Y_K)
                for part in range(2):
                    for m in range(KD):
                        last = g.tensor_tensor(
                            kbd1[part][:, m, :, :],
                            k1[part][:, m, :].bitcast(F32).unsqueeze(1).broadcast_to([P, HPT1, NK]),
                            own_head[:].unsqueeze(2).broadcast_to([P, HPT1, NK]), ALU.mult)
                last.then_inc(y_kmask.sem, 1)

            def x_pv(i, p):
                x_recip.wait(pool, i, p + 1)
                g.tensor_tensor(an[:, p % 3, :], an[:, p % 3, :], sums[:, p % 2, :], ALU.mult).then_inc(
                    x_attn.sem, 1)

            def y_pv(i, p):
                if p % 4 == 3:
                    y_recip.wait(pool, i, p // 4 + 1)
                    g.tensor_tensor(an[:, p // 4, :], an[:, p // 4, :], sums[:, p // 4, :], ALU.mult).then_inc(
                        y_attn.sem, 1)

            def x_lo(i, p):
                x_attn_hi.wait(pool, i, p + 1)
                g.tensor_tensor(q[1][:, p, :], an[:, p % 3, :], q[0][:, p, :].bitcast(F32),
                                ALU.subtract).then_inc(x_attn_lo.sem, 1)

            pool.wait_ge(setup_done, SET_UP)
            run(pool, {"n_stat": n_norm, "n_res": n_res, "p_stat": y_norm2, "y_stat3": y_stat3, "y_norm3": y_res, "y_k": y_k,
                       "x_pv": x_pv, "y_pv": y_pv, "x_hi": x_lo})
            pool.wait_ge(m_norm, 2)
            g.tensor_scalar(m_rstd[:, 0, :], m_mv[:, :, 1], EPS, None, ALU.add).then_inc(m_rs, 1)
            pool.wait_ge(m_rs, 1)
            g.tensor_tensor(m_rstd[:, 1, :], m_rstd[:, 0, :], neg_half[:], ALU.pow).then_inc(m_rs, 1)
            g.memset(m_cT, 0.0).then_inc(m_rs, 1)

        @block.scalar
        def _(act):
            a = nc.scalar
            for n in range(NSPLIT):
                act.wait_ge(stage_in[n % 2], 16 * (n // 2 + 1))
                a.copy(splits[n][1], staged(n)).then_inc(split_hi, 1)
            act.wait_ge(small_in, SMALL)
            a.activation(tg[:], tg[:], ACT.Tanh).then_inc(tanh_done, 1)
            a.preload_act_table_set('natural_log_exp_and_others')
            act.wait_ge(const_done, CONST)
            a.copy(ident_r[:], ident[:, 0:H]).then_inc(setup_done, 1)

            def hi_of(ring, done, i, job, cols, dst):
                ring.full(act, i, job)
                a.copy(dst, ring.bank(job)[:, 0:cols]).then_inc(done.sem, 1)

            def x_tr(i, _):
                hi_of(xr, x_hi, i, X_TR, KD * S, flat(xT[0][:]))

            def x_ctx(i, _):
                xr.full(act, i, X_CTX)
                xr.has_emptied(a.copy(flat(ctxT[:]), xr.bank(X_CTX)[:, 0:KD * NK]), X_CTX)

            def y_ctx(i, _):
                yr.full(act, i, Y_CTX)
                yr.has_emptied(a.copy(flat(ctxT1[:]), yr.bank(Y_CTX)[:, 0:KD * NK]), Y_CTX)

            def n_load(i, _):
                x_resd.wait(act, i, 0)
                act.dma_start(x_in[:], x_rows[i]).then_inc(x_loaded.sem, 16)
                act.dma_start(ctx_in[:], ctx[i]).then_inc(ctx_loaded.sem, 16)

            def p_load(i, _):
                act.dma_start(ctx_in1[:], ctx[i]).then_inc(ctx1_loaded.sem, 16)

            def x_k(i, c):
                xr.full(act, i, X_K[c])
                view = xr.bank(X_K[c])[:, 0:4 * NK].rearrange("p (m n) -> p m n", m=4)
                for half in range(2):
                    rows = slice(64 * half, 64 * half + 64)
                    last = a.copy(kbd[0][rows, 8 * c + half:8 * c + 8:2, :], view[rows])
                last.then_inc(x_hi.sem, 1)

            def x_v(i, c):
                xr.full(act, i, X_V[c])
                view = xr.bank(X_V[c])[0:NK, :].rearrange("p (m o d) -> p m o d", o=2, d=DH0)
                for odd in range(2):
                    last = a.copy(vx[0:NK, 8 * c + odd:8 * c + 8:2, 64 * odd:64 * odd + 64], view[:, :, odd, :])
                xr.has_emptied(last, X_V[c])

            def x_q(i, c):
                hi_of(xr, x_hi, i, X_Q + c, 2 * S, flat(q[0][:, 2 * c:2 * c + 2, :]))

            def y_tr(job):
                return lambda i, _: hi_of(yr, y_hi, i, job, KD * S, flat(yT[0][:]))

            def biased_hi(i, job, cols, dst, b):
                yr.full(act, i, job)
                for m in range(KD):
                    last = a.activation(dst[:, m, :], yr.bank(job)[:, m * cols:(m + 1) * cols], ACT.Identity,
                                        bias=bqkv1_s[:, b, m:m + 1])
                last.then_inc(y_hi.sem, 1)

            def y_k(i, _):
                y_kmask.wait(act, i, 0)
                biased_hi(i, Y_K, NK, k1[0], 1)

            def y_q(i, _):
                biased_hi(i, Y_Q, S, q1[0], 0)

            def y_v(i, _):
                yr.full(act, i, Y_V)
                for gr in range(4):
                    last = a.copy(v1_block(gr, 0)[0:NK], yr.bank(Y_V)[0:NK, gr * 64:(gr + 1) * 64]
                                  .rearrange("p (j d) -> p j d", j=4))
                yr.has_emptied(last, Y_V)

            def y_gate(i, _):
                y_gated.wait(act, i, 2)
                a.activation(flat(lg[:]), flat(lg[:]), ACT.Exp).then_inc(y_exp.sem, 1)

            def y_wt(i, _):
                yr.full(act, i, Y_WT)
                yr.has_emptied(a.copy(wT[0:NE, :], yr.bank(Y_WT)[0:NE, 0:S]), Y_WT)

            def x_maxt_copy(i, t):
                xr.full(act, i, X_MAXT[t])
                xr.has_emptied(a.copy(x_nmT[0:H, t * P:(t + 1) * P], xr.bank(X_MAXT[t])[0:H, 0:P]), X_MAXT[t])

            def y_maxt_copy(i, _):
                yr.full(act, i, Y_MAXT)
                yr.has_emptied(a.copy(y_nmT[0:H, :], yr.bank(Y_MAXT)[0:H, 0:S]), Y_MAXT)

            def st(scored, mixed, probs, scale):
                def step(i, p):
                    scored.wait(act, i, p + 1)
                    if p >= 2:
                        mixed.wait(act, i, p - 1)
                    a.activation(flat(prob[:, p % 2]), scores[p % 2][0:NK, :], ACT.Exp, scale=scale).then_inc(
                        probs.sem, 1)
                return step

            def take(pvo, an, inv, copied, logged, inverted, i, k):
                a.activation(inv[0:64, :], pvo[64:128, 0:S], ACT.Ln)
                a.activation(inv[64:128, :], pvo[0:64, S:2 * S], ACT.Ln).then_inc(logged.sem, 1)
                a.copy(an[0:64, :], pvo[0:64, 0:S])
                a.copy(an[64:128, :], pvo[64:128, S:2 * S]).then_inc(copied.sem, 1)
                logged.wait(act, i, k)
                a.activation(inv, inv, ACT.Exp, scale=-1.0).then_inc(inverted.sem, 1)

            def x_pv(i, p):
                x_mixed.wait(act, i, p + 1)
                if p < 3:
                    y_attn_lo.wait(act, i - 1, 0)
                else:
                    x_attn_lo.wait(act, i, p - 2)
                take(pv[p % 2], an[:, p % 3, :], sums[:, p % 2, :], x_copied, x_logged, x_recip, i, p + 1)

            def y_pv(i, p):
                if p % 4 == 3:
                    m = p // 4
                    y_mixed.wait(act, i, p + 1)
                    take(pv[m], an[:, m, :], sums[:, m, :], y_copied, y_logged, y_recip, i, m + 1)

            def x_attn_split(i, p):
                x_attn.wait(act, i, p + 1)
                a.copy(q[0][:, p, :], an[:, p % 3, :]).then_inc(x_attn_hi.sem, 1)

            def y_attn_split(i, m):
                y_attn.wait(act, i, m + 1)
                a.activation(q1[0][:, m, :], an[:, m, :], ACT.Identity,
                             bias=bqkv1_s[:, 2, m:m + 1]).then_inc(y_attn_hi.sem, 1)

            def x_made_(i, _):
                x_made.wait(act, i, 1)

            run(act, {"n_load": n_load, "p_load": p_load, "n_tr": x_tr, "n_ctx": x_ctx, "n_k": x_k, "n_v": x_v,
                      "n_q": x_q, "p_tr2": y_tr(Y_TR2), "p_ctx": y_ctx, "y_k": y_k, "y_v": y_v, "p_gate": y_gate,
                      "p_wt": y_wt, "y_tr3": y_tr(Y_TR3), "y_q": y_q, "n_maxt": x_maxt_copy, "y_maxt": y_maxt_copy,
                      "x_st": st(x_scored, x_mixed, x_probs, SCALE0), "y_st": st(y_scored, y_mixed, y_probs, SCALE1),
                      "x_pv": x_pv, "y_pv": y_pv, "x_hi": x_attn_split, "y_hi": y_attn_split, "z_hi": y_attn_split, "x_made": x_made_})
            for k in range(KD):
                act.wait_ge(m_tr, k + 1)
                a.copy(xmT[:, k, :], pv[k][:]).then_inc(m_trc, 1)
            act.wait_ge(m_tr, KD + 1)
            act.wait_ge(m_rs, 3)
            a.copy(m_cT[0:NE, :], xg[0][0:NE, :]).then_inc(m_trc, 1)
            for n in range(KD * NE):
                act.wait_ge(m_gate, n + 1)
                if n >= 1:
                    act.wait_ge(m_inter, n)
                a.activation(m_s, m_g, ACT.Sigmoid, scale=SWIGLU_ALPHA).then_inc(m_sig, 1)

        @block.tensor
        def _(pe):
            t_ = nc.tensor
            pe.wait_ge(setup_done, SET_UP)
            pe.wait_ge(const_done, CONST)
            pe.wait_ge(split_lo, NSPLIT)
            pe.wait_ge(last_in, 16 * 4)

            def products(out_, terms, first=True, last=True):
                n = 0
                for lhsT, rhs in terms:
                    for u, v in ((0, 0), (1, 0), (0, 1)):
                        n += 1
                        ins = t_.matmul(out_, lhsT[u], rhs[v], start=first and n == 1,
                                        stop=last and n == 3 * len(terms))
                return ins

            def products32(out_, terms):
                for n, (lhsT, rhs) in enumerate(terms):
                    ins = t_.matmul(out_, lhsT, rhs, start=n == 0, stop=n == len(terms) - 1)
                return ins

            def both(parts, *at):
                return parts[0][at], parts[1][at]

            ALL = slice(None)

            def transposes(ring, job, src, normed, k_normed):
                def step(i, _):
                    normed.wait(pe, i, k_normed)
                    ring.to_fill(pe, i, job)
                    for k in range(KD):
                        for t in range(T):
                            ins = t_.transpose(ring.bank(job)[:, k * S + t * P:k * S + (t + 1) * P],
                                               src[:, t, k * P:(k + 1) * P], ident[:])
                    ring.has_filled(ins, job)
                return step

            def ctx_transposes(ring, job, src, loaded):
                def step(i, _):
                    loaded.wait(pe, i, 16)
                    ring.to_fill(pe, i, job)
                    for k in range(KD):
                        ins = t_.transpose(ring.bank(job)[:, k * NK:(k + 1) * NK], src[:, k * P:(k + 1) * P],
                                           ident[0:NK, 0:NK])
                    ring.has_filled(ins, job)
                return step

            def x_k(i, c):
                xr.empty(pe, i, X_CTX)
                xr.to_fill(pe, i, X_K[c])
                for m in range(4):
                    col = (4 * c + m) * P
                    ins = products32(xr.bank(X_K[c])[:, m * NK:(m + 1) * NK],
                                     [(wk_s[:, k, col:col + P], ctxT[:, k, :]) for k in range(KD)])
                xr.has_filled(ins, X_K[c])

            def x_v(i, c):
                xr.to_fill(pe, i, X_V[c])
                ins = products32(xr.bank(X_V[c])[0:NK, :],
                                 [(ctxT[:, k, :], wv_s[:, k, 512 * c:512 * (c + 1)]) for k in range(KD)])
                xr.has_filled(ins, X_V[c])

            def x_q(i, c):
                xr.empty(pe, i, X_TR)
                xr.to_fill(pe, i, X_Q + c)
                for m in range(2):
                    col = slice((2 * c + m) * P, (2 * c + m + 1) * P)
                    ins = products(xr.bank(X_Q + c)[:, m * S:(m + 1) * S],
                                   [(both(wq_s, ALL, k, col), both(xT, ALL, k, ALL)) for k in range(KD)])
                xr.has_filled(ins, X_Q + c)

            def x_max(i, j):
                t, c = j // 4, j % 4
                xr.empty(pe, i, X_Q + c)
                xr.to_fill(pe, i, X_MAX[j])
                for m in range(2):
                    p = 2 * c + m
                    ins = t_.matmul(xr.bank(X_MAX[j])[:, m * 2 * NK:(m + 1) * 2 * NK],
                                    q[0][:, p, t * P:(t + 1) * P], flat(kbd[0][:, 2 * p:2 * p + 2, :]),
                                    start=True, stop=True)
                xr.has_filled(ins, X_MAX[j])

            def y_max(i, j):
                t, c = j // 4, j % 4
                yr.empty(pe, i, Y_Q)
                y_kmask.wait(pe, i, 1)
                yr.to_fill(pe, i, Y_MAX[j])
                ins = t_.matmul(yr.bank(Y_MAX[j])[:, 0:4 * NK], q1[0][:, c // 2, t * P:(t + 1) * P],
                                flat(kbd1[0][:, c // 2, 4 * (c % 2):4 * (c % 2) + 4, :]), start=True, stop=True)
                yr.has_filled(ins, Y_MAX[j])

            def x_maxt_in_(i, t):
                xr.empty(pe, i, X_MAX[4 * t + 2])
                xr.empty(pe, i, X_MAX[4 * t + 3])
                xr.to_fill(pe, i, X_MAXT[t])
                xr.has_filled(t_.transpose(xr.bank(X_MAXT[t])[0:H, 0:P], x_nm[:, t, :], ident[:]), X_MAXT[t])

            def y_maxt_in_(i, _):
                yr.empty(pe, i, Y_MAX[6])
                yr.empty(pe, i, Y_MAX[7])
                yr.to_fill(pe, i, Y_MAXT)
                for t in range(T):
                    ins = t_.transpose(yr.bank(Y_MAXT)[0:H, t * P:(t + 1) * P], y_nm[:, t, :], ident[:])
                yr.has_filled(ins, Y_MAXT)

            def scores_of_pair(p, keys, queries, nmT):
                for o in range(2):
                    h = 2 * p + o
                    dst = scores[p % 2][0:NK, o * S:(o + 1) * S]
                    products(dst, [(keys(h), queries(h))], last=False)
                    ins = t_.matmul(dst, ident_r[:, h:h + 1].broadcast_to([P, NK]), nmT[:], start=False, stop=True)
                return ins

            def x_st(i, p):
                xr.empty(pe, i, X_MAXT[1])
                if p >= 2:
                    x_probs.wait(pe, i, p - 1)
                scores_of_pair(p, lambda h: both(kbd, ALL, h, ALL), lambda h: both(q, ALL, h // 2, ALL),
                               x_nmT).then_inc(x_scored.sem, 1)

            def y_st(i, p):
                yr.empty(pe, i, Y_MAXT)
                if p >= 2:
                    y_probs.wait(pe, i, p - 1)
                scores_of_pair(p, lambda h: both(kbd1, ALL, h // 8, h % 8, ALL), lambda h: both(q1, ALL, h // 8, ALL),
                               y_nmT).then_inc(y_scored.sem, 1)

            def x_pv(i, p):
                x_probs.wait(pe, i, p + 1)
                if p >= 2:
                    x_copied.wait(pe, i, p - 1)
                elif p == 1:
                    y_made.wait(pe, i - 1, 0)
                for o in range(2):
                    ins = t_.matmul(pv[p % 2][:, o * S:(o + 1) * S], vx[0:NK, 2 * p + o, :], prob[:, p % 2, o, :],
                                    start=True, stop=True)
                ins.then_inc(x_mixed.sem, 1)

            def x_made_(i, _):
                x_made.wait(pe, i, 1)

            def y_pv(i, p):
                y_probs.wait(pe, i, p + 1)
                if p == 4:
                    y_made.wait(pe, i, 0)
                cols = slice((p // 2) % 2 * S, ((p // 2) % 2 + 1) * S)
                for o in range(2):
                    h = 2 * p + o
                    ins = t_.matmul(pv[p // 4][:, cols], vx1[0:NK, h * P:(h + 1) * P], prob[:, p % 2, o, :],
                                    start=h % 4 == 0, stop=h % 4 == 3)
                ins.then_inc(y_mixed.sem, 1)

            def x_out(i, c):
                t, k0 = c // 2, (c % 2) * 4
                if c == 0:
                    x_copied.wait(pe, i, NPAIR)
                x_attn_lo.wait(pe, i, k0 + 4)
                ins = products(pv[0][:, t * D:(t + 1) * D],
                               [(both(q, ALL, k, slice(t * P, (t + 1) * P)), both(wo_s, ALL, k, ALL))
                                for k in range(k0, k0 + 4)], first=k0 == 0, last=k0 == 4)
                if c == 3:
                    ins.then_inc(x_out_in.sem, 1)

            def y_k(i, _):
                yr.empty(pe, i, Y_CTX)
                yr.to_fill(pe, i, Y_K)
                for m in range(KD):
                    ins = products32(yr.bank(Y_K)[:, m * NK:(m + 1) * NK],
                                     [(w1k_s[:, k, m * P:(m + 1) * P], ctxT1[:, k, :]) for k in range(KD)])
                yr.has_filled(ins, Y_K)

            def y_v(i, _):
                yr.to_fill(pe, i, Y_V)
                ins = products32(yr.bank(Y_V)[0:NK, 0:D], [(ctxT1[:, k, :], w1v_s[:, k, :]) for k in range(KD)])
                yr.has_filled(ins, Y_V)

            def y_gate(i, _):
                yr.empty(pe, i, Y_TR2)
                yr.to_fill(pe, i, Y_GATE)
                for t in range(T):
                    ins = products(yr.bank(Y_GATE)[:, t * NE:(t + 1) * NE],
                                   [(both(yT, ALL, k, slice(t * P, (t + 1) * P)),
                                     (gate_s(0)[:, k, :], gate_s(1)[:, k, :])) for k in range(KD)])
                yr.has_filled(ins, Y_GATE)

            def y_wt(i, _):
                y_gated.wait(pe, i, 10)
                yr.to_fill(pe, i, Y_WT)
                for t in range(T):
                    ins = t_.transpose(yr.bank(Y_WT)[0:NE, t * P:(t + 1) * P], lg[:, t, :], ident[:])
                yr.has_filled(ins, Y_WT)

            def y_eb(i, _):
                yr.empty(pe, i, Y_WT)
                yr.to_fill(pe, i, Y_EB)
                for t in range(T):
                    ins = t_.matmul(yr.bank(Y_EB)[:, t * D:(t + 1) * D], wT[:, t * P:(t + 1) * P], eb_s[:],
                                    start=True, stop=True)
                yr.has_filled(ins, Y_EB)

            def y_ffn(i, j):
                t, n = j % T, j // T
                yr.to_fill(pe, i, Y_FFN[j])
                ins = products(yr.bank(Y_FFN[j])[:], [(both(yT, ALL, k, slice(t * P, (t + 1) * P)),
                                                        both(ew_s, ALL, k, slice(2 * D * n, 2 * D * (n + 1))))
                                                       for k in range(KD)])
                yr.has_filled(ins, Y_FFN[j])

            def y_q(i, _):
                yr.empty(pe, i, Y_TR3)
                yr.to_fill(pe, i, Y_Q)
                for m in range(KD):
                    col = slice(m * P, (m + 1) * P)
                    ins = products(yr.bank(Y_Q)[:, m * S:(m + 1) * S],
                                   [((w1q_s(0)[:, k, col], w1q_s(1)[:, k, col]), both(yT, ALL, k, ALL))
                                    for k in range(KD)])
                yr.has_filled(ins, Y_Q)

            def y_out(i, _):
                y_attn_lo.wait(pe, i, 2)
                for t in range(T):
                    ins = products(pv[1][:, t * D:(t + 1) * D],
                                   [(both(q1, ALL, k, slice(t * P, (t + 1) * P)),
                                     (w1o_s(0)[:, k, :], w1o_s(1)[:, k, :])) for k in range(KD)])
                ins.then_inc(y_out_in.sem, 1)

            run(pe, {
                "n_tr": transposes(xr, X_TR, x_xn, x_normed, 1),
                "n_ctx": ctx_transposes(xr, X_CTX, ctx_in, ctx_loaded),
                "p_ctx": ctx_transposes(yr, Y_CTX, ctx_in1, ctx1_loaded),
                "n_k": x_k, "n_v": x_v, "n_q": x_q, "p_tr2": transposes(yr, Y_TR2, y_xn, y_normed, 1),
                "y_k": y_k, "y_v": y_v, "p_gate": y_gate, "n_max": x_max, "p_wt": y_wt, "p_eb": y_eb,
                "y_ffn": y_ffn, "n_maxt": x_maxt_in_, "x_st": x_st, "y_st": y_st,
                "x_pv": x_pv, "y_pv": y_pv, "y_tr3": transposes(yr, Y_TR3, y_xn, y_normed, 2), "y_q": y_q,
                "y_max": y_max, "y_maxt": y_maxt_in_, "x_out": x_out, "x_made": x_made_, "z_out": y_out})

            pe.wait_ge(m_norm, 3)
            for k in range(KD):
                for t in range(TT):
                    ins = t_.transpose(pv[k][:, t * P:(t + 1) * P], xmn[:, t, k * P:(k + 1) * P],
                                       ident[:])
                ins.then_inc(m_tr, 1)
            pe.wait_ge(m_coef, M_COEF)
            for t in range(TT):
                ins = t_.transpose(xg[0][0:NE, t * P:(t + 1) * P], coef[:, :, t], ident[:])
            ins.then_inc(m_tr, 1)
            pe.wait_ge(m_trc, KD + 1)
            pe.wait_ge(m_in, 16 * (NTOK // S + 1))
            for t in range(TT):
                ins = t_.matmul(scores[t // 2][:, (t % 2) * D:(t % 2 + 1) * D],
                                m_cT[:, t * P:(t + 1) * P], eb_s[:], start=True, stop=True)
            ins.then_inc(m_down, 1)
            for e in range(NE):
                pe.wait_ge(m_w[e % 2], 32 * (e // 2 + 1))
                for m in range(KD):
                    n = KD * e + m
                    if n >= 2:
                        pe.wait_ge(m_upc, n - 1)
                    for u in range(2):
                        ins = products32((xg, yg)[n % 2][u][:], [(gu_s[e % 2][:, k, u, m * P:(m + 1) * P],
                                                                 xmT[:, k, :]) for k in range(KD)])
                    ins.then_inc(m_up, 1)
                pe.wait_ge(m_inter, KD * (e + 1))
                pe.wait_ge(m_acc, e + 1)
                for t in range(TT):
                    ins = products32(scores[t // 2][:, (t % 2) * D:(t % 2 + 1) * D],
                                     [(inter[:, k, t * P:(t + 1) * P], dn_s[e % 2][:, k, :]) for k in range(KD)])
                ins.then_inc(m_down, 1)

        @block.vector
        def _(dve):
            v = nc.vector
            for n in range(NSPLIT):
                dve.wait_ge(split_hi, n + 1)
                v.tensor_tensor(splits[n][2], staged(n), splits[n][1].bitcast(F32), ALU.subtract).then_inc(split_lo, 1)
            dve.wait_ge(tanh_done, 1)
            v.tensor_scalar(bo_tg[:], bo_tg[:], tg[:, 0:1], None, ALU.mult).then_inc(setup_done, 1)
            v.tensor_scalar(bo1_tg[:], bo1_tg[:], tg[:, 1:2], None, ALU.mult).then_inc(setup_done, 1)
            for part in range(2):
                v.memset(flat(kbd[part][:]).bitcast(F32), 0.0)
            v.memset(x_nmT[:].bitcast(F32), 0.0).then_inc(setup_done, 1)
            v.memset(y_nmT[:].bitcast(F32), 0.0).then_inc(setup_done, 1)

            def statistics(src, st6, mv, stats):
                for t in range(T):
                    ins = v.bn_stats(st6[:, t, :], src[:, t, :])
                ins.then_inc(stats.sem, 1)
                dve.drain()
                for t in range(T):
                    ins = v.bn_aggr(mv[:, t, :], st6[:, t, :])
                ins.then_inc(stats.sem, 1)

            def normalise(src, mv, rs, dst, normed):
                for t in range(T):
                    ins = v.tensor_scalar(dst[:, t, :], src[:, t, :], mv[:, t, 0:1], rs[:, 1, t:t + 1],
                                          ALU.subtract, ALU.mult)
                ins.then_inc(normed.sem, 1)

            def n_stat(i, _):
                x_loaded.wait(dve, i, 16)
                statistics(x_in, x_st6, x_mv, x_stats)

            def n_norm(i, _):
                x_rs.wait(dve, i, 2)
                normalise(x_in, x_mv, x_rstd, x_xn, x_normed)

            def p_stat(i, _):
                x_made.wait(dve, i, 1)
                statistics(x1, y_st6, y_mv, y_stats)

            def p_norm(i, _):
                y_rs.wait(dve, i, 2)
                normalise(x1, y_mv, y_rstd, y_xn, y_normed)

            def y_stat3(i, _):
                yr.empty(dve, i, Y_FFN[6])
                yr.empty(dve, i, Y_FFN[7])
                statistics(acc, y_st6, y_mv, y_stats)

            def y_norm3(i, _):
                y_rs.wait(dve, i, 4)
                normalise(acc, y_mv, y_rstd, y_xn, y_normed)

            def lo_of(ring, done, k, i, job, cols, dst, hi):
                done.wait(dve, i, k)
                ring.has_emptied(v.tensor_tensor(dst, ring.bank(job)[:, 0:cols], hi.bitcast(F32), ALU.subtract), job)

            def x_tr(i, _):
                lo_of(xr, x_hi, 2, i, X_TR, KD * S, flat(xT[1][:]), flat(xT[0][:]))

            def x_k(i, c):
                x_hi.wait(dve, i, 1 + 2 * c)
                view = xr.bank(X_K[c])[:, 0:4 * NK].rearrange("p (m n) -> p m n", m=4)
                for half in range(2):
                    rows, heads = slice(64 * half, 64 * half + 64), slice(8 * c + half, 8 * c + 8, 2)
                    ins = v.tensor_tensor(kbd[1][rows, heads, :], view[rows], kbd[0][rows, heads, :].bitcast(F32),
                                          ALU.subtract)
                xr.has_emptied(ins, X_K[c])

            def x_q(i, c):
                lo_of(xr, x_hi, 4 + c, i, X_Q + c, 2 * S, flat(q[1][:, 2 * c:2 * c + 2, :]),
                      flat(q[0][:, 2 * c:2 * c + 2, :]))

            def y_tr(job, k):
                return lambda i, _: lo_of(yr, y_hi, k, i, job, KD * S, flat(yT[1][:]), flat(yT[0][:]))

            def biased_lo(i, k, job, cols, parts, b):
                y_hi.wait(dve, i, k)
                for m in range(KD):
                    ins = v.scalar_tensor_tensor(out=parts[1][:, m, :], in0=yr.bank(job)[:, m * cols:(m + 1) * cols],
                                                 scalar=bqkv1_s[:, b, m:m + 1], in1=parts[0][:, m, :].bitcast(F32),
                                                 op0=ALU.add, op1=ALU.subtract)
                yr.has_emptied(ins, job)

            def y_k(i, _):
                y_kmask.wait(dve, i, 0)
                biased_lo(i, 2, Y_K, NK, k1, 1)

            def y_q(i, _):
                biased_lo(i, 4, Y_Q, S, q1, 0)

            def maxima(ring, max_job, nm):
                def step(i, j):
                    t, c = j // 4, j % 4
                    ring.full(dve, i, max_job[j])
                    ring.has_emptied(v.tensor_reduce(
                        nm[:, t, 4 * c:4 * c + 4],
                        ring.bank(max_job[j])[:, 0:4 * NK].rearrange("p (h n) -> p h n", h=4), AX_X, ALU.max,
                        negate=True), max_job[j])
                return step

            def over_experts(a):
                return a.unsqueeze(2).broadcast_to([P, T, NE])

            def y_gate(i, _):
                done = y_gated
                yr.full(dve, i, Y_GATE)
                yr.has_emptied(v.tensor_tensor(
                    lg[:], yr.bank(Y_GATE)[:, 0:T * NE].rearrange("p (t e) -> p t e", t=T),
                    gate_b_s[:].unsqueeze(1).broadcast_to([P, T, NE]), ALU.add), Y_GATE)
                yr.empty(dve, i, Y_GATE)
                v.tensor_reduce(lg_n[:, 0, :], lg[:], AX_X, ALU.max, negate=True).then_inc(done.sem, 1)
                done.wait(dve, i, 1)
                v.tensor_tensor(lg[:], lg[:], over_experts(lg_n[:, 0, :]), ALU.add).then_inc(done.sem, 1)
                y_exp.wait(dve, i, 1)
                v.tensor_reduce(lg_n[:, 1, :], lg[:], AX_X, ALU.add).then_inc(done.sem, 1)
                done.wait(dve, i, 3)
                v.reciprocal(lg_n[:, 2, :], lg_n[:, 1, :]).then_inc(done.sem, 1)
                done.wait(dve, i, 4)
                v.tensor_tensor(lg[:], lg[:], over_experts(lg_n[:, 2, :]), ALU.mult).then_inc(done.sem, 1)
                done.wait(dve, i, 5)
                v.scalar_tensor_tensor(out=flat(lg[:]), in0=flat(lg[:]), scalar=THRESHOLD, in1=flat(lg[:]),
                                       op0=ALU.is_ge, op1=ALU.mult).then_inc(done.sem, 1)
                done.wait(dve, i, 6)
                v.tensor_reduce(lg_n[:, 1, :], lg[:], AX_X, ALU.add).then_inc(done.sem, 1)
                done.wait(dve, i, 7)
                v.scalar_tensor_tensor(out=lg_n[:, 3, :], in0=lg_n[:, 1, :], scalar=0.0, in1=lg_n[:, 1, :],
                                       op0=ALU.is_equal, op1=ALU.add).then_inc(done.sem, 1)
                done.wait(dve, i, 8)
                v.reciprocal(lg_n[:, 2, :], lg_n[:, 3, :]).then_inc(done.sem, 1)
                done.wait(dve, i, 9)
                v.scalar_tensor_tensor(out=lg[:], in0=lg[:], scalar=tg[:, 2:3], in1=over_experts(lg_n[:, 2, :]),
                                       op0=ALU.mult, op1=ALU.mult).then_inc(done.sem, 1)

            def y_eb(i, _):
                y_resd.wait(dve, i, 0)
                yr.full(dve, i, Y_EB)
                yr.has_emptied(v.tensor_tensor(flat(acc[:]), yr.bank(Y_EB)[:], flat(x1[:]), ALU.add), Y_EB)

            def y_ffn(i, j):
                t, n = j % T, j // T
                y_gated.wait(dve, i, 10)
                yr.empty(dve, i, Y_EB)
                yr.full(dve, i, Y_FFN[j])
                for o in range(2):
                    ins = v.scalar_tensor_tensor(out=acc[:, t, :], in0=yr.bank(Y_FFN[j])[:, o * D:(o + 1) * D],
                                                 scalar=lg[:, t, 2 * n + o:2 * n + o + 1], in1=acc[:, t, :],
                                                 op0=ALU.mult, op1=ALU.add)
                    if o == 0:
                        ins.then_inc(y_acc.sem, 1)
                        y_acc.wait(dve, i, j + 1)
                yr.has_emptied(ins, Y_FFN[j])

            def y_attn_split(i, m):
                y_attn_hi.wait(dve, i, m + 1)
                v.scalar_tensor_tensor(out=q1[1][:, m, :], in0=an[:, m, :], scalar=bqkv1_s[:, 2, m:m + 1],
                                       in1=q1[0][:, m, :].bitcast(F32), op0=ALU.add,
                                       op1=ALU.subtract).then_inc(y_attn_lo.sem, 1)

            def x_out(i, c):
                if c == 3:
                    x_resd.wait(dve, i, 1)
                    x_out_in.wait(dve, i, 1)
                    v.scalar_tensor_tensor(out=flat(x1[:]), in0=pv[0][:], scalar=tg[:, 0:1], in1=flat(x_res[:]),
                                           op0=ALU.mult, op1=ALU.add).then_inc(x_made.sem, 1)

            def y_out(i, _):
                y_resd.wait(dve, i, 1)
                y_out_in.wait(dve, i, 1)
                v.scalar_tensor_tensor(out=flat(y_x3[:]), in0=pv[1][:], scalar=tg[:, 1:2], in1=flat(y_x3[:]),
                                       op0=ALU.mult, op1=ALU.add).then_inc(y_made.sem, 1)

            run(dve, {"n_stat": n_stat, "n_norm": n_norm, "p_stat": p_stat, "p_norm": p_norm, "y_stat3": y_stat3,
                      "y_norm3": y_norm3, "n_tr": x_tr, "n_k": x_k, "n_q": x_q,
                      "p_tr2": y_tr(Y_TR2, 1), "y_tr3": y_tr(Y_TR3, 3), "y_k": y_k, "y_q": y_q,
                      "n_max": maxima(xr, X_MAX, x_nm), "y_max": maxima(yr, Y_MAX, y_nm), "p_gate": y_gate,
                      "p_eb": y_eb, "y_ffn": y_ffn, "y_hi": y_attn_split, "z_hi": y_attn_split, "x_out": x_out, "z_out": y_out})

            dve.wait_ge(m_in, 16 * (NTOK // S + 1))
            for t in range(TT):
                ins = v.bn_stats(m_st6[:, t, :], xm[:, t, :])
            ins.then_inc(m_norm, 1)
            dve.wait_ge(m_norm, 1)
            for t in range(TT):
                ins = v.bn_aggr(m_mv[:, t, :], m_st6[:, t, :])
            ins.then_inc(m_norm, 1)
            v.tensor_copy(idx_f[:], idx_s[:]).then_inc(m_coef, 1)
            dve.wait_ge(m_coef, 1)
            n = 1
            for t in range(TT):
                v.tensor_scalar(coef_k[:], expert_no[:], idx_f[:, t, 0:1], None, ALU.is_equal).then_inc(m_coef, 1)
                dve.wait_ge(m_coef, n + 1)
                v.scalar_tensor_tensor(out=coef_k[:], in0=expert_no[:], scalar=idx_f[:, t, 1:2], in1=coef_k[:],
                                       op0=ALU.is_equal, op1=ALU.add).then_inc(m_coef, 1)
                dve.wait_ge(m_coef, n + 2)
                v.scalar_tensor_tensor(out=coef[:, :, t], in0=rw_s[:, t, :], scalar=tg[:, 3:4], in1=coef_k[:],
                                       op0=ALU.mult, op1=ALU.mult).then_inc(m_coef, 1)
                n += 3
                dve.wait_ge(m_coef, n)
            dve.wait_ge(m_rs, 2)
            for t in range(TT):
                ins = v.tensor_scalar(xmn[:, t, :], xm[:, t, :], m_mv[:, t, 0:1], m_rstd[:, 1, t:t + 1],
                                      ALU.subtract, ALU.mult)
            ins.then_inc(m_norm, 1)

            def add_down(t, scalar):
                dst, src = xm[:, t, :], scores[t // 2][:, (t % 2) * D:(t % 2 + 1) * D]
                if scalar is None:
                    return v.tensor_tensor(dst, src, dst, ALU.add)
                return v.scalar_tensor_tensor(out=dst, in0=src, scalar=scalar, in1=dst, op0=ALU.mult, op1=ALU.add)

            dve.wait_ge(m_norm, 3)
            dve.wait_ge(m_down, 1)
            for t in range(TT):
                ins = add_down(t, None)
            ins.then_inc(m_acc, 1)
            for e in range(NE):
                for m in range(KD):
                    n = KD * e + m
                    banks = (xg, yg)[n % 2]
                    dve.wait_ge(m_up, n + 1)
                    v.tensor_scalar(m_g, banks[0][:], gu_b_s[:, e, m, 0:1], LIMIT, ALU.add,
                                    ALU.min).then_inc(m_gate, 1)
                    v.tensor_scalar(m_u, banks[1][:], gu_b_s[:, e, m, 1:2], LIMIT, ALU.add,
                                    ALU.min).then_inc(m_upc, 1)
                    dve.wait_ge(m_upc, n + 1)
                    v.tensor_scalar(m_u, m_u, -LIMIT, 1.0, ALU.max, ALU.add)
                    dve.wait_ge(m_sig, n + 1)
                    v.tensor_tensor(m_g, m_g, m_s, ALU.mult).then_inc(m_glu, 1)
                    dve.wait_ge(m_glu, n + 1)
                    v.tensor_tensor(inter[:, m, :], m_g, m_u, ALU.mult).then_inc(m_inter, 1)
                    dve.wait_ge(m_inter, n + 1)
                dve.wait_ge(m_down, e + 2)
                for t in range(TT):
                    ins = add_down(t, coef[:, e, t:t + 1])
                ins.then_inc(m_acc, 1)
                dve.wait_ge(m_acc, e + 2)


def kernel(**inputs):
    import numpy as _np
    import concourse.bacc as _bacc
    from concourse import mybir as _mybir
    from concourse.bass_utils import run_bass_kernel_spmd as _run

    a = {k: _np.asarray(v) for k, v in inputs.items()}
    kd, ne = D // P, NE

    def rows(w):
        return _np.ascontiguousarray(w.reshape(-1, P, w.shape[-1]).transpose(1, 0, 2))

    def columns(b):
        return b.reshape(-1, P).T

    w1 = _np.concatenate([rows(a[n]).reshape(P, -1) for n in ("L1_xattn_wq", "L1_xattn_wo", "L0_ffn_gate_w")], 1)
    gu = a["L1_ffn_gate_up_proj"].reshape(ne, kd, P, D, 2).transpose(0, 2, 1, 4, 3)
    arrays = {
        "x": a["x"], "ctx": a["ctx_1024"],
        "gates": _np.concatenate([a["g_xattn"], a["g_ffn"]]),
        "wq": rows(a["L0_xattn_Wq"].T), "wk": rows(a["L0_xattn_Wk"].T), "wv": rows(a["L0_xattn_Wv"].T),
        "wo": rows(a["L0_xattn_Wo"].T), "bo": a["L0_xattn_bo"],
        "gate_b": a["L0_ffn_gate_b"],
        "ew": a["L0_ffn_expert_w"].reshape(ne, kd, P, D).transpose(2, 1, 0, 3).reshape(P, kd, ne * D),
        "eb": a["L0_ffn_expert_b"], "w1": w1,
        "w1k": rows(a["L1_xattn_wk"]), "w1v": rows(a["L1_xattn_wv"]),
        "bqkv1": _np.stack([columns(a[n]) for n in ("L1_xattn_bq", "L1_xattn_bk", "L1_xattn_bv")], 1),
        "bo1": a["L1_xattn_bo"],
        "router_idx": a["L1_ffn_router_indices"].reshape(TT, P, 2).transpose(1, 0, 2),
        "router_w": a["L1_ffn_routing_weights"].reshape(TT, P, ne).transpose(1, 0, 2),
        "gu": gu, "gu_b": a["L1_ffn_gate_up_proj_bias"].reshape(ne, kd, P, 2).transpose(2, 0, 1, 3),
        "dn": a["L1_ffn_down_proj"].reshape(ne, kd, P, D).transpose(0, 2, 1, 3), "dn_b": a["L1_ffn_down_proj_bias"],
    }
    order = ["x", "ctx", "gates", "wq", "wk", "wv", "wo", "bo", "gate_b", "ew", "eb", "w1", "w1k", "w1v", "bqkv1",
             "bo1", "router_idx", "router_w", "gu", "gu_b", "dn", "dn_b"]
    nc = _bacc.Bacc("TRN2", target_bir_lowering=False, num_devices=1)
    maps, args = {}, []
    for name in order:
        v = _np.ascontiguousarray(arrays[name])
        maps[f"in_{name}"] = v
        args.append(nc.dram_tensor(f"in_{name}", v.shape, _mybir.dt.from_np(v.dtype), kind="ExternalInput").ap())
    args.append(nc.dram_tensor("out_0", (B, S, D), F32, kind="ExternalOutput").ap())
    flamingo_stack(nc, *args)
    r = _run(nc, [maps], core_ids=[0])
    return r.results[0]["out_0"]
```

```python
from contextlib import ExitStack

import concourse.bass as bass
from concourse import mybir

F32 = mybir.dt.float32
F32R = mybir.dt.float32r
I32 = mybir.dt.int32
ALU = mybir.AluOpType
ACT = mybir.ActivationFunctionType
AX_X = mybir.AxisListType.X

P = 128
B, S, D = 64, 256, 256
NK = 120
T = S // P
KD = D // P
H = 16
DH0, DH1 = 64, 16
INNER = H * DH0
NPAIR = H // 2
HPT1 = P // DH1
NE = 8
NTOK = 512
TT = NTOK // P
EPS = 1e-5
THRESHOLD = 0.1
SWIGLU_ALPHA, LIMIT = 1.702, 7.0
SCALE0, SCALE1 = DH0 ** -0.5, DH1 ** -0.5

X_CTX, X_TR, X_K, X_V, X_Q = 0, 1, (2, 3), (4, 5), 6
X_MAX, X_MAXT = (10, 11, 12, 13, 14, 15, 17, 18), (16, 19)
X_JOBS = 20
Y_TR2, Y_GATE, Y_LG, Y_WT, Y_EB = 0, 1, 2, 4, 5
Y_CTX, Y_K, Y_V = 3, 7, 9
Y_FFN = (6, 8, 10, 11, 12, 13, 14, 15)
Y_TR3, Y_Q, Y_MAX, Y_MAXT = 16, 17, (18, 19, 20, 21, 22, 23, 25, 26), (24, 27)
Y_JOBS = 28


def steps(x, y, n, p, z):
    batch = {"x": x, "y": y, "n": n, "p": p, "z": z}
    out = []

    def do(name, k=0):
        if batch[name[0]] is not None:
            out.append((name, k, batch[name[0]]))

    for s in range(NPAIR):
        if s <= 1:
            do("x_st", s)
        if s < 7:
            do("y_ffn", s)
        if s > 1:
            do("x_st", s)
        do("x_split", s)
        if s == 0:
            do("n_load")
            do("y_k")
            do("z_hi", 1)
        if s == 1:
            do("y_v")
            do("z_out")
        if s >= 1:
            do("x_pv", s - 1)
        if s >= 2:
            do("x_hi", s - 2)
        if s == 3:
            do("n_stat")
        if s == 4:
            do("n_ctx")
            do("n_norm")
        if s == 5:
            do("n_tr")
            do("p_load")
        if s == 6:
            do("y_ffn", 7)
            do("y_stat3")
    do("y_norm3")
    do("n_k", 0)
    do("n_k", 1)
    do("x_pv", 7)
    do("x_hi", 6)
    do("n_v", 0)
    do("y_tr3")
    do("n_v", 1)
    do("x_hi", 7)
    do("y_q")
    do("x_out", 0)
    do("x_out", 1)
    do("y_res")
    do("y_max", 0)
    do("y_max", 1)
    do("x_out", 2)
    do("y_max", 2)
    do("y_max", 3)
    do("x_out", 3)
    do("y_max", 4)
    do("y_max", 5)
    do("n_q", 0)
    do("y_maxt", 0)
    do("y_max", 6)
    do("y_max", 7)
    do("n_q", 1)
    do("y_maxt", 1)
    do("n_q", 2)
    do("x_made")
    for s in range(NPAIR):
        do("y_st", s)
        if s == 0:
            do("n_q", 3)
            do("n_res")
            do("p_stat")
        if s == 4:
            do("n_maxt", 0)
        if s >= 1:
            do("y_pv", s - 1)
        if 1 <= s <= 4:
            do("n_max", 2 * (s - 1))
            do("n_max", 2 * (s - 1) + 1)
        if s == 1:
            do("p_norm")
        if s == 2:
            do("p_tr2")
        if s == 3:
            do("p_gate")
        if s == 4:
            do("p_lg")
        if s == 5:
            do("p_ctx")
            do("y_hi", 0)
        if s == 6:
            do("n_maxt", 1)
            do("p_wt")
    do("y_pv", NPAIR - 1)
    do("p_eb")
    return out


class Signal:

    def __init__(self, sem, per):
        self.sem, self.per = sem, per

    def wait(self, eng, i, k):
        value = i * self.per + k
        if isinstance(value, int) and value <= 0:
            return
        eng.wait_ge(self.sem, value)


class Ring:

    def __init__(self, banks, filled, emptied):
        self.banks, self.filled, self.emptied, self.n = banks, filled, emptied, len(banks)

    def bank(self, job):
        return self.banks[job % self.n]

    def to_fill(self, eng, i, job):
        self.emptied[job % self.n].wait(eng, i, job // self.n)

    def full(self, eng, i, job):
        self.filled[job % self.n].wait(eng, i, job // self.n + 1)

    def empty(self, eng, i, job):
        self.emptied[job % self.n].wait(eng, i, job // self.n + 1)

    def has_filled(self, ins, job):
        ins.then_inc(self.filled[job % self.n].sem, 1)

    def has_emptied(self, ins, job):
        ins.then_inc(self.emptied[job % self.n].sem, 1)


def flamingo_stack(nc, x, ctx, gates, wq, wk, wv, wo, bo, gate_b, ew, eb, w1, w1k, w1v, bqkv1, bo1,
                   router_idx, router_w, gu, gu_b, dn, dn_b, out):
    es = ExitStack()
    with es:
        def sb(name, shape, dt=F32):
            return es.enter_context(nc.sbuf_tensor(name, shape, dt))

        def pb(name):
            return es.enter_context(nc.psum_tensor(name, [P, 512], F32))

        def sem(name):
            return es.enter_context(nc.semaphore(name))

        def signal(name, per=1):
            return Signal(sem(name), per)

        def pair(name, shape):
            return sb(name + "_hi", shape, F32R), sb(name + "_lo", shape, F32R)

        wq_s = pair("wq", [P, KD, INNER])
        wo_s = pair("wo", [P, INNER // P, D])
        ew_s = pair("ew", [P, KD, NE * D])
        w1_s = pair("w1", [P, 2 * KD * D + KD * NE])
        wk_s, wv_s = sb("wk_s", [P, KD, INNER]), sb("wv_s", [P, KD, INNER])
        w1k_s, w1v_s = sb("w1k_s", [P, KD, D]), sb("w1v_s", [P, KD, D])
        eb3 = sb("eb3", [P, D], F32R)
        stage = (wk_s, wv_s)

        def w1q_s(n):
            return w1_s[n][:, 0:KD * D].rearrange("p (k n) -> p k n", k=KD)

        def w1o_s(n):
            return w1_s[n][:, KD * D:2 * KD * D].rearrange("p (k n) -> p k n", k=KD)

        def gate_s(n):
            return w1_s[n][:, 2 * KD * D:].rearrange("p (k n) -> p k n", k=KD)

        ident = sb("ident", [P, P])
        ident_r = sb("ident_r", [P, H], F32R)
        own_head = sb("own_head", [P, HPT1])
        tg = sb("tg", [P, 4])
        bo_tg, bo1_tg = sb("bo_tg", [P, D]), sb("bo1_tg", [P, D])
        gate_b_s = sb("gate_b_s", [NE, 1])
        bqkv1_s = sb("bqkv1_s", [P, 3, KD])
        neg_half, eps = sb("neg_half", [P, TT]), sb("eps", [P, T])
        x_in = sb("x_in", [P, T, D])
        x_res = sb("x_res", [P, T, D])
        x_st6, x_mv, x_rstd = sb("x_st6", [P, T, 6]), sb("x_mv", [P, T, 2]), sb("x_rstd", [P, 2, T])
        xT = pair("xT", [P, KD, S])
        q = pair("q", [P, NPAIR, S])
        kbd = pair("kbd", [P, H, NK])
        vx, vx_lo = sb("vx", [P, H, P], F32R), sb("vx_lo", [P, H, DH0], F32R)
        x_prob = pair("x_prob", [NK, 2, S])
        x_nm, x_nmT = sb("x_nm", [P, T, H]), sb("x_nmT", [P, S], F32R)
        xn = sb("xn", [P, T, D])
        ctx_in, ctxT = sb("ctx_in", [NK, D]), sb("ctxT", [P, KD, NK])
        prob = sb("prob", [NK, 2, 2, S])
        an, sums = sb("an", [P, 3, S]), sb("sums", [P, 2, S])
        x1 = sb("x1", [P, T, D])
        y_st6, y_mv, y_rstd = sb("y_st6", [P, T, 6]), sb("y_mv", [P, T, 2]), sb("y_rstd", [P, 2, T])
        yT = pair("yT", [P, KD, S])
        lg, lg_n, lgT = sb("lg", [P, T, NE]), sb("lg_n", [P, 4, T]), sb("lgT", [P, S])
        wT = sb("wT", [P, S], F32R)
        q1 = pair("q1", [P, KD, S])
        k1 = pair("k1", [P, KD, NK])
        kbd1 = pair("kbd1", [P, KD, HPT1, NK])
        VX1 = H * P + 4 * DH1 + P
        vx1 = sb("vx1", [P, VX1])
        y_nm, y_nmT = sb("y_nm", [P, T, H]), sb("y_nmT", [P, S], F32R)
        y_x3 = sb("y_x3", [P, T, D])
        eb_s = y_x3[:, 0, :]

        def v1_block(g, ones):
            at = g * 4 * P + 64 * ones
            return vx1[:, at:at + 4 * (P + DH1)].rearrange("p (j c) -> p j c", j=4)[:, :, 0:DH1]

        xg, yg = [pb("xg0"), pb("xg1")], [pb("yg0"), pb("yg1")]
        scores, pv = [pb("scores0"), pb("scores1")], [pb("pv0"), pb("pv1")]

        stage_in = [sem("stage_in0"), sem("stage_in1")]
        small_in = sem("small_in")
        last_in = sem("last_in")
        split_hi, split_lo = sem("split_hi"), sem("split_lo")
        tanh_done, const_done, setup_done = sem("tanh_done"), sem("const_done"), sem("setup_done")

        xr = Ring(xg, [signal(f"x_filled{n}", X_JOBS // 2) for n in range(2)],
                  [signal(f"x_emptied{n}", X_JOBS // 2) for n in range(2)])
        yr = Ring(yg, [signal(f"y_filled{n}", Y_JOBS // 2) for n in range(2)],
                  [signal(f"y_emptied{n}", Y_JOBS // 2) for n in range(2)])
        x_loaded, ctx_loaded, ctx1_loaded = (signal("x_loaded", 16), signal("ctx_loaded", 16),
                                             signal("ctx1_loaded", 16))
        x_stats, x_rs, x_resd, x_normed = (signal("x_stats", 2), signal("x_rs", 2), signal("x_resd"),
                                           signal("x_normed"))
        x_hi = signal("x_hi", 7)
        x_scored, x_probs, x_mixed = (signal("x_scored", NPAIR), signal("x_probs", NPAIR),
                                      signal("x_mixed", NPAIR))
        x_prob_hi, x_prob_lo, x_v_hi = signal("x_prob_hi", NPAIR), signal("x_prob_lo", NPAIR), signal("x_v_hi", 2)
        x_logged, y_logged = signal("x_logged", NPAIR), signal("y_logged", 2)
        x_copied, x_recip, x_attn = (signal("x_copied", NPAIR), signal("x_recip", NPAIR),
                                     signal("x_attn", NPAIR))
        x_out_in, x_made = signal("x_out_in"), signal("x_made")
        y_out_in, y_made = signal("y_out_in"), signal("y_made")
        x_attn_hi, x_attn_lo = signal("x_attn_hi", NPAIR), signal("x_attn_lo", NPAIR)
        y_stats, y_rs, y_resd, y_normed = (signal("y_stats", 4), signal("y_rs", 4), signal("y_resd"),
                                           signal("y_normed", 2))
        y_hi, y_kmask = signal("y_hi", 4), signal("y_kmask", 1)
        y_gated, y_exp, y_wt_hi = signal("y_gated", 9), signal("y_exp"), signal("y_wt_hi")
        y_acc = signal("y_acc", NE)
        y_scored, y_probs, y_mixed = (signal("y_scored", NPAIR), signal("y_probs", NPAIR),
                                      signal("y_mixed", NPAIR))
        y_copied, y_recip, y_attn = signal("y_copied", 2), signal("y_recip", 2), signal("y_attn", 2)
        y_attn_hi, y_attn_lo = signal("y_attn_hi", 2), signal("y_attn_lo", 2)
        y_stored = signal("y_stored", 16)
        m_in, m_zeroed, m_gu_in, m_dn_in = sem("m_in"), sem("m_zeroed"), [sem(f"m_gu_in{r}") for r in range(2)], [sem(f"m_dn_in{r}") for r in range(2)]
        (m_norm, m_rs, m_coef, m_tr, m_trc, m_up, m_gate, m_upc, m_sig, m_inter, m_down, m_acc, m_stored, m_glu) = (
            sem(n) for n in ("m_norm", "m_rs", "m_coef", "m_tr", "m_trc", "m_up", "m_gate", "m_upc", "m_sig",
                             "m_inter", "m_down", "m_acc", "m_stored", "m_glu"))

        x_rows = x.rearrange("b (t p) d -> b p t d", p=P)
        out_rows = out.rearrange("b (t p) d -> b p t d", p=P)

        def flat(a):
            return a.rearrange("p k n -> p (k n)")

        wv_f, wk_f = flat(wv_s[:]), flat(wk_s[:])
        xm = wv_f[:, 0:TT * D].rearrange("p (t d) -> p t d", t=TT)
        xmn = wv_f[:, TT * D:2 * TT * D].rearrange("p (t d) -> p t d", t=TT)
        xmT = vx1[:, 0:KD * NTOK].rearrange("p (k n) -> p k n", k=KD)
        inter = [a.rearrange("p (k n) -> p k n", k=KD) for a in (
            vx1[:, KD * NTOK:2 * KD * NTOK], wv_f[:, TT * D:2 * TT * D])]
        gu_s = [wk_f[:, r * 4 * D:(r + 1) * 4 * D].rearrange("p (k g n) -> p k g n", k=KD, g=2) for r in range(2)]
        dn_s = [w1k_s, w1v_s]
        m_g, m_u, m_s = flat(x_in[:]), flat(xn[:]), flat(x_res[:])
        m_cT = flat(x1[:])
        M_COEF = 1 + 3 * TT
        coef, coef_k = sb("coef", [P, NE, TT]), sb("coef_k", [P, NE])
        rw_s, idx_s, idx_f = sb("rw_s", [P, TT, NE]), sb("idx_s", [P, TT, 2], I32), sb("idx_f", [P, TT, 2])
        gu_b_s, expert_no = sb("gu_b_s", [P, NE, KD, 2]), sb("expert_no", [P, NE])
        m_st6, m_mv, m_rstd = sb("m_st6", [P, TT, 6]), sb("m_mv", [P, TT, 2]), sb("m_rstd", [P, 2, TT])

        block = es.enter_context(nc.Block())

        def run(eng, table):
            def one(*batches):
                for name, k, i in steps(*batches):
                    if name in table:
                        table[name](i, k)

            one(None, None, 0, None, None)
            one(0, None, 1, 0, None)
            one(1, 0, 2, 1, None)
            with eng.Fori(2, B - 1) as i:
                one(i, i - 1, i + 1, i, i - 2)
            one(B - 1, B - 2, None, B - 1, B - 3)
            one(None, B - 1, None, None, B - 2)
            one(None, None, None, None, B - 1)

        splits = [(flat(wq), flat(wq_s[0][:]), flat(wq_s[1][:])), (flat(wo), flat(wo_s[0][:]), flat(wo_s[1][:]))]
        splits += [(ew[:, k, :], ew_s[0][:, k, :], ew_s[1][:, k, :]) for k in range(KD)]
        splits += [(w1, w1_s[0][:], w1_s[1][:])]
        NSPLIT = len(splits)

        def staged(n):
            return flat(stage[n % 2][:])[:, 0:splits[n][0].shape[1]]

        EB_ROWS = (0, 32, 64)
        SMALL = 16 * 11
        ZEROED, CONST = 8, 13
        SET_UP = 6

        @block.sync
        def _(sp):
            for n in range(NSPLIT):
                if n >= 2:
                    sp.wait_ge(split_lo, n - 1)
                sp.dma_start(staged(n), splits[n][0]).then_inc(stage_in[n % 2], 16)
                if n == 0:
                    for dst, src in ((tg, gates), (bo_tg, bo), (bo1_tg, bo1)):
                        sp.dma_start(dst[:], src.partition_broadcast(P)).then_inc(small_in, 16)
                    for dst, src in ((gate_b_s, gate_b), (bqkv1_s, bqkv1), (rw_s, router_w), (idx_s, router_idx), (gu_b_s, gu_b)):
                        sp.dma_start(dst[:], src).then_inc(small_in, 16)
                    sp.wait_ge(const_done, ZEROED)
                    for r in EB_ROWS:
                        sp.dma_start(eb_s[r:r + NE, :], eb).then_inc(small_in, 16)
            sp.dma_start(w1k_s[:], w1k).then_inc(last_in, 16)
            sp.dma_start(w1v_s[:], w1v).then_inc(last_in, 16)
            sp.wait_ge(split_lo, NSPLIT)
            sp.dma_start(wk_s[:], wk).then_inc(last_in, 16)
            sp.dma_start(wv_s[:], wv).then_inc(last_in, 16)

            def y_out(i, _):
                y_made.wait(sp, i, 1)
                sp.dma_start(out_rows[i], y_x3[:]).then_inc(y_stored.sem, 16)

            run(sp, {"z_out": y_out})
            sp.wait_ge(y_stored.sem, 16 * B)
            for b in range(NTOK // S):
                sp.dma_start(xm[:, b * T:(b + 1) * T, :], out_rows[b]).then_inc(m_in, 16)
            sp.wait_ge(m_zeroed, 1)
            sp.dma_start(eb_s[0:NE, :], dn_b).then_inc(m_in, 16)
            for e in range(NE):
                if e >= 2:
                    sp.wait_ge(m_up, KD * (e - 1))
                sp.dma_start(gu_s[e % 2], gu[e]).then_inc(m_gu_in[e % 2], 16)
                if e >= 2:
                    sp.wait_ge(m_down, e)
                sp.dma_start(dn_s[e % 2][:], dn[e]).then_inc(m_dn_in[e % 2], 16)
            sp.wait_ge(m_acc, 1 + NE)
            for b in range(NTOK // S):
                sp.dma_start(out_rows[b], xm[:, b * T:(b + 1) * T, :]).then_inc(m_stored, 16)
            sp.wait_ge(m_stored, 16 * (NTOK // S))

        @block.gpsimd
        def _(pool):
            g = nc.gpsimd
            for tile, value in ((ident, 0.0), (own_head, 1.0), (neg_half, -0.5), (eps, EPS), (y_x3, 0.0), (vx1, 0.0)):
                g.memset(tile[:], value).then_inc(const_done, 1)
            g.iota(expert_no[:], pattern=[[1, NE]], base=0, channel_multiplier=0,
                   allow_small_or_imprecise_dtypes=True).then_inc(const_done, 1)
            g.memset(vx[:].bitcast(F32), 1.0).then_inc(const_done, 1)
            pool.wait_ge(const_done, ZEROED)
            g.affine_select(out=ident[:], in_=ident[:], compare_op=ALU.not_equal, fill=1.0, base=0,
                            pattern=[[-1, P]], channel_multiplier=1).then_inc(const_done, 1)
            g.affine_select(out=own_head[:], in_=own_head[:], compare_op=ALU.is_ge, fill=0.0, base=0,
                            pattern=[[-DH1, HPT1]], channel_multiplier=1).then_inc(const_done, 1)
            pool.wait_ge(const_done, ZEROED + 2)
            g.affine_select(out=own_head[:], in_=own_head[:], compare_op=ALU.is_ge, fill=0.0, base=DH1 - 1,
                            pattern=[[DH1, HPT1]], channel_multiplier=-1).then_inc(const_done, 1)
            for half in range(2):
                for gr in range(half, 4, 2):
                    last = g.memset(v1_block(gr, 1), 1.0)
                last.then_inc(const_done, 1)

            def rstd(mv, rs, stats, k_stats, done, k, i):
                stats.wait(pool, i, k_stats)
                g.tensor_tensor(rs[:, 0, :], mv[:, :, 1], eps[:], ALU.add).then_inc(done.sem, 1)
                done.wait(pool, i, k + 1)
                g.tensor_tensor(rs[:, 1, :], rs[:, 0, :], neg_half[:, 0:T], ALU.pow).then_inc(done.sem, 1)

            def n_norm(i, _):
                rstd(x_mv, x_rstd, x_stats, 2, x_rs, 0, i)

            def n_res(i, _):
                x_loaded.wait(pool, i, 16)
                x_made.wait(pool, i, 0)
                g.tensor_tensor(x_res[:], x_in[:], bo_tg[:].unsqueeze(1).broadcast_to([P, T, D]),
                                ALU.add).then_inc(x_resd.sem, 1)

            def y_norm2(i, _):
                rstd(y_mv, y_rstd, y_stats, 2, y_rs, 0, i)

            def y_stat3(i, _):
                rstd(y_mv, y_rstd, y_stats, 4, y_rs, 2, i)

            def y_res(i, _):
                y_stored.wait(pool, i, 0)
                g.tensor_tensor(y_x3[:], x1[:], bo1_tg[:].unsqueeze(1).broadcast_to([P, T, D]),
                                ALU.add).then_inc(y_resd.sem, 1)

            def y_k(i, _):
                yr.empty(pool, i, Y_K)
                for part in range(2):
                    for m in range(KD):
                        last = g.tensor_tensor(
                            kbd1[part][:, m, :, :],
                            k1[part][:, m, :].bitcast(F32).unsqueeze(1).broadcast_to([P, HPT1, NK]),
                            own_head[:].unsqueeze(2).broadcast_to([P, HPT1, NK]), ALU.mult)
                last.then_inc(y_kmask.sem, 1)

            def x_pv(i, p):
                x_recip.wait(pool, i, p + 1)
                g.tensor_tensor(an[:, p % 3, :], an[:, p % 3, :], sums[:, p % 2, :], ALU.mult).then_inc(
                    x_attn.sem, 1)

            def y_pv(i, p):
                if p % 4 == 3:
                    y_recip.wait(pool, i, p // 4 + 1)
                    g.tensor_tensor(an[:, p // 4, :], an[:, p // 4, :], sums[:, p // 4, :], ALU.mult).then_inc(
                        y_attn.sem, 1)

            def x_lo(i, p):
                x_attn_hi.wait(pool, i, p + 1)
                g.tensor_tensor(q[1][:, p, :], an[:, p % 3, :], q[0][:, p, :].bitcast(F32),
                                ALU.subtract).then_inc(x_attn_lo.sem, 1)

            pool.wait_ge(setup_done, SET_UP)
            run(pool, {"n_stat": n_norm, "n_res": n_res, "p_stat": y_norm2, "y_stat3": y_stat3, "y_res": y_res, "y_k": y_k,
                       "x_pv": x_pv, "y_pv": y_pv, "x_hi": x_lo})
            pool.wait_ge(y_stored.sem, 16 * B)
            g.memset(eb_s, 0.0).then_inc(m_zeroed, 1)
            pool.wait_ge(m_norm, 2)
            g.tensor_scalar(m_rstd[:, 0, :], m_mv[:, :, 1], EPS, None, ALU.add).then_inc(m_rs, 1)
            pool.wait_ge(m_rs, 1)
            g.tensor_tensor(m_rstd[:, 1, :], m_rstd[:, 0, :], neg_half[:], ALU.pow).then_inc(m_rs, 1)
            g.memset(m_cT, 0.0).then_inc(m_rs, 1)

        @block.scalar
        def _(act):
            a = nc.scalar
            for n in range(NSPLIT):
                act.wait_ge(stage_in[n % 2], 16 * (n // 2 + 1))
                a.copy(splits[n][1], staged(n)).then_inc(split_hi, 1)
            act.wait_ge(small_in, SMALL)
            a.activation(tg[:], tg[:], ACT.Tanh).then_inc(tanh_done, 1)
            a.preload_act_table_set('natural_log_exp_and_others')
            act.wait_ge(const_done, CONST)
            a.copy(eb3[:], eb_s)
            a.copy(ident_r[:], ident[:, 0:H]).then_inc(setup_done, 1)

            def hi_of(ring, done, i, job, cols, dst):
                ring.full(act, i, job)
                a.copy(dst, ring.bank(job)[:, 0:cols]).then_inc(done.sem, 1)

            def x_tr(i, _):
                hi_of(xr, x_hi, i, X_TR, KD * S, flat(xT[0][:]))

            def x_ctx(i, _):
                xr.full(act, i, X_CTX)
                xr.has_emptied(a.copy(flat(ctxT[:]), xr.bank(X_CTX)[:, 0:KD * NK]), X_CTX)

            def y_ctx(i, _):
                yr.full(act, i, Y_CTX)
                yr.has_emptied(a.copy(flat(ctxT[:]), yr.bank(Y_CTX)[:, 0:KD * NK]), Y_CTX)

            def n_load(i, _):
                x_resd.wait(act, i, 0)
                act.dma_start(x_in[:], x_rows[i]).then_inc(x_loaded.sem, 16)
                act.dma_start(ctx_in[:], ctx[i]).then_inc(ctx_loaded.sem, 16)

            def p_load(i, _):
                act.dma_start(ctx_in[:], ctx[i]).then_inc(ctx1_loaded.sem, 16)

            def x_k(i, c):
                xr.full(act, i, X_K[c])
                view = xr.bank(X_K[c])[:, 0:4 * NK].rearrange("p (m n) -> p m n", m=4)
                for half in range(2):
                    rows = slice(64 * half, 64 * half + 64)
                    last = a.copy(kbd[0][rows, 8 * c + half:8 * c + 8:2, :], view[rows])
                last.then_inc(x_hi.sem, 1)

            def x_v(i, c):
                xr.full(act, i, X_V[c])
                a.copy(vx[0:NK, 8 * c:8 * c + 8, 0:DH0],
                       xr.bank(X_V[c])[0:NK, :].rearrange("p (h d) -> p h d", d=DH0)).then_inc(x_v_hi.sem, 1)

            def x_q(i, c):
                hi_of(xr, x_hi, i, X_Q + c, 2 * S, flat(q[0][:, 2 * c:2 * c + 2, :]))

            def y_tr(job):
                return lambda i, _: hi_of(yr, y_hi, i, job, KD * S, flat(yT[0][:]))

            def biased_hi(i, job, cols, dst, b):
                yr.full(act, i, job)
                for m in range(KD):
                    last = a.activation(dst[:, m, :], yr.bank(job)[:, m * cols:(m + 1) * cols], ACT.Identity,
                                        bias=bqkv1_s[:, b, m:m + 1])
                last.then_inc(y_hi.sem, 1)

            def y_k(i, _):
                y_kmask.wait(act, i, 0)
                biased_hi(i, Y_K, NK, k1[0], 1)

            def y_q(i, _):
                biased_hi(i, Y_Q, S, q1[0], 0)

            def y_v(i, _):
                yr.full(act, i, Y_V)
                for gr in range(4):
                    last = a.copy(v1_block(gr, 0)[0:NK], yr.bank(Y_V)[0:NK, gr * 64:(gr + 1) * 64]
                                  .rearrange("p (j d) -> p j d", j=4))
                yr.has_emptied(last, Y_V)

            def y_gate(i, _):
                yr.full(act, i, Y_GATE)
                yr.has_emptied(a.activation(lgT[0:NE, :], yr.bank(Y_GATE)[0:NE, 0:S], ACT.Identity, bias=gate_b_s[:]),
                               Y_GATE)

            def y_lg(i, _):
                yr.empty(act, i, Y_LG)
                a.activation(flat(lg[:]), flat(lg[:]), ACT.Exp).then_inc(y_exp.sem, 1)

            def y_wt(i, _):
                yr.full(act, i, Y_WT)
                for r in (EB_ROWS[0], EB_ROWS[2]):
                    last = a.copy(wT[r:r + NE, :], yr.bank(Y_WT)[0:NE, 0:S])
                last.then_inc(y_wt_hi.sem, 1)

            def x_maxt_copy(i, t):
                xr.full(act, i, X_MAXT[t])
                xr.has_emptied(a.copy(x_nmT[0:H, t * P:(t + 1) * P], xr.bank(X_MAXT[t])[0:H, 0:P]), X_MAXT[t])

            def y_maxt_copy(i, t):
                yr.full(act, i, Y_MAXT[t])
                yr.has_emptied(a.copy(y_nmT[0:H, t * P:(t + 1) * P], yr.bank(Y_MAXT[t])[0:H, 0:P]), Y_MAXT[t])

            def st(scored, used, probs, scale):
                def step(i, p):
                    scored.wait(act, i, p + 1)
                    if p >= 2:
                        used.wait(act, i, p - 1)
                    a.activation(flat(prob[:, p % 2]), scores[p % 2][0:NK, :], ACT.Exp, scale=scale).then_inc(
                        probs.sem, 1)
                return step

            def take(pvo, an, inv, copied, logged, inverted, i, k):
                for o in range(2):
                    last = a.activation(inv[64 * o:64 * o + 64, :], pvo[64:128, o * S:(o + 1) * S], ACT.Ln)
                last.then_inc(logged.sem, 1)
                for o in range(2):
                    last = a.copy(an[64 * o:64 * o + 64, :], pvo[0:64, o * S:(o + 1) * S])
                last.then_inc(copied.sem, 1)
                logged.wait(act, i, k)
                a.activation(inv, inv, ACT.Exp, scale=-1.0).then_inc(inverted.sem, 1)

            def x_pv(i, p):
                x_mixed.wait(act, i, p + 1)
                if p < 3:
                    y_attn_lo.wait(act, i - 1, 0)
                else:
                    x_attn_lo.wait(act, i, p - 2)
                take(pv[p % 2], an[:, p % 3, :], sums[:, p % 2, :], x_copied, x_logged, x_recip, i, p + 1)

            def y_pv(i, p):
                if p % 4 == 3:
                    m = p // 4
                    y_mixed.wait(act, i, p + 1)
                    take(pv[m], an[:, m, :], sums[:, m, :], y_copied, y_logged, y_recip, i, m + 1)

            def x_attn_split(i, p):
                x_attn.wait(act, i, p + 1)
                a.copy(q[0][:, p, :], an[:, p % 3, :]).then_inc(x_attn_hi.sem, 1)

            def y_attn_split(i, m):
                y_attn.wait(act, i, m + 1)
                a.activation(q1[0][:, m, :], an[:, m, :], ACT.Identity,
                             bias=bqkv1_s[:, 2, m:m + 1]).then_inc(y_attn_hi.sem, 1)

            def x_made_(i, _):
                x_made.wait(act, i, 1)

            run(act, {"n_load": n_load, "p_load": p_load, "n_tr": x_tr, "n_ctx": x_ctx, "n_k": x_k, "n_v": x_v,
                      "n_q": x_q, "p_tr2": y_tr(Y_TR2), "p_ctx": y_ctx, "y_k": y_k, "y_v": y_v, "p_gate": y_gate, "p_lg": y_lg,
                      "p_wt": y_wt, "y_tr3": y_tr(Y_TR3), "y_q": y_q, "n_maxt": x_maxt_copy, "y_maxt": y_maxt_copy,
                      "x_st": st(x_scored, x_prob_lo, x_probs, SCALE0), "y_st": st(y_scored, y_mixed, y_probs, SCALE1),
                      "x_pv": x_pv, "y_pv": y_pv, "x_hi": x_attn_split, "y_hi": y_attn_split, "z_hi": y_attn_split, "x_made": x_made_})
            for k in range(KD):
                act.wait_ge(m_tr, k + 1)
                a.copy(xmT[:, k, :], pv[k][:]).then_inc(m_trc, 1)
            act.wait_ge(m_tr, KD + 1)
            act.wait_ge(m_rs, 3)
            a.copy(m_cT[0:NE, :], xg[0][0:NE, :]).then_inc(m_trc, 1)
            for n in range(KD * NE):
                act.wait_ge(m_gate, n + 1)
                if n >= 1:
                    act.wait_ge(m_inter, n)
                a.activation(m_s, m_g, ACT.Sigmoid, scale=SWIGLU_ALPHA).then_inc(m_sig, 1)

        @block.tensor
        def _(pe):
            t_ = nc.tensor
            pe.wait_ge(setup_done, SET_UP)
            pe.wait_ge(const_done, CONST)
            pe.wait_ge(split_lo, NSPLIT)
            pe.wait_ge(last_in, 16 * 4)

            def products(out_, terms, first=True, last=True):
                n = 0
                for lhsT, rhs in terms:
                    for u, v in ((0, 0), (1, 0), (0, 1)):
                        n += 1
                        ins = t_.matmul(out_, lhsT[u], rhs[v], start=first and n == 1,
                                        stop=last and n == 3 * len(terms))
                return ins

            def products32(out_, terms):
                for n, (lhsT, rhs) in enumerate(terms):
                    ins = t_.matmul(out_, lhsT, rhs, start=n == 0, stop=n == len(terms) - 1)
                return ins

            def both(parts, *at):
                return parts[0][at], parts[1][at]

            ALL = slice(None)

            def transposes(ring, job, src, normed, k_normed):
                def step(i, _):
                    normed.wait(pe, i, k_normed)
                    ring.to_fill(pe, i, job)
                    for k in range(KD):
                        for t in range(T):
                            ins = t_.transpose(ring.bank(job)[:, k * S + t * P:k * S + (t + 1) * P],
                                               src[:, t, k * P:(k + 1) * P], ident[:])
                    ring.has_filled(ins, job)
                return step

            def ctx_transposes(ring, job, src, loaded):
                def step(i, _):
                    loaded.wait(pe, i, 16)
                    ring.to_fill(pe, i, job)
                    for k in range(KD):
                        ins = t_.transpose(ring.bank(job)[:, k * NK:(k + 1) * NK], src[:, k * P:(k + 1) * P],
                                           ident[0:NK, 0:NK])
                    ring.has_filled(ins, job)
                return step

            def x_k(i, c):
                xr.empty(pe, i, X_CTX)
                xr.to_fill(pe, i, X_K[c])
                for m in range(4):
                    col = (4 * c + m) * P
                    ins = products32(xr.bank(X_K[c])[:, m * NK:(m + 1) * NK],
                                     [(wk_s[:, k, col:col + P], ctxT[:, k, :]) for k in range(KD)])
                xr.has_filled(ins, X_K[c])

            def x_v(i, c):
                xr.to_fill(pe, i, X_V[c])
                ins = products32(xr.bank(X_V[c])[0:NK, :],
                                 [(ctxT[:, k, :], wv_s[:, k, 512 * c:512 * (c + 1)]) for k in range(KD)])
                xr.has_filled(ins, X_V[c])

            def x_q(i, c):
                xr.empty(pe, i, X_TR)
                xr.to_fill(pe, i, X_Q + c)
                for m in range(2):
                    col = slice((2 * c + m) * P, (2 * c + m + 1) * P)
                    ins = products(xr.bank(X_Q + c)[:, m * S:(m + 1) * S],
                                   [(both(wq_s, ALL, k, col), both(xT, ALL, k, ALL)) for k in range(KD)])
                xr.has_filled(ins, X_Q + c)

            def x_max(i, j):
                t, c = j // 4, j % 4
                xr.empty(pe, i, X_Q + c)
                xr.to_fill(pe, i, X_MAX[j])
                for m in range(2):
                    p = 2 * c + m
                    ins = t_.matmul(xr.bank(X_MAX[j])[:, m * 2 * NK:(m + 1) * 2 * NK],
                                    q[0][:, p, t * P:(t + 1) * P], flat(kbd[0][:, 2 * p:2 * p + 2, :]),
                                    start=True, stop=True)
                xr.has_filled(ins, X_MAX[j])

            def y_max(i, j):
                t, c = j // 4, j % 4
                yr.empty(pe, i, Y_Q)
                y_kmask.wait(pe, i, 1)
                yr.to_fill(pe, i, Y_MAX[j])
                ins = t_.matmul(yr.bank(Y_MAX[j])[:, 0:4 * NK], q1[0][:, c // 2, t * P:(t + 1) * P],
                                flat(kbd1[0][:, c // 2, 4 * (c % 2):4 * (c % 2) + 4, :]), start=True, stop=True)
                yr.has_filled(ins, Y_MAX[j])

            def x_maxt_in_(i, t):
                if (X_MAXT[t] - X_MAX[4 * t + 3]) % xr.n:
                    xr.empty(pe, i, X_MAX[4 * t + 3])
                xr.to_fill(pe, i, X_MAXT[t])
                xr.has_filled(t_.transpose(xr.bank(X_MAXT[t])[0:H, 0:P], x_nm[:, t, :], ident[:]), X_MAXT[t])

            def y_maxt_in_(i, t):
                if (Y_MAXT[t] - Y_MAX[4 * t + 3]) % yr.n:
                    yr.empty(pe, i, Y_MAX[4 * t + 3])
                yr.to_fill(pe, i, Y_MAXT[t])
                yr.has_filled(t_.transpose(yr.bank(Y_MAXT[t])[0:H, 0:P], y_nm[:, t, :], ident[:]), Y_MAXT[t])

            def scores_of_pair(p, keys, queries, nmT):
                for o in range(2):
                    h = 2 * p + o
                    dst = scores[p % 2][0:NK, o * S:(o + 1) * S]
                    products(dst, [(keys(h), queries(h))], last=False)
                    ins = t_.matmul(dst, ident_r[:, h:h + 1].broadcast_to([P, NK]), nmT[:], start=False, stop=True)
                return ins

            def x_st(i, p):
                xr.empty(pe, i, X_MAXT[1])
                if p >= 2:
                    x_probs.wait(pe, i, p - 1)
                scores_of_pair(p, lambda h: both(kbd, ALL, h, ALL), lambda h: both(q, ALL, h // 2, ALL),
                               x_nmT).then_inc(x_scored.sem, 1)

            def y_st(i, p):
                yr.empty(pe, i, Y_MAXT[1])
                if p >= 2:
                    y_probs.wait(pe, i, p - 1)
                scores_of_pair(p, lambda h: both(kbd1, ALL, h // 8, h % 8, ALL), lambda h: both(q1, ALL, h // 8, ALL),
                               y_nmT).then_inc(y_scored.sem, 1)

            def x_pv(i, p):
                x_prob_lo.wait(pe, i, p + 1)
                if p >= 2:
                    x_copied.wait(pe, i, p - 1)
                elif p == 1:
                    y_made.wait(pe, i - 1, 0)
                for o in range(2):
                    cols, v_ones = slice(o * S, (o + 1) * S), vx[0:NK, 2 * p + o, :]
                    t_.matmul(pv[p % 2][:, cols], v_ones, x_prob[0][:, o, :], start=True, stop=False)
                    t_.matmul(pv[p % 2][0:DH0, cols], vx_lo[0:NK, 2 * p + o, :], x_prob[0][:, o, :], start=False,
                              stop=False)
                    ins = t_.matmul(pv[p % 2][:, cols], v_ones, x_prob[1][:, o, :], start=False, stop=True)
                ins.then_inc(x_mixed.sem, 1)

            def x_made_(i, _):
                x_made.wait(pe, i, 1)

            def y_pv(i, p):
                y_probs.wait(pe, i, p + 1)
                if p == 4:
                    y_made.wait(pe, i, 0)
                cols = slice((p // 2) % 2 * S, ((p // 2) % 2 + 1) * S)
                for o in range(2):
                    h = 2 * p + o
                    ins = t_.matmul(pv[p // 4][:, cols], vx1[0:NK, h * P:(h + 1) * P], prob[:, p % 2, o, :],
                                    start=h % 4 == 0, stop=h % 4 == 3)
                ins.then_inc(y_mixed.sem, 1)

            def x_out(i, c):
                t, k0 = c // 2, (c % 2) * 4
                if c == 0:
                    x_copied.wait(pe, i, NPAIR)
                x_attn_lo.wait(pe, i, k0 + 4)
                ins = products(pv[0][:, t * D:(t + 1) * D],
                               [(both(q, ALL, k, slice(t * P, (t + 1) * P)), both(wo_s, ALL, k, ALL))
                                for k in range(k0, k0 + 4)], first=k0 == 0, last=k0 == 4)
                if c == 3:
                    ins.then_inc(x_out_in.sem, 1)

            def y_k(i, _):
                yr.empty(pe, i, Y_CTX)
                yr.to_fill(pe, i, Y_K)
                for m in range(KD):
                    ins = products32(yr.bank(Y_K)[:, m * NK:(m + 1) * NK],
                                     [(w1k_s[:, k, m * P:(m + 1) * P], ctxT[:, k, :]) for k in range(KD)])
                yr.has_filled(ins, Y_K)

            def y_v(i, _):
                yr.to_fill(pe, i, Y_V)
                ins = products32(yr.bank(Y_V)[0:NK, 0:D], [(ctxT[:, k, :], w1v_s[:, k, :]) for k in range(KD)])
                yr.has_filled(ins, Y_V)

            def y_gate(i, _):
                yr.empty(pe, i, Y_TR2)
                yr.to_fill(pe, i, Y_GATE)
                yr.has_filled(products(yr.bank(Y_GATE)[0:NE, 0:S],
                                       [((gate_s(0)[:, k, :], gate_s(1)[:, k, :]), both(yT, ALL, k, ALL))
                                        for k in range(KD)]), Y_GATE)

            def y_lg(i, _):
                yr.empty(pe, i, Y_GATE)
                yr.to_fill(pe, i, Y_LG)
                for t in range(T):
                    ins = t_.transpose(yr.bank(Y_LG)[:, t * P:(t + 1) * P], lgT[:, t * P:(t + 1) * P], ident[:])
                yr.has_filled(ins, Y_LG)

            def y_wt(i, _):
                y_gated.wait(pe, i, 9)
                yr.to_fill(pe, i, Y_WT)
                for t in range(T):
                    ins = t_.transpose(yr.bank(Y_WT)[0:NE, t * P:(t + 1) * P], lg[:, t, :], ident[:])
                yr.has_filled(ins, Y_WT)

            def y_eb(i, _):
                yr.empty(pe, i, Y_WT)
                yr.to_fill(pe, i, Y_EB)
                for t in range(T):
                    ins = t_.matmul(yr.bank(Y_EB)[:, t * D:(t + 1) * D], wT[:, t * P:(t + 1) * P], eb3[:],
                                    start=True, stop=True)
                yr.has_filled(ins, Y_EB)

            def y_ffn(i, j):
                t, n = j % T, j // T
                yr.to_fill(pe, i, Y_FFN[j])
                ins = products(yr.bank(Y_FFN[j])[:], [(both(yT, ALL, k, slice(t * P, (t + 1) * P)),
                                                        both(ew_s, ALL, k, slice(2 * D * n, 2 * D * (n + 1))))
                                                       for k in range(KD)])
                yr.has_filled(ins, Y_FFN[j])

            def y_q(i, _):
                yr.empty(pe, i, Y_TR3)
                yr.to_fill(pe, i, Y_Q)
                for m in range(KD):
                    col = slice(m * P, (m + 1) * P)
                    ins = products(yr.bank(Y_Q)[:, m * S:(m + 1) * S],
                                   [((w1q_s(0)[:, k, col], w1q_s(1)[:, k, col]), both(yT, ALL, k, ALL))
                                    for k in range(KD)])
                yr.has_filled(ins, Y_Q)

            def y_out(i, _):
                y_attn_lo.wait(pe, i, 2)
                for t in range(T):
                    ins = products(pv[1][:, t * D:(t + 1) * D],
                                   [(both(q1, ALL, k, slice(t * P, (t + 1) * P)),
                                     (w1o_s(0)[:, k, :], w1o_s(1)[:, k, :])) for k in range(KD)])
                ins.then_inc(y_out_in.sem, 1)

            run(pe, {
                "n_tr": transposes(xr, X_TR, xn, x_normed, 1),
                "n_ctx": ctx_transposes(xr, X_CTX, ctx_in, ctx_loaded),
                "p_ctx": ctx_transposes(yr, Y_CTX, ctx_in, ctx1_loaded),
                "n_k": x_k, "n_v": x_v, "n_q": x_q, "p_tr2": transposes(yr, Y_TR2, xn, y_normed, 1),
                "y_k": y_k, "y_v": y_v, "p_gate": y_gate, "p_lg": y_lg, "n_max": x_max, "p_wt": y_wt, "p_eb": y_eb,
                "y_ffn": y_ffn, "n_maxt": x_maxt_in_, "x_st": x_st, "y_st": y_st,
                "x_pv": x_pv, "y_pv": y_pv, "y_tr3": transposes(yr, Y_TR3, xn, y_normed, 2), "y_q": y_q,
                "y_max": y_max, "y_maxt": y_maxt_in_, "x_out": x_out, "x_made": x_made_, "z_out": y_out})

            pe.wait_ge(m_norm, 3)
            for k in range(KD):
                for t in range(TT):
                    ins = t_.transpose(pv[k][:, t * P:(t + 1) * P], xmn[:, t, k * P:(k + 1) * P],
                                       ident[:])
                ins.then_inc(m_tr, 1)
            pe.wait_ge(m_coef, M_COEF)
            for t in range(TT):
                ins = t_.transpose(xg[0][0:NE, t * P:(t + 1) * P], coef[:, :, t], ident[:])
            ins.then_inc(m_tr, 1)
            pe.wait_ge(m_trc, KD + 1)
            pe.wait_ge(m_in, 16 * (NTOK // S + 1))
            for t in range(TT):
                ins = t_.matmul(scores[t // 2][:, (t % 2) * D:(t % 2 + 1) * D],
                                m_cT[:, t * P:(t + 1) * P], eb_s, start=True, stop=True)
            ins.then_inc(m_down, 1)

            def gates_and_ups(e):
                pe.wait_ge(m_gu_in[e % 2], 16 * (e // 2 + 1))
                for m in range(KD):
                    n = KD * e + m
                    if n >= 2:
                        pe.wait_ge(m_upc, n - 1)
                    for u in range(2):
                        ins = products32((xg, yg)[m][u][:], [(gu_s[e % 2][:, k, u, m * P:(m + 1) * P], xmT[:, k, :])
                                                             for k in range(KD)])
                    ins.then_inc(m_up, 1)

            gates_and_ups(0)
            for e in range(NE):
                if e + 1 < NE:
                    gates_and_ups(e + 1)
                pe.wait_ge(m_dn_in[e % 2], 16 * (e // 2 + 1))
                pe.wait_ge(m_inter, KD * (e + 1))
                pe.wait_ge(m_acc, e + 1)
                for t in range(TT):
                    ins = products32(scores[t // 2][:, (t % 2) * D:(t % 2 + 1) * D],
                                     [(inter[e % 2][:, k, t * P:(t + 1) * P], dn_s[e % 2][:, k, :])
                                      for k in range(KD)])
                ins.then_inc(m_down, 1)

        @block.vector
        def _(dve):
            v = nc.vector
            for part in range(2):
                v.memset(flat(kbd[part][:]).bitcast(F32), 0.0)
            v.memset(lgT[:], 0.0)
            v.memset(wT[:].bitcast(F32), 0.0)
            for n in range(NSPLIT):
                dve.wait_ge(split_hi, n + 1)
                v.tensor_tensor(splits[n][2], staged(n), splits[n][1].bitcast(F32), ALU.subtract).then_inc(split_lo, 1)
            dve.wait_ge(tanh_done, 1)
            v.tensor_scalar(bo_tg[:], bo_tg[:], tg[:, 0:1], None, ALU.mult).then_inc(setup_done, 1)
            v.tensor_scalar(bo1_tg[:], bo1_tg[:], tg[:, 1:2], None, ALU.mult).then_inc(setup_done, 1)
            v.memset(x_nmT[:].bitcast(F32), 0.0).then_inc(setup_done, 1)
            v.memset(y_nmT[:].bitcast(F32), 0.0).then_inc(setup_done, 1)
            dve.wait_ge(setup_done, SET_UP - 1)
            lo_rows = slice(EB_ROWS[2], EB_ROWS[2] + NE)
            v.tensor_tensor(eb3[lo_rows, :], eb_s[lo_rows, :], eb3[lo_rows, :].bitcast(F32),
                            ALU.subtract).then_inc(setup_done, 1)

            def statistics(src, st6, mv, stats):
                for t in range(T):
                    ins = v.bn_stats(st6[:, t, :], src[:, t, :])
                ins.then_inc(stats.sem, 1)
                dve.drain()
                for t in range(T):
                    ins = v.bn_aggr(mv[:, t, :], st6[:, t, :])
                ins.then_inc(stats.sem, 1)

            def normalise(src, mv, rs, dst, normed):
                for t in range(T):
                    ins = v.tensor_scalar(dst[:, t, :], src[:, t, :], mv[:, t, 0:1], rs[:, 1, t:t + 1],
                                          ALU.subtract, ALU.mult)
                ins.then_inc(normed.sem, 1)

            def n_stat(i, _):
                x_loaded.wait(dve, i, 16)
                statistics(x_in, x_st6, x_mv, x_stats)

            def n_norm(i, _):
                x_rs.wait(dve, i, 2)
                normalise(x_in, x_mv, x_rstd, xn, x_normed)

            def p_stat(i, _):
                x_made.wait(dve, i, 1)
                statistics(x1, y_st6, y_mv, y_stats)

            def p_norm(i, _):
                y_rs.wait(dve, i, 2)
                normalise(x1, y_mv, y_rstd, xn, y_normed)

            def y_stat3(i, _):
                yr.empty(dve, i, Y_FFN[6])
                yr.empty(dve, i, Y_FFN[7])
                statistics(x1, y_st6, y_mv, y_stats)

            def y_norm3(i, _):
                y_rs.wait(dve, i, 4)
                normalise(x1, y_mv, y_rstd, xn, y_normed)

            def lo_of(ring, done, k, i, job, cols, dst, hi):
                done.wait(dve, i, k)
                ring.has_emptied(v.tensor_tensor(dst, ring.bank(job)[:, 0:cols], hi.bitcast(F32), ALU.subtract), job)

            def x_tr(i, _):
                lo_of(xr, x_hi, 1, i, X_TR, KD * S, flat(xT[1][:]), flat(xT[0][:]))

            def x_k(i, c):
                x_hi.wait(dve, i, 2 + c)
                view = xr.bank(X_K[c])[:, 0:4 * NK].rearrange("p (m n) -> p m n", m=4)
                for half in range(2):
                    rows, heads = slice(64 * half, 64 * half + 64), slice(8 * c + half, 8 * c + 8, 2)
                    ins = v.tensor_tensor(kbd[1][rows, heads, :], view[rows], kbd[0][rows, heads, :].bitcast(F32),
                                          ALU.subtract)
                xr.has_emptied(ins, X_K[c])

            def x_v(i, c):
                x_v_hi.wait(dve, i, c + 1)
                heads = slice(8 * c, 8 * c + 8)
                xr.has_emptied(v.tensor_tensor(
                    vx_lo[0:NK, heads, :], xr.bank(X_V[c])[0:NK, :].rearrange("p (h d) -> p h d", d=DH0),
                    vx[0:NK, heads, 0:DH0].bitcast(F32), ALU.subtract), X_V[c])

            def x_split(i, p):
                x_probs.wait(dve, i, p + 1)
                x_mixed.wait(dve, i, p)
                v.tensor_copy(x_prob[0][:], prob[:, p % 2]).then_inc(x_prob_hi.sem, 1)
                x_prob_hi.wait(dve, i, p + 1)
                v.tensor_tensor(x_prob[1][:], prob[:, p % 2], x_prob[0][:].bitcast(F32),
                                ALU.subtract).then_inc(x_prob_lo.sem, 1)

            def x_q(i, c):
                lo_of(xr, x_hi, 4 + c, i, X_Q + c, 2 * S, flat(q[1][:, 2 * c:2 * c + 2, :]),
                      flat(q[0][:, 2 * c:2 * c + 2, :]))

            def y_tr(job, k):
                return lambda i, _: lo_of(yr, y_hi, k, i, job, KD * S, flat(yT[1][:]), flat(yT[0][:]))

            def biased_lo(i, k, job, cols, parts, b):
                y_hi.wait(dve, i, k)
                for m in range(KD):
                    ins = v.scalar_tensor_tensor(out=parts[1][:, m, :], in0=yr.bank(job)[:, m * cols:(m + 1) * cols],
                                                 scalar=bqkv1_s[:, b, m:m + 1], in1=parts[0][:, m, :].bitcast(F32),
                                                 op0=ALU.add, op1=ALU.subtract)
                yr.has_emptied(ins, job)

            def y_k(i, _):
                y_kmask.wait(dve, i, 0)
                biased_lo(i, 2, Y_K, NK, k1, 1)

            def y_q(i, _):
                biased_lo(i, 4, Y_Q, S, q1, 0)

            def maxima(ring, max_job, nm):
                def step(i, j):
                    t, c = j // 4, j % 4
                    ring.full(dve, i, max_job[j])
                    ring.has_emptied(v.tensor_reduce(
                        nm[:, t, 4 * c:4 * c + 4],
                        ring.bank(max_job[j])[:, 0:4 * NK].rearrange("p (h n) -> p h n", h=4), AX_X, ALU.max,
                        negate=True), max_job[j])
                return step

            def over_experts(a):
                return a.unsqueeze(2).broadcast_to([P, T, NE])

            def y_gate(i, _):
                done = y_gated
                yr.full(dve, i, Y_LG)
                logits = yr.bank(Y_LG)[:, 0:T * P].rearrange("p (t e) -> p t e", t=T)[:, :, 0:NE]
                v.tensor_reduce(lg_n[:, 0, :], logits, AX_X, ALU.max, negate=True).then_inc(done.sem, 1)
                done.wait(dve, i, 1)
                yr.has_emptied(v.tensor_tensor(lg[:], logits, over_experts(lg_n[:, 0, :]), ALU.add), Y_LG)
                yr.empty(dve, i, Y_LG)
                y_exp.wait(dve, i, 1)
                v.tensor_reduce(lg_n[:, 1, :], lg[:], AX_X, ALU.add).then_inc(done.sem, 1)
                done.wait(dve, i, 2)
                v.reciprocal(lg_n[:, 2, :], lg_n[:, 1, :]).then_inc(done.sem, 1)
                done.wait(dve, i, 3)
                v.tensor_tensor(lg[:], lg[:], over_experts(lg_n[:, 2, :]), ALU.mult).then_inc(done.sem, 1)
                done.wait(dve, i, 4)
                v.scalar_tensor_tensor(out=flat(lg[:]), in0=flat(lg[:]), scalar=THRESHOLD, in1=flat(lg[:]),
                                       op0=ALU.is_ge, op1=ALU.mult).then_inc(done.sem, 1)
                done.wait(dve, i, 5)
                v.tensor_reduce(lg_n[:, 1, :], lg[:], AX_X, ALU.add).then_inc(done.sem, 1)
                done.wait(dve, i, 6)
                v.scalar_tensor_tensor(out=lg_n[:, 3, :], in0=lg_n[:, 1, :], scalar=0.0, in1=lg_n[:, 1, :],
                                       op0=ALU.is_equal, op1=ALU.add).then_inc(done.sem, 1)
                done.wait(dve, i, 7)
                v.reciprocal(lg_n[:, 2, :], lg_n[:, 3, :]).then_inc(done.sem, 1)
                done.wait(dve, i, 8)
                v.scalar_tensor_tensor(out=lg[:], in0=lg[:], scalar=tg[:, 2:3], in1=over_experts(lg_n[:, 2, :]),
                                       op0=ALU.mult, op1=ALU.mult).then_inc(done.sem, 1)

            def y_wt(i, _):
                y_wt_hi.wait(dve, i, 1)
                lo_rows = slice(EB_ROWS[1], EB_ROWS[1] + NE)
                yr.has_emptied(v.tensor_tensor(wT[lo_rows, :], yr.bank(Y_WT)[0:NE, 0:S], wT[0:NE, :].bitcast(F32),
                                               ALU.subtract), Y_WT)

            def y_eb(i, _):
                yr.full(dve, i, Y_EB)
                yr.has_emptied(v.tensor_tensor(flat(x1[:]), yr.bank(Y_EB)[:], flat(x1[:]), ALU.add), Y_EB)

            def y_ffn(i, j):
                t, n = j % T, j // T
                y_gated.wait(dve, i, 9)
                yr.empty(dve, i, Y_EB)
                yr.full(dve, i, Y_FFN[j])
                for o in range(2):
                    ins = v.scalar_tensor_tensor(out=x1[:, t, :], in0=yr.bank(Y_FFN[j])[:, o * D:(o + 1) * D],
                                                 scalar=lg[:, t, 2 * n + o:2 * n + o + 1], in1=x1[:, t, :],
                                                 op0=ALU.mult, op1=ALU.add)
                    if o == 0:
                        ins.then_inc(y_acc.sem, 1)
                        y_acc.wait(dve, i, j + 1)
                yr.has_emptied(ins, Y_FFN[j])

            def y_attn_split(i, m):
                y_attn_hi.wait(dve, i, m + 1)
                v.scalar_tensor_tensor(out=q1[1][:, m, :], in0=an[:, m, :], scalar=bqkv1_s[:, 2, m:m + 1],
                                       in1=q1[0][:, m, :].bitcast(F32), op0=ALU.add,
                                       op1=ALU.subtract).then_inc(y_attn_lo.sem, 1)

            def x_out(i, c):
                if c == 3:
                    x_resd.wait(dve, i, 1)
                    y_resd.wait(dve, i, 0)
                    x_out_in.wait(dve, i, 1)
                    v.scalar_tensor_tensor(out=flat(x1[:]), in0=pv[0][:], scalar=tg[:, 0:1], in1=flat(x_res[:]),
                                           op0=ALU.mult, op1=ALU.add).then_inc(x_made.sem, 1)

            def y_out(i, _):
                y_resd.wait(dve, i, 1)
                y_out_in.wait(dve, i, 1)
                v.scalar_tensor_tensor(out=flat(y_x3[:]), in0=pv[1][:], scalar=tg[:, 1:2], in1=flat(y_x3[:]),
                                       op0=ALU.mult, op1=ALU.add).then_inc(y_made.sem, 1)

            run(dve, {"n_stat": n_stat, "n_norm": n_norm, "p_stat": p_stat, "p_norm": p_norm, "y_stat3": y_stat3,
                      "y_norm3": y_norm3, "n_tr": x_tr, "n_k": x_k, "n_v": x_v, "n_q": x_q,
                      "x_split": x_split, "p_tr2": y_tr(Y_TR2, 1), "y_tr3": y_tr(Y_TR3, 3), "y_k": y_k, "y_q": y_q,
                      "n_max": maxima(xr, X_MAX, x_nm), "y_max": maxima(yr, Y_MAX, y_nm), "p_lg": y_gate, "p_wt": y_wt,
                      "p_eb": y_eb, "y_ffn": y_ffn, "y_hi": y_attn_split, "z_hi": y_attn_split, "x_out": x_out, "z_out": y_out})

            dve.wait_ge(m_in, 16 * (NTOK // S + 1))
            for t in range(TT):
                ins = v.bn_stats(m_st6[:, t, :], xm[:, t, :])
            ins.then_inc(m_norm, 1)
            dve.wait_ge(m_norm, 1)
            for t in range(TT):
                ins = v.bn_aggr(m_mv[:, t, :], m_st6[:, t, :])
            ins.then_inc(m_norm, 1)
            v.tensor_copy(idx_f[:], idx_s[:]).then_inc(m_coef, 1)
            dve.wait_ge(m_coef, 1)
            n = 1
            for t in range(TT):
                v.tensor_scalar(coef_k[:], expert_no[:], idx_f[:, t, 0:1], None, ALU.is_equal).then_inc(m_coef, 1)
                dve.wait_ge(m_coef, n + 1)
                v.scalar_tensor_tensor(out=coef_k[:], in0=expert_no[:], scalar=idx_f[:, t, 1:2], in1=coef_k[:],
                                       op0=ALU.is_equal, op1=ALU.add).then_inc(m_coef, 1)
                dve.wait_ge(m_coef, n + 2)
                v.scalar_tensor_tensor(out=coef[:, :, t], in0=rw_s[:, t, :], scalar=tg[:, 3:4], in1=coef_k[:],
                                       op0=ALU.mult, op1=ALU.mult).then_inc(m_coef, 1)
                n += 3
                dve.wait_ge(m_coef, n)
            dve.wait_ge(m_rs, 2)
            for t in range(TT):
                ins = v.tensor_scalar(xmn[:, t, :], xm[:, t, :], m_mv[:, t, 0:1], m_rstd[:, 1, t:t + 1],
                                      ALU.subtract, ALU.mult)
            ins.then_inc(m_norm, 1)

            def add_down(t, scalar):
                dst, src = xm[:, t, :], scores[t // 2][:, (t % 2) * D:(t % 2 + 1) * D]
                if scalar is None:
                    return v.tensor_tensor(dst, src, dst, ALU.add)
                return v.scalar_tensor_tensor(out=dst, in0=src, scalar=scalar, in1=dst, op0=ALU.mult, op1=ALU.add)

            dve.wait_ge(m_norm, 3)
            dve.wait_ge(m_down, 1)
            for t in range(TT):
                ins = add_down(t, None)
            ins.then_inc(m_acc, 1)

            def add_expert(e):
                dve.wait_ge(m_down, e + 2)
                for t in range(TT):
                    ins = add_down(t, coef[:, e, t:t + 1])
                ins.then_inc(m_acc, 1)
                dve.wait_ge(m_acc, e + 2)

            for e in range(NE):
                if e >= 2:
                    dve.wait_ge(m_down, e)
                for m in range(KD):
                    n = KD * e + m
                    banks = (xg, yg)[m]
                    dve.wait_ge(m_up, n + 1)
                    v.tensor_scalar(m_g, banks[0][:], gu_b_s[:, e, m, 0:1], LIMIT, ALU.add,
                                    ALU.min).then_inc(m_gate, 1)
                    v.tensor_scalar(m_u, banks[1][:], gu_b_s[:, e, m, 1:2], LIMIT, ALU.add,
                                    ALU.min).then_inc(m_upc, 1)
                    dve.wait_ge(m_upc, n + 1)
                    v.tensor_scalar(m_u, m_u, -LIMIT, 1.0, ALU.max, ALU.add)
                    dve.wait_ge(m_sig, n + 1)
                    v.tensor_tensor(m_g, m_g, m_s, ALU.mult).then_inc(m_glu, 1)
                    dve.wait_ge(m_glu, n + 1)
                    v.tensor_tensor(inter[e % 2][:, m, :], m_g, m_u, ALU.mult).then_inc(m_inter, 1)
                    dve.wait_ge(m_inter, n + 1)
                if e >= 1:
                    add_expert(e - 1)
            add_expert(NE - 1)


def kernel(**inputs):
    import numpy as _np
    import concourse.bacc as _bacc
    from concourse import mybir as _mybir
    from concourse.bass_utils import run_bass_kernel_spmd as _run

    a = {k: _np.asarray(v) for k, v in inputs.items()}
    kd, ne = D // P, NE

    def rows(w):
        return _np.ascontiguousarray(w.reshape(-1, P, w.shape[-1]).transpose(1, 0, 2))

    def columns(b):
        return b.reshape(-1, P).T

    w1 = _np.concatenate([rows(a[n]).reshape(P, -1) for n in ("L1_xattn_wq", "L1_xattn_wo", "L0_ffn_gate_w")], 1)
    gu = a["L1_ffn_gate_up_proj"].reshape(ne, kd, P, D, 2).transpose(0, 2, 1, 4, 3)
    arrays = {
        "x": a["x"], "ctx": a["ctx_1024"],
        "gates": _np.concatenate([a["g_xattn"], a["g_ffn"]]),
        "wq": rows(a["L0_xattn_Wq"].T), "wk": rows(a["L0_xattn_Wk"].T), "wv": rows(a["L0_xattn_Wv"].T),
        "wo": rows(a["L0_xattn_Wo"].T), "bo": a["L0_xattn_bo"],
        "gate_b": a["L0_ffn_gate_b"].reshape(ne, 1),
        "ew": a["L0_ffn_expert_w"].reshape(ne, kd, P, D).transpose(2, 1, 0, 3).reshape(P, kd, ne * D),
        "eb": a["L0_ffn_expert_b"], "w1": w1,
        "w1k": rows(a["L1_xattn_wk"]), "w1v": rows(a["L1_xattn_wv"]),
        "bqkv1": _np.stack([columns(a[n]) for n in ("L1_xattn_bq", "L1_xattn_bk", "L1_xattn_bv")], 1),
        "bo1": a["L1_xattn_bo"],
        "router_idx": a["L1_ffn_router_indices"].reshape(TT, P, 2).transpose(1, 0, 2),
        "router_w": a["L1_ffn_routing_weights"].reshape(TT, P, ne).transpose(1, 0, 2),
        "gu": gu, "gu_b": a["L1_ffn_gate_up_proj_bias"].reshape(ne, kd, P, 2).transpose(2, 0, 1, 3),
        "dn": a["L1_ffn_down_proj"].reshape(ne, kd, P, D).transpose(0, 2, 1, 3), "dn_b": a["L1_ffn_down_proj_bias"],
    }
    order = ["x", "ctx", "gates", "wq", "wk", "wv", "wo", "bo", "gate_b", "ew", "eb", "w1", "w1k", "w1v", "bqkv1",
             "bo1", "router_idx", "router_w", "gu", "gu_b", "dn", "dn_b"]
    nc = _bacc.Bacc("TRN2", target_bir_lowering=False, num_devices=1)
    maps, args = {}, []
    for name in order:
        v = _np.ascontiguousarray(arrays[name])
        maps[f"in_{name}"] = v
        args.append(nc.dram_tensor(f"in_{name}", v.shape, _mybir.dt.from_np(v.dtype), kind="ExternalInput").ap())
    args.append(nc.dram_tensor("out_0", (B, S, D), F32, kind="ExternalOutput").ap())
    flamingo_stack(nc, *args)
    r = _run(nc, [maps], core_ids=[0])
    return r.results[0]["out_0"]
```
